# Optimizing a Trainium2 kernel written in Bass

```python
import numpy as np
import jax
import jax.numpy as jnp

def _softmax(x, axis=-1):
    return jax.nn.softmax(x, axis=axis)

def _gelu(x):
    return jax.nn.gelu(x, approximate=True)

def _silu(x):
    return jax.nn.silu(x)

def _sigmoid(x):
    return jax.nn.sigmoid(x)

def _layernorm(x, axis=-1, eps=1e-05):
    m = jnp.mean(x, axis=axis, keepdims=True)
    v = jnp.var(x, axis=axis, keepdims=True)
    return (x - m) / jnp.sqrt(v + eps)

def _scatter_add(tgt, idx, src, axis=0):
    return tgt.at[idx].add(src)

def _segment_sum(src, seg, n):
    return jax.ops.segment_sum(src, seg, n)
kernel_name = 'mk_seq_postln_d2_jaxref_r8_2af678'

def setup_inputs(seed: int=0):
    np.random.seed(seed)
    _w = jnp.asarray

    def _L0_attn_setup():
        import jax, jax.numpy as jnp
        import numpy as np
        D_MODEL = 256
        B, L = (4, 256)

        def _dwconv(x, w, b):
            y = jax.lax.conv_general_dilated(x, w, window_strides=(1,), padding=[(2, 0)], feature_group_count=x.shape[1], dimension_numbers=('NCH', 'OIH', 'NCH'))
            return y + b[None, :, None]
        key = jax.random.key(seed)
        ks = jax.random.split(key, 12)
        D = D_MODEL
        s = 0.02
        inp = {'u': jax.random.normal(ks[0], (B, L, D), jnp.float32), 'Wq': jax.random.normal(ks[1], (D, D), jnp.float32) * s, 'bq': jnp.zeros((D,), jnp.float32), 'Wk': jax.random.normal(ks[2], (D, D), jnp.float32) * s, 'bk': jnp.zeros((D,), jnp.float32), 'Wv': jax.random.normal(ks[3], (D, D), jnp.float32) * s, 'bv': jnp.zeros((D,), jnp.float32), 'convq_w': jax.random.normal(ks[4], (D, 1, 3), jnp.float32) * 0.5, 'convq_b': jnp.zeros((D,), jnp.float32), 'convk_w': jax.random.normal(ks[5], (D, 1, 3), jnp.float32) * 0.5, 'convk_b': jnp.zeros((D,), jnp.float32), 'ssm_kernel': jax.random.normal(ks[6], (D, L), jnp.float32) * 0.01, 'D_skip': jax.random.normal(ks[7], (D,), jnp.float32), 'Wo': jax.random.normal(ks[8], (D, D), jnp.float32) * s, 'bo': jnp.zeros((D,), jnp.float32)}
        return inp
    _L0_attn_in = _L0_attn_setup()

    def _L0_ffn_setup():
        import jax, jax.numpy as jnp
        import numpy as np
        B_, S, D = (2, 256, 256)
        F_ = 1024
        R = 16
        H = 16
        HD = D // H
        MOD_SCALE = 0.1
        EPS = 1e-06

        def _rmsnorm(x, w):
            v = jnp.mean(x * x, axis=-1, keepdims=True)
            return x * jax.lax.rsqrt(v + EPS) * w

        def _attention(x, Wq, Wk, Wv, Wo):
            b, s, d = x.shape
            q = (x @ Wq.T).reshape(b, s, H, HD)
            k = (x @ Wk.T).reshape(b, s, H, HD)
            v = (x @ Wv.T).reshape(b, s, H, HD)
            scores = jnp.einsum('bqhd,bkhd->bhqk', q, k) / np.sqrt(HD).astype(np.float32)
            causal = jnp.tril(jnp.ones((s, s), bool))
            scores = jnp.where(causal, scores, jnp.finfo(scores.dtype).min)
            probs = jax.nn.softmax(scores, axis=-1)
            out = jnp.einsum('bhqk,bkhd->bqhd', probs, v).reshape(b, s, d)
            return out @ Wo.T
        key = jax.random.key(seed)
        ks = jax.random.split(key, 12)
        sd = 0.02
        return {'hidden_states': jax.random.normal(ks[0], (B_, S, D), jnp.float32), 'ln1_w': jnp.ones((D,), jnp.float32), 'ln2_w': jnp.ones((D,), jnp.float32), 'Wq': jax.random.normal(ks[1], (D, D), jnp.float32) * sd, 'Wk': jax.random.normal(ks[2], (D, D), jnp.float32) * sd, 'Wv': jax.random.normal(ks[3], (D, D), jnp.float32) * sd, 'Wo': jax.random.normal(ks[4], (D, D), jnp.float32) * sd, 'A': jax.random.normal(ks[5], (D, R), jnp.float32) * (0.01 / np.sqrt(D)), 'B': jax.random.normal(ks[6], (R, F_), jnp.float32) * (0.01 / np.sqrt(R)), 'W_in_base': jax.random.normal(ks[7], (F_, D), jnp.float32) * sd, 'W_up_base': jax.random.normal(ks[8], (F_, D), jnp.float32) * sd, 'W_down': jax.random.normal(ks[9], (D, F_), jnp.float32) * sd}
    _L0_ffn_in = _L0_ffn_setup()

    def _L1_attn_setup():
        import jax, jax.numpy as jnp
        import numpy as np
        D = 256
        key = jax.random.key(seed)
        ks = jax.random.split(key, 5)
        scale = 1.0 / np.sqrt(D)
        x = jax.random.normal(ks[0], (4, 512, D), dtype=jnp.float32)
        Wq = jax.random.normal(ks[1], (D, D), dtype=jnp.float32) * scale
        Wk = jax.random.normal(ks[2], (D, D), dtype=jnp.float32) * scale
        Wv = jax.random.normal(ks[3], (D, D), dtype=jnp.float32) * scale
        Wo = jax.random.normal(ks[4], (D, D), dtype=jnp.float32) * scale
        return {'x': x, 'Wq': Wq, 'Wk': Wk, 'Wv': Wv, 'Wo': Wo}
    _L1_attn_in = _L1_attn_setup()

    def _L1_ffn_setup():
        import jax, jax.numpy as jnp
        import numpy as np
        B, S, H = (2, 64, 256)
        E, I, K = (64, 176, 6)
        NS = 2
        SH_I = I * NS
        key = jax.random.key(seed)
        ks = jax.random.split(key, 6)
        s = 0.02
        return {'hidden_states': jax.random.normal(ks[0], (B, S, H), jnp.float32), 'gate_w': jax.random.normal(ks[1], (E, H), jnp.float32) * s, 'experts_w1': jax.random.normal(ks[2], (E, I, H), jnp.float32) * s, 'experts_w2': jax.random.normal(ks[3], (E, H, I), jnp.float32) * s, 'shared_gate_up': jax.random.normal(ks[4], (2 * SH_I, H), jnp.float32) * s, 'shared_down': jax.random.normal(ks[5], (H, SH_I), jnp.float32) * s}
    _L1_ffn_in = _L1_ffn_setup()
    _d = {'L0_attn_u': _L0_attn_in['u'], 'L0_attn_Wq': _L0_attn_in['Wq'], 'L0_attn_bq': _L0_attn_in['bq'], 'L0_attn_Wk': _L0_attn_in['Wk'], 'L0_attn_bk': _L0_attn_in['bk'], 'L0_attn_Wv': _L0_attn_in['Wv'], 'L0_attn_bv': _L0_attn_in['bv'], 'L0_attn_convq_w': _L0_attn_in['convq_w'], 'L0_attn_convq_b': _L0_attn_in['convq_b'], 'L0_attn_convk_w': _L0_attn_in['convk_w'], 'L0_attn_convk_b': _L0_attn_in['convk_b'], 'L0_attn_ssm_kernel': _L0_attn_in['ssm_kernel'], 'L0_attn_D_skip': _L0_attn_in['D_skip'], 'L0_attn_Wo': _L0_attn_in['Wo'], 'L0_attn_bo': _L0_attn_in['bo'], 'L0_ffn_ln1_w': _L0_ffn_in['ln1_w'], 'L0_ffn_ln2_w': _L0_ffn_in['ln2_w'], 'L0_ffn_Wq': _L0_ffn_in['Wq'], 'L0_ffn_Wk': _L0_ffn_in['Wk'], 'L0_ffn_Wv': _L0_ffn_in['Wv'], 'L0_ffn_Wo': _L0_ffn_in['Wo'], 'L0_ffn_A': _L0_ffn_in['A'], 'L0_ffn_B': _L0_ffn_in['B'], 'L0_ffn_W_in_base': _L0_ffn_in['W_in_base'], 'L0_ffn_W_up_base': _L0_ffn_in['W_up_base'], 'L0_ffn_W_down': _L0_ffn_in['W_down'], 'L1_attn_Wq': _L1_attn_in['Wq'], 'L1_attn_Wk': _L1_attn_in['Wk'], 'L1_attn_Wv': _L1_attn_in['Wv'], 'L1_attn_Wo': _L1_attn_in['Wo'], 'L1_ffn_gate_w': _L1_ffn_in['gate_w'], 'L1_ffn_experts_w1': _L1_ffn_in['experts_w1'], 'L1_ffn_experts_w2': _L1_ffn_in['experts_w2'], 'L1_ffn_shared_gate_up': _L1_ffn_in['shared_gate_up'], 'L1_ffn_shared_down': _L1_ffn_in['shared_down']}
    _x0 = _d['L0_attn_u']
    _d['L0_attn_u'] = jax.random.normal(jax.random.fold_in(jax.random.key(seed), 1), (8, 256, 256), dtype=_x0.dtype)
    del _x0
    return _d

def reference(L0_attn_u, L0_attn_Wq, L0_attn_bq, L0_attn_Wk, L0_attn_bk, L0_attn_Wv, L0_attn_bv, L0_attn_convq_w, L0_attn_convq_b, L0_attn_convk_w, L0_attn_convk_b, L0_attn_ssm_kernel, L0_attn_D_skip, L0_attn_Wo, L0_attn_bo, L0_ffn_ln1_w, L0_ffn_ln2_w, L0_ffn_Wq, L0_ffn_Wk, L0_ffn_Wv, L0_ffn_Wo, L0_ffn_A, L0_ffn_B, L0_ffn_W_in_base, L0_ffn_W_up_base, L0_ffn_W_down, L1_attn_Wq, L1_attn_Wk, L1_attn_Wv, L1_attn_Wo, L1_ffn_gate_w, L1_ffn_experts_w1, L1_ffn_experts_w2, L1_ffn_shared_gate_up, L1_ffn_shared_down):

    def _L0_attn_ref(u, Wq, bq, Wk, bk, Wv, bv, convq_w, convq_b, convk_w, convk_b, ssm_kernel, D_skip, Wo, bo):
        import jax, jax.numpy as jnp
        import numpy as np
        D_MODEL = 256
        B, L = (4, 256)

        def _dwconv(x, w, b):
            y = jax.lax.conv_general_dilated(x, w, window_strides=(1,), padding=[(2, 0)], feature_group_count=x.shape[1], dimension_numbers=('NCH', 'OIH', 'NCH'))
            return y + b[None, :, None]
        Lq = u.shape[1]
        fft_size = 2 * Lq
        q = jnp.einsum('blh,eh->ble', u, Wq) + bq
        k = jnp.einsum('blh,eh->ble', u, Wk) + bk
        v = jnp.einsum('blh,eh->ble', u, Wv) + bv
        q = jnp.transpose(q, (0, 2, 1))
        k = jnp.transpose(k, (0, 2, 1))
        v = jnp.transpose(v, (0, 2, 1))
        q = _dwconv(q, convq_w, convq_b)
        k = _dwconv(k, convk_w, convk_b)
        kv = k * v
        kv_f = jnp.fft.rfft(kv, n=fft_size)
        kernel_f = jnp.fft.rfft(ssm_kernel, n=fft_size)
        y = jnp.fft.irfft(kv_f * kernel_f, n=fft_size)[..., :Lq]
        y = (y + kv * D_skip[None, :, None]) * q
        y = jnp.transpose(y, (0, 2, 1))
        return jnp.einsum('blh,eh->ble', y, Wo) + bo

    def _L0_ffn_ref(hidden_states, ln1_w, ln2_w, Wq, Wk, Wv, Wo, A, B, W_in_base, W_up_base, W_down):
        import jax, jax.numpy as jnp
        import numpy as np
        B_, S, D = (2, 256, 256)
        F_ = 1024
        R = 16
        H = 16
        HD = D // H
        MOD_SCALE = 0.1
        EPS = 1e-06

        def _rmsnorm(x, w):
            v = jnp.mean(x * x, axis=-1, keepdims=True)
            return x * jax.lax.rsqrt(v + EPS) * w

        def _attention(x, Wq, Wk, Wv, Wo):
            b, s, d = x.shape
            q = (x @ Wq.T).reshape(b, s, H, HD)
            k = (x @ Wk.T).reshape(b, s, H, HD)
            v = (x @ Wv.T).reshape(b, s, H, HD)
            scores = jnp.einsum('bqhd,bkhd->bhqk', q, k) / np.sqrt(HD).astype(np.float32)
            causal = jnp.tril(jnp.ones((s, s), bool))
            scores = jnp.where(causal, scores, jnp.finfo(scores.dtype).min)
            probs = jax.nn.softmax(scores, axis=-1)
            out = jnp.einsum('bhqk,bkhd->bqhd', probs, v).reshape(b, s, d)
            return out @ Wo.T
        residual = hidden_states
        x = _rmsnorm(hidden_states, ln1_w)
        attn = _attention(x, Wq, Wk, Wv, Wo)
        mod = MOD_SCALE * jnp.tanh(attn @ A)
        h = _rmsnorm(residual, ln2_w)
        gate_pre = h @ W_in_base.T + mod * (h @ A) @ B
        gate = jax.nn.silu(gate_pre)
        up = h @ W_up_base.T
        mlp_out = gate * up @ W_down.T
        return residual + mlp_out

    def _L1_attn_ref(x, Wq, Wk, Wv, Wo):
        import jax, jax.numpy as jnp
        import numpy as np
        D = 256
        q = jnp.einsum('bsd,ed->bse', x, Wq)
        k = jnp.einsum('bsd,ed->bse', x, Wk)
        v = jnp.einsum('bsd,ed->bse', x, Wv)
        seq = x.shape[-2]
        denom = jnp.sqrt(jnp.float32(x.shape[-1])) / seq
        kvt = jnp.cumsum(k * v, axis=-2) * denom
        vhat = q * kvt
        return jnp.einsum('bse,fe->bsf', vhat, Wo)

    def _L1_ffn_ref(hidden_states, gate_w, experts_w1, experts_w2, shared_gate_up, shared_down):
        import jax, jax.numpy as jnp
        import numpy as np
        B, S, H = (2, 64, 256)
        E, I, K = (64, 176, 6)
        NS = 2
        SH_I = I * NS
        orig_shape = hidden_states.shape
        x = hidden_states.reshape(-1, orig_shape[-1])
        router_logits = x @ gate_w.T
        probs = jax.nn.softmax(router_logits, axis=-1)
        topk_w, topk_idx = jax.lax.top_k(probs, K)
        topk_w = topk_w / jnp.sum(topk_w, axis=-1, keepdims=True)
        combine = jnp.sum(jax.nn.one_hot(topk_idx, E, dtype=x.dtype) * topk_w[..., None], axis=1)
        h = jax.nn.silu(jnp.einsum('th,eih->tei', x, experts_w1))
        y = jnp.einsum('tei,ehi->teh', h, experts_w2)
        routed_out = jnp.einsum('teh,te->th', y, combine)
        gu = x @ shared_gate_up.T
        g, u = jnp.split(gu, 2, axis=-1)
        shared_out = jax.nn.silu(g) * u @ shared_down.T
        return (routed_out + shared_out).reshape(orig_shape)
    x = L0_attn_u
    x = _layernorm(x + _L0_attn_ref(x, L0_attn_Wq, L0_attn_bq, L0_attn_Wk, L0_attn_bk, L0_attn_Wv, L0_attn_bv, L0_attn_convq_w, L0_attn_convq_b, L0_attn_convk_w, L0_attn_convk_b, L0_attn_ssm_kernel, L0_attn_D_skip, L0_attn_Wo, L0_attn_bo), axis=-1)
    x = _layernorm(x + _L0_ffn_ref(x, L0_ffn_ln1_w, L0_ffn_ln2_w, L0_ffn_Wq, L0_ffn_Wk, L0_ffn_Wv, L0_ffn_Wo, L0_ffn_A, L0_ffn_B, L0_ffn_W_in_base, L0_ffn_W_up_base, L0_ffn_W_down), axis=-1)
    x = _layernorm(x + _L1_attn_ref(x, L1_attn_Wq, L1_attn_Wk, L1_attn_Wv, L1_attn_Wo), axis=-1)
    x = _layernorm(x + _L1_ffn_ref(x, L1_ffn_gate_w, L1_ffn_experts_w1, L1_ffn_experts_w2, L1_ffn_shared_gate_up, L1_ffn_shared_down), axis=-1)
    return x

_drawn_inputs = setup_inputs


def setup_inputs(seed=0):
    import zlib

    import numpy as np

    out = dict(_drawn_inputs(seed))
    spreads = {'L0_attn_bq': (0.0, 0.8),
     'L0_attn_bk': (0.0, 0.8),
     'L0_attn_bv': (0.0, 0.8),
     'L0_attn_convq_b': (0.0, 0.8),
     'L0_attn_convk_b': (0.0, 0.8),
     'L0_attn_bo': (0.0, 2.0),
     'L0_ffn_ln1_w': (1.0, 0.6),
     'L0_ffn_ln2_w': (1.0, 0.6)}
    factors = {'L0_attn_Wq': 4.781,
     'L0_attn_Wk': 4.576,
     'L0_attn_Wv': 4.283,
     'L0_attn_convq_w': 3.678,
     'L0_attn_convk_w': 4.72,
     'L0_attn_ssm_kernel': 8.0,
     'L0_attn_D_skip': 4.283,
     'L0_attn_Wo': 4.141,
     'L0_ffn_Wq': 200.0,
     'L0_ffn_Wk': 200.0,
     'L0_ffn_Wv': 200.0,
     'L0_ffn_Wo': 200.0,
     'L0_ffn_A': 200.0,
     'L0_ffn_B': 200.0,
     'L1_ffn_gate_w': 3.184,
     'L1_ffn_experts_w1': 2.997,
     'L1_ffn_experts_w2': 2.977,
     'L1_ffn_shared_gate_up': 2.83,
     'L1_ffn_shared_down': 2.814}
    for name, (base, spread) in spreads.items():
        noise = np.random.default_rng([zlib.crc32(name.encode()), seed]).standard_normal(out[name].shape)
        drawn = base * np.exp(spread * noise) if base else spread * noise
        out[name] = jnp.asarray(drawn.astype(out[name].dtype))
    for name, factor in factors.items():
        out[name] = (out[name] * factor).astype(out[name].dtype)
    return out
```

```python
from contextlib import ExitStack

import numpy as np

import concourse.bass as bass
from concourse import mybir

P = 128
NB, L, D = 8, 256, 256
KT = D // P
TT = L // P
NT = NB * TT
HEADS, HD = 16, 16
PAIR = 2 * HD
GROUPS = P // PAIR
F_MLP = 1024
FT = F_MLP // P
R_MOD = 16
MOD_SCALE = 0.1
E_N, I_N, TOPK = 64, 176, 6
IH = I_N // 2
SH_I = 2 * I_N
SH_TILES = [(0, 128), (128, 128), (256, SH_I - 256)]
PAIRS = NB * L * TOPK
CHUNKS = E_N + (PAIRS - E_N) // P
CAP = P + NB * L
X_ROWS = (E_N + 1) * CAP
NFFT = 2 * L
FREQ_TILES = L // P
RING = 6
HEAD = 9
LN_EPS, RMS_EPS = 1e-5, 1e-6
NEG = -1e38
RSQRT_MAGIC = 0x5F3759DF
ROUND = 8388608.0

F32, BF16 = mybir.dt.float32, mybir.dt.bfloat16
I32, U32 = mybir.dt.int32, mybir.dt.uint32
ALU = mybir.AluOpType
ACT = mybir.ActivationFunctionType
AX = mybir.AxisListType.X

VEC = {"bq": 0, "bk": 2, "bv": 4, "cqb": 6, "ckb": 8, "skip": 10, "ln1": 12, "ln2": 14, "cqw": 16, "ckw": 22}
VEC_N = 28
CST = {"ident": 0, "iota": 128, "region": 192, "even": 256, "odd": 257, "chunk": 258}
CST_N = 260
CSB = {"ident": 0, "ones": 128, "before": 256, "mask0": 384, "mask1": 896}
CSB_N = 1408


def constants():
    p = np.arange(P)
    c = np.zeros((P, CST_N), np.float32)
    c[:, 0:128] = np.eye(P)
    c[:, 128:192] = np.arange(E_N)
    c[:, 192:256] = np.arange(E_N) * CAP + P
    c[:, 256] = np.where(p % PAIR < HD, HD ** -0.5, 0)
    c[:, 257] = np.where(p % PAIR < HD, 0, HD ** -0.5)
    c[:, 258] = 2 * p
    c[:, 259] = 2 * p + 1
    b = np.zeros((P, CSB_N), np.float32)
    b[:, 0:128] = np.eye(P)
    b[:, 128:256] = 1
    b[:, 256:384] = p[:, None] < p[None, :]
    tri = np.where(p[None, :] <= p[:, None], 0, NEG)
    for n in range(4):
        b[:, 384 + 128 * n:512 + 128 * n] = tri
    for n in range(2):
        b[:, 1024 + 256 * n:1152 + 256 * n] = tri
    t = np.arange(L)[:, None]
    f = np.arange(L)[None, :]
    w = 2 * np.pi * ((t * f) % NFFT) / NFFT
    re, im = np.cos(w), -np.sin(w)
    sign = 1.0 - 2.0 * (np.arange(L) % 2)
    im_packed = im.copy()
    im_packed[:, 0] = sign
    re_nyq = re[:, :P].copy()
    re_nyq[:, 0] = sign
    fwd = np.concatenate([re, im_packed, im[:, :P], re_nyq], 1)
    fwd = fwd.reshape(KT, P, 6 * P).transpose(1, 0, 2)
    weight = np.where(np.arange(L) == 0, 1.0, 2.0)[:, None] / NFFT
    ire = weight * re.T
    iim = weight * im.T
    iim[0] = sign / NFFT
    inv = np.concatenate([ire, iim], 0).reshape(2 * FREQ_TILES, P, L).transpose(1, 0, 2)
    return {
        "cst": c, "csb": b.astype(mybir.dt.np(BF16)),
        "fwd": np.ascontiguousarray(fwd, np.float32), "inv": np.ascontiguousarray(inv, np.float32),
    }


def build(nc, d):
    x_rows = nc.dram_tensor("x_rows", (X_ROWS, D), F32, kind="Internal").ap()
    y_rows = nc.dram_tensor("y_rows", (CHUNKS * P, D), F32, kind="Internal").ap()

    with ExitStack() as ctx:
        def sb(name, shape, dt=F32):
            return ctx.enter_context(nc.sbuf_tensor(name, shape, dt))

        def sem(name):
            return ctx.enter_context(nc.semaphore(name))

        bank = ctx.enter_context(nc.psum_tensor("bank", [P, 8, 512], F32))

        cst, csb = sb("cst", [P, CST_N]), sb("csb", [P, CSB_N], BF16)
        ident, iota, region = cst[:, 0:128], cst[:, 128:192], cst[:, 192:256]
        even, odd, chunk_no = cst[:, 256:257], cst[:, 257:258], cst[:, 258:260]
        identb, onesb, beforeb = csb[:, 0:128], csb[:, 128:256], csb[:, 256:384]
        mask0, mask1 = csb[:, 384:896], csb[:, 896:1408]
        vec = sb("vec", [P, VEC_N])
        fwd, inv = sb("fwd", [P, KT, 6 * P]), sb("inv", [P, 2 * FREQ_TILES, L])
        ssm = sb("ssm", [P, KT, D])
        a_w = {n: sb(f"a_w{n}", [P, KT, D]) for n in "qkvo"}
        bo = sb("bo", [P, D])
        b_w = {n: sb(f"b_w{n}", [P, KT, D]) for n in "qkv"}
        b_wo = sb("b_wo", [P, KT, D])
        b_a, b_b = sb("b_a", [P, KT, R_MOD]), sb("b_b", [R_MOD, F_MLP])
        w_in, w_up = sb("w_in", [P, KT, F_MLP]), sb("w_up", [P, KT, F_MLP])
        w_down = sb("w_down", [P, FT, D])
        d_w = {n: sb(f"d_w{n}", [P, KT, D]) for n in "qkvo"}
        gate_w = sb("gate_w", [P, KT, E_N])
        sh_gu = sb("sh_gu", [P, KT, 2 * SH_I])
        sh_dn = sb("sh_dn", [P, len(SH_TILES), D])

        X = sb("X", [P, NT, D])
        TOPW = sb("TOPW", [P, NT, TOPK])
        TOPI = sb("TOPI", [P, NT, 8])
        DEST = sb("DEST", [P, NT, TOPK])

        uT = sb("uT", [P, KT, L])
        q_sb, k_sb = sb("q_sb", [P, KT, L + 2]), sb("k_sb", [P, KT, L + 2])
        v_sb, qc, kc = sb("v_sb", [P, KT, L]), sb("qc", [P, KT, L]), sb("kc", [P, KT, L])
        kv, kvT = sb("kv", [P, KT, L]), sb("kvT", [P, TT, D])
        tabA, tabB, tabD = (sb(n, [P, FREQ_TILES, D]) for n in ("tabA", "tabB", "tabD"))
        products = sb("products", [P, 4, FREQ_TILES, D])
        pr = [products[:, n] for n in range(4)]
        Yre, Yim = pr[0], pr[2]
        z = sb("z", [P, KT, L])
        xn = sb("xn", [P, TT, D])
        d_kv = sb("d_kv", [P, KT, L])
        nrm = {}
        for s, r in (("A", qc), ("B", xn), ("D", d_kv)):
            nrm[s] = dict(r=r, st=sb(f"st{s}", [P, TT, 6]), mv=sb(f"mv{s}", [P, TT, 2]),
                          v=sb(f"v{s}", [P, TT]), i=sb(f"i{s}", [P, TT], I32), y=sb(f"y{s}", [P, TT]),
                          t=sb(f"t{s}", [P, TT]))
        ms = sb("ms", [P, TT])
        h1T, h2T = sb("h1T", [P, KT, L]), sb("h2T", [P, KT, L])
        qm = [sb("qE", [P, KT, L]), sb("qO", [P, KT, L])]
        kT = sb("kT", [P, KT, L])
        v1 = sb("v1", [P, TT, HEADS, HD + 1])
        UNITS = GROUPS + 2 * GROUPS
        nmx = sb("nmx", [P, UNITS, 4])
        prob, probT = sb("prob", [P, 2, 512]), sb("probT", [P, 2, 4, P])
        rec, att = sb("rec", [P, TT, HEADS]), sb("att", [P, TT, D])
        attT = sb("attT", [P, KT, L])
        woa = sb("woa", [P, KT, R_MOD])
        th, mh = sb("th", [R_MOD, L]), sb("mh", [R_MOD, L])
        gt, gs = sb("gt", [P, 2, L]), sb("gs", [P, 2, L])
        actT = sb("actT", [P, FT, L])
        x2, x2T = sb("x2", [P, TT, D]), sb("x2T", [P, KT, L])
        d_k, d_cs, vh = (sb(n, [P, KT, L]) for n in ("d_k", "d_cs", "vh"))
        ones_row = sb("ones_row", [P, L])
        x3, x3T = sb("x3", [P, TT, D]), sb("x3T", [P, KT, L])
        lg8, nlg = sb("lg8", [P, TT, 8]), sb("nlg", [P, TT])
        ex, top8, top8i = sb("ex", [P, TT, E_N]), sb("top8", [P, TT, 8]), sb("top8i", [P, TT, 8], U32)
        idxf, wsum, wrec = sb("idxf", [P, TT, 8]), sb("wsum", [P, TT]), sb("wrec", [P, TT])
        mk, mkb = sb("mk", [P, TT, E_N]), sb("mkb", [P, TT, E_N], BF16)
        seen = sb("seen", [P, E_N], BF16)
        pos, hit = sb("pos", [P, TT, E_N]), sb("hit", [P, TT, TOPK, E_N])
        destf, desti = sb("destf", [P, TT, TOPK]), sb("desti", [P, TT * TOPK], I32)
        sgt, sgs, sact = sb("sgt", [P, L]), sb("sgs", [P, L]), sb("sact", [P, len(SH_TILES), L])
        zeros = sb("zeros", [P, D])
        spare = sb("spare", [P, 2])
        cn, cum, before_e = sb("cn", [P, E_N]), sb("cum", [P, E_N]), sb("before_e", [P, E_N])
        shift_e, pad_e = sb("shift_e", [P, E_N]), sb("pad_e", [P, E_N])
        ce, cb, co, crow = (sb(n, [P, 2]) for n in ("ce", "cb", "co", "crow"))
        ctab, table = sb("ctab", [P, 4]), sb("table", [1, 4 * P], I32)
        scr = sb("scr", [P, 3, E_N])
        dead = [[t[:].rearrange("p a b -> p (a b)"), 0] for t in (w_in, w_up, w_down, fwd, inv, sh_gu)]

        def again(rows, a, b):
            for t in dead:
                if t[1] + a * b <= t[0].shape[1]:
                    at, t[1] = t[1], t[1] + a * b
                    return t[0][0:rows, at:at + a * b].rearrange("p (a b) -> p a b", a=a)

        def ring(n, *shape):
            return [again(*shape) for _ in range(n)]

        w2, w1 = ring(RING, IH, 2, D), ring(RING, P, KT, I_N)
        xc = ring(RING, P, KT, P)
        xcT, hs = ring(3, P, KT, P), ring(3, IH, 2, P)
        yc, outb = ring(3, P, 1, D), ring(2, P, 1, D)
        yc, outb = [t[:, 0, :] for t in yc], [t[:, 0, :] for t in outb]
        yg = [actT[:].rearrange("p a b -> p (a b)")[:, 0:TOPK * D].rearrange("p (k d) -> p k d", k=TOPK),
              products[:].rearrange("p n f d -> p (n f) d")[:, 0:TOPK, :]]
        look = hit[:, 0, :, :]
        ROWF, rowi = sb("ROWF", [P, NT, TOPK]), [sb(f"rowi{n}", [P, TOPK], I32) for n in range(2)]

        S = {n: sem(n) for n in (
            "p_spare ld_u ld_uT ld_cst ld_a ld_ssm ld_b ld_d set_pool set_dve set_pe set_tab set_woa ub "
            "a_q a_k a_v a_q_out a_k_out a_v_out a_qc a_kc a_kv a_kvT a_kvT_out a_X a_pr a_Y a_y a_z a_zq a_o a_r a_x1 "
            "b_ms b_xn b_hT b_h1 b_h2 b_q b_k b_v b_qm b_k_out b_v_out b_s b_max b_exp b_pT b_pT_out b_pv b_att "
            "b_attT b_attT_out b_mod b_tanh b_mh b_gu b_gt b_act b_dn b_r b_x2 "
            "d_xT d_xT_out d_q d_k_ps d_v d_k_out d_kv d_vh d_o d_r d_x3 d_x3T d_x3T_out d_lg d_max d_ex d_mask "
            "d_rank d_pos d_dest d_scat d_sg d_sgt d_sact d_sd d_base "
            "ch_a ch_b ch_d ch_r ch_f ch_w r_tot r_tab r_row r_table r_fill "
            "m_w0 m_x0 m_w1 m_x1 m_w2 m_x2 m_w3 m_x3 m_w4 m_x4 m_w5 m_x5 m_xT m_xT_out m_h m_hs m_y m_y_out m_st0 m_st1 m_st2 "
            "f_rows f_row f_g0 f_g1 f_used f_out f_st0 f_st1").split()}

        def need(eng, name, value):
            if isinstance(value, int) and value <= 0:
                return
            eng.wait_ge(S[name], value)

        def first(b):
            return isinstance(b, int) and b == 0

        def alone(eng):
            if eng.engine == nc.vector.engine:
                eng.memset(spare[:, 0:1], 0.0)
            else:
                eng.tensor_tensor(spare[:, 1:2], ones_row[:, 0:1], ones_row[:, 1:2], ALU.mult).then_inc(S["p_spare"], 1)

        class Chain:

            def __init__(self, eng, name, per):
                self.eng, self.name, self.per, self.k, self.b = eng, name, per, 0, 0

            def start(self, b):
                self.b, self.k = b, 0

            def step(self, ins):
                self.k += 1
                ins.then_inc(S[self.name], 1)

            def wait(self):
                self.eng.wait_ge(S[self.name], self.b * self.per + self.k)

            def link(self, ins):
                self.step(ins)
                self.wait()

        TURN = ["B1", "D1", "A1", "B2", "D2", "B3", "A2", "B4", "D3", "A3", "B5", "D4", "A4", "B6", "D5", "B7", "A5",
                "D6", "B8"]
        LAG = {"A": 0, "B": 1, "D": 2}

        def turns(eng, parts):
            def turn(it):
                for name in TURN:
                    b = it - LAG[name[0]]
                    if isinstance(b, int) and not 0 <= b < NB:
                        continue
                    if name in parts:
                        parts[name](b)
            for it in range(3):
                turn(it)
            with eng.Fori(3, NB) as it:
                turn(it)
            turn(NB)
            turn(NB + 1)

        class Chunk:

            def __init__(self, i, off):
                self.i, self.off, self.no = i, off, i * RING + off

            def slot(self, n):
                return self.off % n

            def before(self, n):
                return self.i * (RING // n) + self.off // n

        def chunk_loop(eng, skewed, each=None):
            def step(i, off):
                for lag, work in enumerate(skewed):
                    c = Chunk(i, off - lag)
                    if not isinstance(c.no, int) or 0 <= c.no < CHUNKS:
                        work(c)

            def body(i):
                for off in range(HEAD, HEAD + RING):
                    step(i, off)

            turns_in_all = (CHUNKS - HEAD) // RING
            assert HEAD + turns_in_all * RING == CHUNKS and NT < turns_in_all
            for off in range(HEAD):
                step(0, off)
            if each:
                with eng.Fori(0, NT) as i:
                    body(i)
                    each(i)
                with eng.Fori(NT, turns_in_all) as i:
                    body(i)
            else:
                with eng.Fori(0, turns_in_all) as i:
                    body(i)
            for off in range(CHUNKS, CHUNKS + len(skewed) - 1):
                step(0, off)

        def unit_heads(u):
            if u < GROUPS:
                return [(u, eh, par) for eh in range(KT) for par in range(2)]
            return [((u - GROUPS) // KT, (u - GROUPS) % KT, par) for par in range(2)]

        block = ctx.enter_context(nc.Block())

        def psum(n, a=0, b=512):
            return bank[:, n, a:b]

        def psum3(n):
            return bank[:, n, :].rearrange("p (a b) -> p a b", a=2)

        @block.sync
        def _(sp):
            sp.dma_start(cst[:], d["cst"]).then_inc(S["ld_cst"], 16)
            sp.dma_start(vec[:], d["vec"]).then_inc(S["ld_cst"], 16)
            for n in "qkv":
                sp.dma_start(a_w[n][:], d[f"a_w{n}"]).then_inc(S["ld_a"], 16)
            sp.dma_start(uT[:], d["uT"][0]).then_inc(S["ld_uT"], 16)
            sp.dma_start(fwd[:], d["fwd"]).then_inc(S["ld_ssm"], 16)
            sp.dma_start(ssm[:], d["ssm"]).then_inc(S["ld_ssm"], 16)
            sp.dma_start(inv[:], d["inv"]).then_inc(S["ld_ssm"], 16)
            sp.dma_start(a_w["o"][:], d["a_wo"]).then_inc(S["ld_ssm"], 16)
            for n in "qkv":
                sp.dma_start(b_w[n][:], d[f"b_w{n}"]).then_inc(S["ld_b"], 16)
            for t, n in ((b_wo, "b_wo"), (b_a, "b_a"), (b_b, "b_b"), (w_in, "w_in"), (w_up, "w_up"), (w_down, "w_down")):
                sp.dma_start(t[:], d[n]).then_inc(S["ld_b"], 16)
            for n in "qkvo":
                sp.dma_start(d_w[n][:], d[f"d_w{n}"]).then_inc(S["ld_d"], 16)
            sp.dma_start(gate_w[:], d["gate_w"]).then_inc(S["ld_d"], 16)
            sp.dma_start(sh_gu[:], d["sh_gu"]).then_inc(S["ld_d"], 16)
            sp.dma_start(sh_dn[:, 0:2, :], d["sh_dn"][0:256].rearrange("(k p) n -> p k n", p=P)).then_inc(S["ld_d"], 16)
            sp.dma_start(sh_dn[0:SH_I - 256, 2, :], d["sh_dn"][256:SH_I]).then_inc(S["ld_d"], 16)
            sp.wait_ge(S["set_pool"], 1)
            front = x_rows.rearrange("(e c) d -> c e d", c=CAP)[0:P]
            sp.dma_start(front, zeros[:].rearrange("p (o d) -> p o d", o=1).broadcast_to([P, E_N + 1, D])).then_inc(S["r_fill"], 16)
            with sp.Fori(1, NB) as b:
                sp.wait_ge(S["a_v"], b)
                sp.dma_start(uT[:], d["uT"][bass.ds(b, 1)].rearrange("o p k l -> p (o k) l")).then_inc(S["ld_uT"], 16)
            sp.wait_ge(S["r_table"], 1)
            sp.wait_ge(S["d_scat"], 16 * TT * TOPK * NB)

            why = "the table was clamped where it was worked out"

            def load(c):
                at = slice(2 * c.no, 2 * c.no + 2) if isinstance(c.no, int) else bass.ds(c.no * 2, 2)
                e, row = nc.values_load_multi_w_load_instructions(table[0:1, at], engines=(sp.engine,), min_val=0,
                                                                  max_val=X_ROWS - P, skip_runtime_bounds_check_because=why)[1]
                e = nc.s_assert_within(e, 0, E_N - 1, skip_runtime_bounds_check_because=why)
                s = c.slot(RING)
                need(sp, "m_xT", c.no - (RING - 1))
                sp.dma_start(xc[s], x_rows[bass.ds(row, P), :].rearrange("p (a b) -> p a b", a=KT)).then_inc(S[f"m_x{s}"], 16)
                need(sp, "m_h", c.no - (RING - 1))
                sp.dma_start(w1[s], d["e_w1"][bass.ds(e, 1)].rearrange("o p k i -> p (o k) i")).then_inc(S[f"m_w{s}"], 16)
                need(sp, "m_y", c.no - (RING - 1))
                sp.dma_start(w2[s], d["e_w2"][bass.ds(e, 1)].rearrange("o p k h -> p (o k) h")).then_inc(S[f"m_w{s}"], 16)

            chunk_loop(sp, [load])

        @block.gpsimd
        def _(pool):
            for t in (q_sb, k_sb):
                pool.memset(t[:, :, 0:2], 0.0)
            pool.memset(v1[:, :, :, HD:HD + 1], 1.0)
            pool.memset(ones_row[:], 1.0)
            pool.memset(seen[:], 0.0)
            pool.memset(zeros[:], 0.0).then_inc(S["set_pool"], 1)
            pool.wait_ge(S["ld_u"], 32)
            pool.tensor_tensor(X[:], X[:], bo[:].rearrange("p (o n) -> p o n", o=1).broadcast_to([P, NT, D]),
                               ALU.add).then_inc(S["ub"], 1)

            def A3(b):
                need(pool, "a_pr", b + 1)
                pool.tensor_tensor(Yre, pr[0], pr[1], ALU.subtract)
                pool.tensor_tensor(Yim, pr[2], pr[3], ALU.add).then_inc(S["a_Y"], 1)

            def D6(b):
                need(pool, "p_spare", b)
                if first(b):
                    pool.wait_ge(S["r_fill"], 16)
                need(pool, "d_dest", b + 1)
                alone(pool)
                for tt in range(TT):
                    for k in range(TOPK):
                        n = tt * TOPK + k
                        pool.indirect_dma_start(x_rows, bass.IndirectOffsetOnAxis(ap=desti[:, n:n + 1].bitcast(U32), axis=0),
                                                x3[:, tt, :], None).then_inc(S["d_scat"], 16)

            turns(pool, {"A3": A3, "D6": D6})

            def gather(i, s, nth):
                need(pool, "p_spare", NB + i)
                need(pool, "f_row", i + 1)
                need(pool, "f_used", i - 1)
                alone(pool)
                for k in range(TOPK):
                    pool.indirect_dma_start(yg[s][:, k, :], None, y_rows,
                                            bass.IndirectOffsetOnAxis(ap=rowi[s][:, k:k + 1].bitcast(U32), axis=0)
                                            ).then_inc(S[f"f_g{s}"], 16)

            for s in range(3):
                pool.wait_ge(S[f"m_st{s}"], 16 * (CHUNKS // 3))
            gather(0, 0, 0)
            gather(1, 1, 0)
            with pool.Fori(1, NT // 2) as i:
                gather(i * 2, 0, i)
                gather(i * 2 + 1, 1, i)

        @block.tensor
        def _(pe):
            def project(out, w, x):
                for eh in range(KT):
                    for kt in range(KT):
                        mm = pe.matmul(out[:, eh * L:(eh + 1) * L], w[:, kt, eh * P:(eh + 1) * P], x[:, kt, :],
                                       start=(kt == 0), stop=(kt == KT - 1))
                return mm

            def by_token(out, x, w):
                for tt in range(TT):
                    for kt in range(KT):
                        mm = pe.matmul(out[:, tt * D:(tt + 1) * D], x[:, kt, tt * P:(tt + 1) * P], w[:, kt, :],
                                       start=(kt == 0), stop=(kt == KT - 1))
                return mm

            def turn_tiles(out, x):
                for a in range(2):
                    for b in range(2):
                        t = pe.transpose(out[:, b * 256 + a * P:b * 256 + (a + 1) * P], x[:, a, b * P:(b + 1) * P], ident)
                return t

            pe.wait_ge(S["ld_cst"], 48)
            pe.wait_ge(S["ld_ssm"], 64)
            for n, tile0, tile1 in ((0, 0, 1), (1, 4, 3), (2, 5, 1)):
                for ft, m in enumerate((tile0, tile1)):
                    for kt in range(KT):
                        mm = pe.matmul(psum(n, ft * D, (ft + 1) * D), fwd[:, kt, m * P:(m + 1) * P], ssm[:, kt, :],
                                       start=(kt == 0), stop=(kt == KT - 1))
                mm.then_inc(S["set_pe"], 1)

            def A1(b):
                need(pe, "ld_uT", b * 16 + 16)
                if first(b):
                    pe.wait_ge(S["ld_a"], 48)
                need(pe, "a_z", b)
                project(psum(4), a_w["q"], uT).then_inc(S["a_q"], 1)
                need(pe, "a_r", b)
                project(psum(5), a_w["k"], uT).then_inc(S["a_k"], 1)
                need(pe, "a_q_out", b + 1)
                project(psum(4), a_w["v"], uT).then_inc(S["a_v"], 1)

            def A2(b):
                need(pe, "a_kv", b + 1)
                need(pe, "a_k_out", b + 1)
                turn_tiles(psum(5), kv).then_inc(S["a_kvT"], 1)

            def A3(b):
                need(pe, "a_kvT_out", b + 1)
                need(pe, "a_v_out", b + 1)
                for n in range(4):
                    for kt in range(KT):
                        mm = pe.matmul(psum(4 + n // 2, (n % 2) * D, (n % 2 + 1) * D), fwd[:, kt, n * P:(n + 1) * P],
                                       kvT[:, kt, :], start=(kt == 0), stop=(kt == KT - 1))
                mm.then_inc(S["a_X"], 1)

            def A4(b):
                need(pe, "a_Y", b + 1)
                for dh in range(KT):
                    for n in range(2 * FREQ_TILES):
                        y = Yre if n < FREQ_TILES else Yim
                        mm = pe.matmul(psum(4, dh * L, (dh + 1) * L), y[:, n % FREQ_TILES, dh * P:(dh + 1) * P],
                                       inv[:, n, :], start=(n == 0), stop=(n == 2 * FREQ_TILES - 1))
                mm.then_inc(S["a_y"], 1)

            def A5(b):
                need(pe, "a_zq", b + 1)
                by_token(psum(5), z, a_w["o"]).then_inc(S["a_o"], 1)

            def B1(b):
                if first(b):
                    pe.wait_ge(S["ld_b"], 144)
                    for eh in range(KT):
                        for kt in range(KT):
                            mm = pe.matmul(psum(1, eh * R_MOD, (eh + 1) * R_MOD), b_wo[:, kt, eh * P:(eh + 1) * P],
                                           b_a[:, kt, :], start=(kt == 0), stop=(kt == KT - 1))
                    mm.then_inc(S["set_woa"], 1)
                    pe.wait_ge(S["set_dve"], 2)
                need(pe, "b_xn", b + 1)
                need(pe, "b_act", b * FT)
                turn_tiles(psum(0), xn).then_inc(S["b_hT"], 1)

            def B2(b):
                need(pe, "b_h1", b + 1)
                need(pe, "b_r", b)
                project(psum(1), b_w["q"], h1T).then_inc(S["b_q"], 1)
                project(psum(2), b_w["k"], h1T).then_inc(S["b_k"], 1)
                by_token(psum(3), h1T, b_w["v"]).then_inc(S["b_v"], 1)

            def scores(b, u):
                if u == 0:
                    need(pe, "b_h2", b + 1)
                    need(pe, "b_qm", b + 1)
                    need(pe, "b_k_out", b + 1)
                if u >= 2:
                    need(pe, "b_exp", b * UNITS + u - 1)
                n = u % 2
                pe.matmul(psum(n), identb, mask0 if u < GROUPS else mask1, start=True, stop=False, skip_group_check=True)
                for h, (g, eh, par) in enumerate(unit_heads(u)):
                    rows = slice(PAIR * g, PAIR * (g + 1))
                    if u < GROUPS:
                        out, qs, ks = psum(n, h * P, (h + 1) * P), slice(0, P), slice(0, P)
                    else:
                        out, qs, ks = psum(n, h * L, (h + 1) * L), slice(P, L), slice(0, L)
                    mm = pe.matmul(out, qm[par][rows, eh, qs], kT[rows, eh, ks], start=False, stop=True,
                                   tile_position=(PAIR * g, 0), skip_group_check=True)
                mm.then_inc(S["b_s"], 1)

            def turn_probs(b, u):
                need(pe, "b_exp", b * UNITS + u + 1)
                if u == 0:
                    need(pe, "b_k_out", b + 1)
                else:
                    need(pe, "b_pT_out", b * UNITS + u)
                for j in range(4):
                    t = pe.transpose(psum(2, j * P, (j + 1) * P), prob[:, u % 2, j * P:(j + 1) * P], ident)
                t.then_inc(S["b_pT"], 1)

            def values(b, u):
                need(pe, "b_pT_out", b * UNITS + u + 1)
                if u == 0:
                    need(pe, "b_v_out", b + 1)
                if u == GROUPS:
                    need(pe, "b_att", b * 2 + 1)
                for h, (g, eh, par) in enumerate(unit_heads(u)):
                    head = eh * 8 + 2 * g + par
                    out = psum(3, head * (HD + 1), (head + 1) * (HD + 1))
                    if u < GROUPS:
                        mm = pe.matmul(out, probT[:, u % 2, h, :], v1[:, 0, head, :], start=True, stop=True)
                    else:
                        for kt in range(TT):
                            mm = pe.matmul(out, probT[:, u % 2, 2 * h + kt, :], v1[:, kt, head, :],
                                           start=(kt == 0), stop=(kt == TT - 1))
                mm.then_inc(S["b_pv"], 1)

            def attention(b, lo, hi):
                for u in range(lo, hi):
                    if u < UNITS:
                        scores(b, u)
                    if 1 <= u <= UNITS:
                        turn_probs(b, u - 1)
                    if 2 <= u:
                        values(b, u - 2)

            def B6(b):
                need(pe, "b_att", b * 2 + 2)
                turn_tiles(psum(0), att).then_inc(S["b_attT"], 1)
                need(pe, "b_attT_out", b + 1)
                for kt in range(KT):
                    pe.matmul(bank[0:R_MOD, 1, 0:L], woa[:, kt, :], attT[:, kt, :], start=(kt == 0), stop=(kt == KT - 1))
                for kt in range(KT):
                    mm = pe.matmul(bank[0:R_MOD, 1, L:2 * L], b_a[:, kt, :], h2T[:, kt, :], start=(kt == 0), stop=(kt == KT - 1))
                mm.then_inc(S["b_mod"], 1)

            def B7(b):
                for f in range(FT):
                    n = (0, 2, 3)[f % 3]
                    cols = slice(f * P, (f + 1) * P)
                    if f >= 3:
                        need(pe, "b_act", b * FT + f - 2)
                    for kt in range(KT):
                        pe.matmul(psum(n, L, 2 * L), w_up[:, kt, cols], h2T[:, kt, :], start=(kt == 0), stop=(kt == KT - 1))
                    for kt in range(KT):
                        pe.matmul(psum(n, 0, L), w_in[:, kt, cols], h2T[:, kt, :], start=(kt == 0), stop=False)
                    if f == 0:
                        need(pe, "b_mh", b + 1)
                    pe.matmul(psum(n, 0, L), b_b[:, cols], mh[:], start=False, stop=True).then_inc(S["b_gu"], 1)

            def B8(b):
                for tt in range(TT):
                    for f in range(FT):
                        if tt == 0:
                            need(pe, "b_act", b * FT + f + 1)
                        mm = pe.matmul(psum(1, tt * D, (tt + 1) * D), actT[:, f, tt * P:(tt + 1) * P], w_down[:, f, :],
                                       start=(f == 0), stop=(f == FT - 1))
                mm.then_inc(S["b_dn"], 1)

            def D1(b):
                need(pe, "b_x2", b + 1)
                need(pe, "d_base", b)
                turn_tiles(psum(6), x2).then_inc(S["d_xT"], 1)

            def D2(b):
                if first(b):
                    pe.wait_ge(S["ld_d"], 128)
                need(pe, "d_xT_out", b + 1)
                need(pe, "d_sact", b * 3)
                project(psum(7), d_w["k"], x2T).then_inc(S["d_k_ps"], 1)
                project(psum(6), d_w["v"], x2T).then_inc(S["d_v"], 1)
                need(pe, "d_k_out", b + 1)
                project(psum(7), d_w["q"], x2T).then_inc(S["d_q"], 1)

            def D3(b):
                need(pe, "d_vh", b + 1)
                by_token(psum(6), vh, d_w["o"]).then_inc(S["d_o"], 1)

            def D4(b):
                need(pe, "d_x3", b + 1)
                turn_tiles(psum(7), x3).then_inc(S["d_x3T"], 1)
                need(pe, "d_x3T_out", b + 1)
                need(pe, "d_r", b + 1)
                for tt in range(TT):
                    for kt in range(KT):
                        mm = pe.matmul(psum(6, tt * E_N, (tt + 1) * E_N), x3T[:, kt, tt * P:(tt + 1) * P], gate_w[:, kt, :],
                                       start=(kt == 0), stop=(kt == KT - 1))
                mm.then_inc(S["d_lg"], 1)

            def shared(b, n, bk):
                at, w = SH_TILES[n]
                for g in range(2):
                    for kt in range(KT):
                        mm = pe.matmul(bank[0:w, bk, g * L:(g + 1) * L], sh_gu[:, kt, g * SH_I + at:g * SH_I + at + w],
                                       x3T[:, kt, :], start=(kt == 0), stop=(kt == KT - 1))
                mm.then_inc(S["d_sg"], 1)

            def D5(b):
                shared(b, 0, 7)
                need(pe, "d_mask", b + 1)
                pe.matmul(psum(6, 128, 192), beforeb, mkb[:, 0, :], start=True, stop=False)
                pe.matmul(psum(6, 128, 192), onesb, seen[:], start=False, stop=True)
                pe.matmul(psum(6, 192, 256), beforeb, mkb[:, 1, :], start=True, stop=False)
                pe.matmul(psum(6, 192, 256), onesb, mkb[:, 0, :], start=False, stop=False)
                pe.matmul(psum(6, 192, 256), onesb, seen[:], start=False, stop=True).then_inc(S["d_rank"], 1)
                need(pe, "d_sact", b * 3 + 1)
                shared(b, 1, 7)

            def D6(b):
                need(pe, "d_pos", b + 1)
                shared(b, 2, 6)
                need(pe, "d_sact", b * 3 + 3)
                for tt in range(TT):
                    for n, (_, w) in enumerate(SH_TILES):
                        mm = pe.matmul(psum(6, tt * D, (tt + 1) * D), sact[0:w, n, tt * P:(tt + 1) * P], sh_dn[0:w, n, :],
                                       start=(n == 0), stop=(n == len(SH_TILES) - 1))
                mm.then_inc(S["d_sd"], 1)

            turns(pe, {"A1": A1, "A2": A2, "A3": A3, "A4": A4, "A5": A5, "B1": B1, "B2": B2,
                       "B3": lambda b: attention(b, 0, 5), "B4": lambda b: attention(b, 5, 10),
                       "B5": lambda b: attention(b, 10, UNITS + 2), "B6": B6, "B7": B7, "B8": B8,
                       "D1": D1, "D2": D2, "D3": D3, "D4": D4, "D5": D5, "D6": D6})

            pe.wait_ge(S["d_pos"], NB)
            pe.wait_ge(S["d_base"], NB)
            pe.wait_ge(S["d_dest"], NB)
            pe.matmul(psum(6, 0, E_N), onesb, seen[:], start=True, stop=True).then_inc(S["r_tot"], 1)
            pe.wait_ge(S["r_tab"], 1)
            for j in range(4):
                mm = pe.matmul(bank[0:1, 7, :].rearrange("o (c j) -> o c j", j=4)[:, :, j], ctab[:, j:j + 1], ident,
                               start=True, stop=True)
            mm.then_inc(S["r_row"], 1)

            def turn_rows(c):
                s, out = c.slot(RING), psum(c.slot(3))
                need(pe, f"m_x{s}", c.before(RING) * 16 + 16)
                need(pe, "m_xT_out", c.no - 2)
                for kt in range(KT):
                    t = pe.transpose(out[:, kt * P:(kt + 1) * P], xc[s][:, kt, :], ident)
                t.then_inc(S["m_xT"], 1)

            def inner(c):
                s, n = c.slot(RING), c.slot(3)
                need(pe, f"m_w{s}", c.before(RING) * 32 + 32)
                need(pe, "m_xT_out", c.no + 1)
                need(pe, "m_hs", c.no - 2)
                for m in range(2):
                    for kt in range(KT):
                        mm = pe.matmul(bank[0:IH, 3 + n, m * P:(m + 1) * P], w1[s][:, kt, m * IH:(m + 1) * IH], xcT[n][:, kt, :],
                                       start=(kt == 0), stop=(kt == KT - 1))
                mm.then_inc(S["m_h"], 1)

            def outer(c):
                s, n = c.slot(RING), c.slot(3)
                need(pe, "m_hs", c.no + 1)
                need(pe, "m_y_out", c.no - 1)
                for m in range(2):
                    mm = pe.matmul(psum(6 + c.slot(2), 0, D), hs[n][:, m, :], w2[s][:, m, :], start=(m == 0), stop=(m == 1))
                mm.then_inc(S["m_y"], 1)

            chunk_loop(pe, [turn_rows, inner, outer])

        @block.scalar
        def _(act):
            act.dma_start(csb[:], d["csb"]).then_inc(S["ld_cst"], 16)
            act.dma_start(X[:], d["u"].rearrange("b (t p) d -> p (b t) d", p=P)).then_inc(S["ld_u"], 16)
            act.dma_start(bo[:], d["bo"]).then_inc(S["ld_u"], 16)

            def column(name, kt):
                return vec[:, VEC[name] + kt:VEC[name] + kt + 1]

            act.wait_ge(S["ld_cst"], 48)
            act.wait_ge(S["set_pool"], 1)

            def A1(b):
                for n, dst, at, bk, used in (("q", q_sb, 2, 4, "a_qc"), ("k", k_sb, 2, 5, "a_kc"), ("v", v_sb, 0, 4, "a_kv")):
                    need(act, f"a_{n}", b + 1)
                    need(act, used, b)
                    for eh in range(KT):
                        i = act.activation(dst[:, eh, at:at + L], psum(bk, eh * L, (eh + 1) * L), ACT.Identity,
                                           bias=column("b" + n, eh))
                    i.then_inc(S[f"a_{n}_out"], 1)

            def A2(b):
                need(act, "a_kvT", b + 1)
                need(act, "a_X", b)
                act.activation(kvT[:], psum3(5), ACT.Copy).then_inc(S["a_kvT_out"], 1)

            def B1(b):
                need(act, "b_hT", b + 1)
                need(act, "b_v", b)
                for kt in range(KT):
                    i = act.activation(h1T[:, kt, :], psum(0, kt * L, (kt + 1) * L), ACT.Identity, scale=column("ln1", kt))
                i.then_inc(S["b_h1"], 1)
                need(act, "b_gu", b * FT)
                for kt in range(KT):
                    i = act.activation(h2T[:, kt, :], psum(0, kt * L, (kt + 1) * L), ACT.Identity, scale=column("ln2", kt))
                i.then_inc(S["b_h2"], 1)

            def B2(b):
                need(act, "b_k", b + 1)
                need(act, "b_s", b * UNITS)
                act.activation(kT[:], psum3(2), ACT.Copy).then_inc(S["b_k_out"], 1)
                need(act, "b_v", b + 1)
                need(act, "b_pv", b * UNITS)
                act.activation(v1[:, :, :, 0:HD], bank[:, 3, :].rearrange("p (t h e) -> p t h e", t=TT, h=HEADS),
                               ACT.Copy).then_inc(S["b_v_out"], 1)

            def attention(b, lo, hi):
                for u in range(lo, min(hi, UNITS)):
                    need(act, "b_max", b * UNITS + u + 1)
                    need(act, "b_pT", b * UNITS + u - 1 if u else b * UNITS - 1)
                    w = P if u < GROUPS else L
                    for h in range(512 // w):
                        i = act.activation(prob[:, u % 2, h * w:(h + 1) * w], psum(u % 2, h * w, (h + 1) * w), ACT.Exp,
                                           bias=nmx[:, u, h:h + 1])
                    i.then_inc(S["b_exp"], 1)

            def B6(b):
                need(act, "b_attT", b + 1)
                need(act, "b_mod", b)
                act.activation(attT[:], psum3(0), ACT.Copy).then_inc(S["b_attT_out"], 1)
                need(act, "b_mod", b + 1)
                need(act, "b_mh", b)
                act.activation(th[:], bank[0:R_MOD, 1, 0:L], ACT.Tanh).then_inc(S["b_tanh"], 1)

            def B7(b):
                for f in range(FT):
                    need(act, "b_gu", b * FT + f + 1)
                    need(act, "b_act", b * FT + f - 1 if f else b * FT - 1)
                    act.activation(gt[:, f % 2, :], psum((0, 2, 3)[f % 3], 0, L), ACT.Tanh, scale=0.5).then_inc(S["b_gt"], 1)

            def D1(b):
                need(act, "d_xT", b + 1)
                need(act, "d_q", b)
                act.activation(x2T[:], psum3(6), ACT.Copy).then_inc(S["d_xT_out"], 1)

            def D2(b):
                need(act, "d_k_ps", b + 1)
                need(act, "d_kv", b)
                act.activation(d_k[:], psum3(7), ACT.Copy, scale=float(D) ** 0.5 / L).then_inc(S["d_k_out"], 1)

            def D4(b):
                need(act, "d_x3T", b + 1)
                need(act, "d_sg", b * 3)
                act.activation(x3T[:], psum3(7), ACT.Copy).then_inc(S["d_x3T_out"], 1)
                need(act, "d_max", b + 1)
                for tt in range(TT):
                    i = act.activation(ex[:, tt, :], psum(6, tt * E_N, (tt + 1) * E_N), ACT.Exp, bias=nlg[:, tt:tt + 1])
                i.then_inc(S["d_ex"], 1)

            def shared(b, n, bk):
                w = SH_TILES[n][1]
                need(act, "d_sg", b * 3 + n + 1)
                need(act, "d_sact", b * 3 + n)
                act.activation(sgt[0:w, :], bank[0:w, bk, 0:L], ACT.Tanh, scale=0.5).then_inc(S["d_sgt"], 1)

            def D5(b):
                shared(b, 0, 7)
                shared(b, 1, 7)

            turns(act, {"A1": A1, "A2": A2, "B1": B1, "B2": B2, "B3": lambda b: attention(b, 0, 5),
                        "B4": lambda b: attention(b, 5, 10), "B5": lambda b: attention(b, 10, UNITS + 2),
                        "B6": B6, "B7": B7, "D1": D1, "D2": D2, "D4": D4, "D5": D5, "D6": lambda b: shared(b, 2, 6)})

            def silu(c):
                n = c.slot(3)
                need(act, "m_h", c.no + 1)
                need(act, "m_y", c.no - 2)
                act.activation(hs[n], bank[0:IH, 3 + n, 0:2 * P].rearrange("p (a b) -> p a b", a=2), ACT.Silu
                               ).then_inc(S["m_hs"], 1)

            def store(c):
                n = c.slot(3)
                need(act, "m_y_out", c.no + 1)
                rows = slice(c.no * P, (c.no + 1) * P) if isinstance(c.no, int) else bass.ds(c.no * P, P)
                act.dma_start(y_rows[rows, :], yc[n]).then_inc(S[f"m_st{n}"], 16)

            chunk_loop(act, [lambda c: None, silu, store])

            out = d["out"].rearrange("b (t p) d -> (b t) p d", p=P)
            def put(i, s):
                need(act, "f_out", i + 1)
                n = slice(i, i + 1) if isinstance(i, int) else bass.ds(i, 1)
                act.dma_start(out[n].rearrange("o p d -> p (o d)"), outb[s]).then_inc(S[f"f_st{s}"], 16)
            with act.Fori(0, NT // 2) as i:
                put(i * 2, 0)
                put(i * 2 + 1, 1)
            for s in range(2):
                act.wait_ge(S[f"f_st{s}"], 16 * (NT // 2))

        @block.vector
        def _(dve):
            ca, cbn, cd = Chain(dve, "ch_a", 21), Chain(dve, "ch_b", 43), Chain(dve, "ch_d", 39)

            def col(name, kt, n=1, j=0):
                at = VEC[name] + kt * n + j
                return vec[:, at:at + 1]

            def rsqrt(ch, m, var, eps, n=TT):
                v, i, y, t = (m[k][:, 0:n] for k in ("v", "i", "y", "t"))
                ch.link(dve.tensor_scalar(v, var, eps, None, ALU.add))
                ch.link(dve.tensor_scalar(i, v.bitcast(I32), 1, None, ALU.logical_shift_right))
                ch.link(dve.tensor_scalar(y.bitcast(I32), i, -1.0, float(RSQRT_MAGIC), ALU.mult, ALU.add))
                for _ in range(3):
                    ch.link(dve.tensor_tensor(t, y, y, ALU.mult))
                    ch.link(dve.tensor_tensor(t, t, v, ALU.mult))
                    ch.link(dve.tensor_scalar(t, t, -0.5, 1.5, ALU.mult, ALU.add))
                    ch.link(dve.tensor_tensor(y, y, t, ALU.mult))

            def norm(ch, m, outs, n=TT):
                for t in range(n):
                    i = dve.bn_stats(m["st"][:, t, :], m["r"][:, t, :])
                ch.link(i)
                alone(dve)
                for t in range(n):
                    i = dve.bn_aggr(m["mv"][:, t, :], m["st"][:, t, :])
                ch.link(i)
                rsqrt(ch, m, m["mv"][:, 0:n, 1], LN_EPS, n)
                for t in range(n):
                    i = dve.tensor_scalar(outs[t], m["r"][:, t, :], m["mv"][:, t, 0:1], m["y"][:, t:t + 1], ALU.subtract, ALU.mult)
                return i

            def slot(b, tt):
                n = b * TT + tt
                return X[:, n, :] if isinstance(n, int) else X[:, bass.ds(n, 1), :].rearrange("p o d -> p (o d)")

            def slots(t, b):
                return t[:, b * TT:(b + 1) * TT] if isinstance(b, int) else t[:, bass.ds(b * TT, TT)]

            dve.wait_ge(S["set_pe"], 3)
            for n, t in enumerate((tabA, tabB, tabD)):
                i = dve.tensor_copy(t[:], psum3(n))
            i.then_inc(S["set_dve"], 1)
            dve.wait_ge(S["set_dve"], 1)
            dve.wait_ge(S["ld_cst"], 48)
            dve.wait_ge(S["set_pool"], 1)

            def A1(b):
                ca.start(b)
                need(dve, "a_x1", b)
                for n, src, dst in (("q", q_sb, qc), ("k", k_sb, kc)):
                    need(dve, f"a_{n}_out", b + 1)
                    for eh in range(KT):
                        i = dve.tensor_scalar(dst[:, eh, :], src[:, eh, 2:2 + L], col(f"c{n}w", eh, 3, 2), col(f"c{n}b", eh),
                                              ALU.mult, ALU.add)
                    ca.link(i)
                    for j in (1, 0):
                        for eh in range(KT):
                            i = dve.scalar_tensor_tensor(dst[:, eh, :], src[:, eh, j:j + L], col(f"c{n}w", eh, 3, j),
                                                         dst[:, eh, :], ALU.mult, ALU.add)
                        if j == 1:
                            ca.link(i)
                    i.then_inc(S[f"a_{n}c"], 1)
                need(dve, "a_kc", b + 1)
                need(dve, "a_v_out", b + 1)
                need(dve, "a_kvT", b)
                dve.tensor_tensor(kv[:], kc[:], v_sb[:], ALU.mult).then_inc(S["a_kv"], 1)

            def A3(b):
                need(dve, "a_X", b + 1)
                need(dve, "a_y", b)
                for n, (bk, tab) in enumerate(((4, tabA), (5, tabB), (4, tabB), (5, tabD))):
                    i = dve.tensor_tensor(pr[n], psum3(bk), tab[:], ALU.mult)
                i.then_inc(S["a_pr"], 1)

            def A4(b):
                need(dve, "a_y", b + 1)
                need(dve, "a_kv", b + 1)
                for eh in range(KT):
                    i = dve.scalar_tensor_tensor(kv[:, eh, :], kv[:, eh, :], col("skip", eh), psum(4, eh * L, (eh + 1) * L),
                                                 ALU.mult, ALU.add)
                i.then_inc(S["a_z"], 1)
                need(dve, "a_z", b + 1)
                need(dve, "a_qc", b + 1)
                need(dve, "a_o", b)
                dve.tensor_tensor(z[:], kv[:], qc[:], ALU.mult).then_inc(S["a_zq"], 1)

            def A5(b):
                need(dve, "a_o", b + 1)
                if first(b):
                    dve.wait_ge(S["ub"], 1)
                m = nrm["A"]
                dve.tensor_tensor(m["r"][:], psum3(5), slots(X, b), ALU.add).then_inc(S["a_r"], 1)
                need(dve, "a_r", b + 1)
                norm(ca, m, [slot(b, tt) for tt in range(TT)]).then_inc(S["a_x1"], 1)

            def B1(b):
                cbn.start(b)
                if first(b):
                    dve.wait_ge(S["set_woa"], 1)
                    dve.tensor_copy(woa[:], psum(1, 0, KT * R_MOD).rearrange("p (k r) -> p k r", k=KT)).then_inc(S["set_dve"], 1)
                need(dve, "a_x1", b + 1)
                need(dve, "b_hT", b)
                need(dve, "b_x2", b)
                for tt in range(TT):
                    i = dve.scalar_tensor_tensor(xn[:, tt, :], slot(b, tt), 1.0 / D, slot(b, tt), ALU.mult, ALU.mult,
                                                 accum_out=ms[:, tt:tt + 1])
                cbn.link(i)
                m = nrm["B"]
                rsqrt(cbn, m, ms[:], RMS_EPS)
                for tt in range(TT):
                    i = dve.tensor_scalar(xn[:, tt, :], slot(b, tt), m["y"][:, tt:tt + 1], None, ALU.mult)
                i.then_inc(S["b_xn"], 1)

            def B2(b):
                need(dve, "b_q", b + 1)
                need(dve, "b_s", b * UNITS)
                for par, keep in enumerate((even, odd)):
                    i = dve.tensor_scalar(qm[par][:], psum3(1), keep, None, ALU.mult)
                i.then_inc(S["b_qm"], 1)

            def attention(b, lo, hi):
                for u in range(lo, hi):
                    if u < UNITS:
                        w = P if u < GROUPS else L
                        need(dve, "b_s", b * UNITS + u + 1)
                        need(dve, "b_exp", b * UNITS - UNITS + u + 1 if isinstance(b, int) else (b - 1) * UNITS + u + 1)
                        dve.tensor_reduce(nmx[:, u, 0:512 // w], bank[:, u % 2, :].rearrange("p (h k) -> p h k", k=w), AX, ALU.max,
                                          negate=True).then_inc(S["b_max"], 1)
                    if 1 <= u <= UNITS:
                        need(dve, "b_pT", b * UNITS + u)
                        need(dve, "b_pv", b * UNITS + u - 2 if u >= 2 else b * UNITS + u - 2)
                        dve.tensor_copy(probT[:, (u - 1) % 2, :, :], bank[:, 2, :].rearrange("p (j q) -> p j q", j=4)
                                        ).then_inc(S["b_pT_out"], 1)
                    for tt, last in enumerate((GROUPS, UNITS)):
                        if u == last + 1:
                            need(dve, "b_pv", b * UNITS + last)
                            o = psum(3, 0, HEADS * (HD + 1)).rearrange("p (h e) -> p h e", h=HEADS)
                            cbn.link(dve.reciprocal(rec[:, tt, :], o[:, :, HD]))
                            if tt == 0:
                                need(dve, "b_attT", b)
                            dve.tensor_tensor(att[:, tt, :].rearrange("p (h e) -> p h e", h=HEADS), o[:, :, 0:HD],
                                              rec[:, tt, :].rearrange("p (h o) -> p h o", o=1).broadcast_to([P, HEADS, HD]),
                                              ALU.mult).then_inc(S["b_att"], 1)

            def B6(b):
                need(dve, "b_tanh", b + 1)
                need(dve, "b_gu", b * FT)
                dve.scalar_tensor_tensor(mh[:], th[:], MOD_SCALE, bank[0:R_MOD, 1, L:2 * L], ALU.mult, ALU.mult
                                         ).then_inc(S["b_mh"], 1)

            def B7(b):
                if True:
                    need(dve, "b_dn", b)
                for f in range(FT):
                    n = (0, 2, 3)[f % 3]
                    need(dve, "b_gt", b * FT + f + 1)
                    cbn.link(dve.scalar_tensor_tensor(gs[:, f % 2, :], gt[:, f % 2, :], 1.0, psum(n, 0, L), ALU.add, ALU.mult))
                    dve.scalar_tensor_tensor(actT[:, f, :], gs[:, f % 2, :], 0.5, psum(n, L, 2 * L), ALU.mult, ALU.mult
                                             ).then_inc(S["b_act"], 1)

            def B8(b):
                need(dve, "b_dn", b + 1)
                m = nrm["B"]
                for tt in range(TT):
                    i = dve.scalar_tensor_tensor(m["r"][:, tt, :], slot(b, tt), 2.0, psum(1, tt * D, (tt + 1) * D), ALU.mult, ALU.add)
                i.then_inc(S["b_r"], 1)
                need(dve, "b_r", b + 1)
                need(dve, "d_r", b)
                need(dve, "d_xT", b)
                norm(cbn, m, [x2[:, tt, :] for tt in range(TT)]).then_inc(S["b_x2"], 1)

            def D2(b):
                cd.start(b)
                need(dve, "d_x3", b)
                need(dve, "d_k_out", b + 1)
                need(dve, "d_v", b + 1)
                dve.tensor_tensor(d_kv[:], d_k[:], psum3(6), ALU.mult).then_inc(S["d_kv"], 1)
                need(dve, "d_kv", b + 1)
                for eh in range(KT):
                    i = dve.tensor_tensor_scan(d_cs[:, eh, :], ones_row[:], d_kv[:, eh, :], 0.0, ALU.mult, ALU.add)
                cd.link(i)
                need(dve, "d_q", b + 1)
                need(dve, "d_o", b)
                dve.tensor_tensor(vh[:], psum3(7), d_cs[:], ALU.mult).then_inc(S["d_vh"], 1)

            def D3(b):
                need(dve, "d_o", b + 1)
                need(dve, "b_x2", b + 1)
                m = nrm["D"]
                dve.tensor_tensor(m["r"][:], psum3(6), x2[:], ALU.add).then_inc(S["d_r"], 1)
                need(dve, "d_r", b + 1)
                need(dve, "d_scat", b * 16 * TT * TOPK)
                norm(cd, m, [x3[:, tt, :] for tt in range(TT)]).then_inc(S["d_x3"], 1)

            def D4(b):
                need(dve, "d_lg", b + 1)
                alone(dve)
                for tt in range(TT):
                    i = dve.max(lg8[:, tt, :], psum(6, tt * E_N, (tt + 1) * E_N))
                cd.link(i)
                dve.tensor_scalar(nlg[:], lg8[:, :, 0], -1.0, None, ALU.mult).then_inc(S["d_max"], 1)
                need(dve, "d_ex", b + 1)
                alone(dve)
                for tt in range(TT):
                    i = dve.max(top8[:, tt, :], ex[:, tt, :])
                cd.link(i)
                alone(dve)
                for tt in range(TT):
                    i = dve.max_index(top8i[:, tt, :], top8[:, tt, :], ex[:, tt, :])
                cd.link(i)
                cd.link(dve.tensor_copy(idxf[:], top8i[:]))
                for k in range(TOPK):
                    for tt in range(TT):
                        if k == 0:
                            i = dve.tensor_scalar(mk[:, tt, :], iota, idxf[:, tt, 0:1], None, ALU.is_equal)
                        else:
                            dst = mkb if k == TOPK - 1 else mk
                            i = dve.scalar_tensor_tensor(dst[:, tt, :], iota, idxf[:, tt, k:k + 1], mk[:, tt, :], ALU.is_equal, ALU.add)
                    if k < TOPK - 1:
                        cd.link(i)
                i.then_inc(S["d_mask"], 1)
                cd.link(dve.tensor_reduce(wsum[:], top8[:, :, 0:TOPK], AX, ALU.add))
                cd.link(dve.reciprocal(wrec[:], wsum[:]))
                cd.step(dve.tensor_tensor(slots(TOPW, b), top8[:, :, 0:TOPK],
                                          wrec[:].rearrange("p (t o) -> p t o", o=1).broadcast_to([P, TT, TOPK]), ALU.mult))
                cd.link(dve.tensor_copy(slots(TOPI, b), idxf[:]))

            def shared(b, n, bk):
                w = SH_TILES[n][1]
                need(dve, "d_sgt", b * 3 + n + 1)
                cd.link(dve.scalar_tensor_tensor(sgs[0:w, :], sgt[0:w, :], 1.0, bank[0:w, bk, 0:L], ALU.add, ALU.mult))
                if n == 0:
                    need(dve, "d_sd", b)
                dve.scalar_tensor_tensor(sact[0:w, n, :], sgs[0:w, :], 0.5, bank[0:w, bk, L:2 * L], ALU.mult, ALU.mult
                                         ).then_inc(S["d_sact"], 1)

            def D5(b):
                shared(b, 0, 7)
                need(dve, "d_rank", b + 1)
                for tt in range(TT):
                    i = dve.tensor_tensor(pos[:, tt, :], psum(6, 128 + tt * E_N, 192 + tt * E_N), region, ALU.add)
                i.then_inc(S["d_pos"], 1)
                for tt in range(TT):
                    cd.link(dve.tensor_tensor(seen[:], seen[:], mkb[:, tt, :], ALU.add))
                need(dve, "d_pos", b + 1)
                for tt in range(TT):
                    for k in range(TOPK):
                        i = dve.scalar_tensor_tensor(hit[:, tt, k, :], iota, idxf[:, tt, k:k + 1], pos[:, tt, :], ALU.is_equal, ALU.mult)
                cd.link(i)
                cd.link(dve.tensor_reduce(destf[:], hit[:], AX, ALU.add))
                need(dve, "d_scat", b * 16 * TT * TOPK)
                cd.step(dve.tensor_copy(slots(DEST, b), destf[:]))
                dve.tensor_copy(desti[:].rearrange("p (t k) -> p t k", t=TT), destf[:]).then_inc(S["d_dest"], 1)
                shared(b, 1, 7)

            def D6(b):
                shared(b, 2, 6)
                need(dve, "d_sd", b + 1)
                for tt in range(TT):
                    i = dve.tensor_tensor(slot(b, tt), psum(6, tt * D, (tt + 1) * D), x3[:, tt, :], ALU.add)
                i.then_inc(S["d_base"], 1)

            turns(dve, {"A1": A1, "A3": A3, "A4": A4, "A5": A5, "B1": B1, "B2": B2, "B3": lambda b: attention(b, 0, 5),
                        "B4": lambda b: attention(b, 5, 10), "B5": lambda b: attention(b, 10, UNITS + 2), "B6": B6, "B7": B7,
                        "B8": B8, "D2": D2, "D3": D3, "D4": D4, "D5": D5, "D6": D6})
            for ch in (ca, cbn, cd):
                assert ch.k == ch.per, (ch.name, ch.k, ch.per)

            cr = Chain(dve, "ch_r", 0)
            dve.wait_ge(S["r_tot"], 1)
            tot = psum(6, 0, E_N)
            cr.link(dve.tensor_scalar(cn[:], tot, 1.0 / P, (P - 1.0) / P - 0.5 + 0.5 / P / 2, ALU.mult, ALU.add))
            cr.link(dve.tensor_scalar(cn[:], cn[:], ROUND, None, ALU.add))
            cr.link(dve.tensor_scalar(cn[:], cn[:], -ROUND, None, ALU.add))
            cr.step(dve.scalar_tensor_tensor(pad_e[:], cn[:], -float(P), tot, ALU.mult, ALU.add))
            cr.link(dve.tensor_tensor_scan(cum[:], ones_row[:, 0:E_N], cn[:], 0.0, ALU.mult, ALU.add))
            for k in range(2):
                cr.step(dve.scalar_tensor_tensor(scr[:, 0, :], cum[:], chunk_no[:, k:k + 1], ones_row[:, 0:E_N], ALU.is_le, ALU.mult,
                                                 accum_out=ce[:, k:k + 1]))
                cr.link(dve.scalar_tensor_tensor(scr[:, 1, :], cum[:], chunk_no[:, k:k + 1], cn[:], ALU.is_le, ALU.mult,
                                                 accum_out=cb[:, k:k + 1]))
                cr.link(dve.scalar_tensor_tensor(scr[:, 2, :], iota, ce[:, k:k + 1], pad_e[:], ALU.is_equal, ALU.mult,
                                                 accum_out=co[:, k:k + 1]))
            cr.link(dve.tensor_tensor(cb[:], chunk_no, cb[:], ALU.subtract))
            cr.link(dve.scalar_tensor_tensor(co[:], cb[:], float(P), co[:], ALU.mult, ALU.add))
            cr.link(dve.scalar_tensor_tensor(crow[:], ce[:], float(CAP), co[:], ALU.mult, ALU.add))
            dve.tensor_scalar(ctab[:, 1::2], crow[:], float(P), float(E_N * CAP), ALU.add, ALU.min)
            dve.tensor_scalar(ctab[:, 0::2], ce[:], float(E_N - 1), None, ALU.min).then_inc(S["r_tab"], 1)
            cr.link(dve.tensor_tensor(before_e[:], cum[:], cn[:], ALU.subtract))
            cr.link(dve.scalar_tensor_tensor(shift_e[:], before_e[:], float(P), region, ALU.mult, ALU.subtract))
            cr.link(dve.tensor_tensor(shift_e[:], shift_e[:], pad_e[:], ALU.subtract))
            dve.wait_ge(S["r_row"], 1)
            dve.tensor_copy(table[:], bank[0:1, 7, :]).then_inc(S["r_table"], 1)

            def turned(c):
                n = c.slot(3)
                need(dve, "m_xT", c.no + 1)
                need(dve, "m_h", c.no - 2)
                dve.tensor_copy(xcT[n], bank[:, n, 0:2 * P].rearrange("p (a b) -> p a b", a=2)).then_inc(S["m_xT_out"], 1)

            def result(c):
                n = c.slot(3)
                need(dve, "m_y", c.no + 1)
                need(dve, f"m_st{n}", c.before(3) * 16)
                dve.tensor_copy(yc[n], psum(6 + c.slot(2), 0, D)).then_inc(S["m_y_out"], 1)

            def tile_of(t, i):
                n = slice(i, i + 1) if isinstance(i, int) else bass.ds(i, 1)
                return t[:, n, :].rearrange("p o k -> p (o k)")

            cw, cf = Chain(dve, "ch_w", 2), Chain(dve, "ch_f", TOPK - 1 + 17)
            m = nrm["A"]

            def row_numbers(i):
                cw.start(i)
                for k in range(TOPK):
                    j = dve.scalar_tensor_tensor(look[:, k, :], iota, tile_of(TOPI, i)[:, k:k + 1], shift_e[:],
                                                 ALU.is_equal, ALU.mult)
                cw.link(j)
                cw.link(dve.tensor_reduce(tile_of(ROWF, i), look, AX, ALU.add))
                dve.tensor_tensor(tile_of(ROWF, i), tile_of(ROWF, i), tile_of(DEST, i), ALU.add).then_inc(S["f_rows"], 1)

            chunk_loop(dve, [turned, lambda c: None, result], row_numbers)

            dve.wait_ge(S["f_rows"], NT)

            def rows(i, s, nth):
                need(dve, f"f_g{s}", nth * 16 * TOPK)
                dve.tensor_copy(rowi[s][:], tile_of(ROWF, i)).then_inc(S["f_row"], 1)

            def combine(i, s, nth):
                cf.start(i)
                need(dve, f"f_g{s}", (nth + 1) * 16 * TOPK)
                need(dve, "f_out", i)
                r = m["r"][:, 0, :]
                for k in range(TOPK):
                    j = dve.scalar_tensor_tensor(r, yg[s][:, k, :], tile_of(TOPW, i)[:, k:k + 1], tile_of(X, i) if k == 0 else r,
                                                 ALU.mult, ALU.add)
                    if k < TOPK - 1:
                        cf.link(j)
                j.then_inc(S["f_used"], 1)
                need(dve, "f_used", i + 1)
                need(dve, f"f_st{s}", nth * 16)
                norm(cf, m, [outb[s]], 1).then_inc(S["f_out"], 1)

            rows(0, 0, 0)
            rows(1, 1, 0)
            for s in range(2):
                combine(s, s, 0)
                rows(2 + s, s, 1)
            with dve.Fori(1, NT // 2 - 1) as i:
                for s in range(2):
                    combine(i * 2 + s, s, i)
                    rows(i * 2 + (2 + s), s, i + 1)
            for s in range(2):
                combine(NT - 2 + s, s, NT // 2 - 1)


def layouts(x):
    def tiles(a, p=P):
        return np.ascontiguousarray(a.reshape(-1, p, a.shape[-1]).swapaxes(0, 1))

    def transposed(name):
        return tiles(x[name].T)

    def channel(name):
        return x[name].reshape(KT, P, -1).swapaxes(0, 1).reshape(P, -1)

    u = x["L0_attn_u"]
    a = {"u": u, "uT": np.ascontiguousarray(u.swapaxes(1, 2).reshape(NB, KT, P, L).swapaxes(1, 2))}
    a["vec"] = np.concatenate([channel(n) for n in (
        "L0_attn_bq", "L0_attn_bk", "L0_attn_bv", "L0_attn_convq_b", "L0_attn_convk_b", "L0_attn_D_skip", "L0_ffn_ln1_w",
        "L0_ffn_ln2_w", "L0_attn_convq_w", "L0_attn_convk_w")], 1)
    a["bo"] = np.ascontiguousarray(np.broadcast_to(x["L0_attn_bo"], (P, D)))
    a["ssm"] = transposed("L0_attn_ssm_kernel")
    for n in "qkvo":
        a[f"a_w{n}"] = transposed(f"L0_attn_W{n}")
        a[f"d_w{n}"] = transposed(f"L1_attn_W{n}")
    for n in "qkv":
        a[f"b_w{n}"] = transposed(f"L0_ffn_W{n}")
    a["b_wo"], a["b_a"], a["b_b"] = tiles(x["L0_ffn_Wo"]), tiles(x["L0_ffn_A"]), x["L0_ffn_B"]
    a["w_in"], a["w_up"], a["w_down"] = (transposed(f"L0_ffn_W_{n}") for n in ("in_base", "up_base", "down"))
    a["gate_w"] = transposed("L1_ffn_gate_w")
    a["sh_gu"] = transposed("L1_ffn_shared_gate_up")
    a["sh_dn"] = np.ascontiguousarray(x["L1_ffn_shared_down"].T)
    a["e_w1"] = np.ascontiguousarray(x["L1_ffn_experts_w1"].swapaxes(1, 2).reshape(E_N, KT, P, I_N).swapaxes(1, 2))
    a["e_w2"] = np.ascontiguousarray(x["L1_ffn_experts_w2"].swapaxes(1, 2).reshape(E_N, 2, IH, D).swapaxes(1, 2))
    return a


def kernel(**inputs):
    import concourse.bacc as bacc
    from concourse.bass_utils import run_bass_kernel_spmd

    arrays = {n: np.ascontiguousarray(a) for n, a in layouts({n: np.asarray(v) for n, v in inputs.items()}).items()}
    arrays.update(constants())
    nc = bacc.Bacc("TRN2", target_bir_lowering=False, num_devices=1)
    d = {n: nc.dram_tensor(f"in_{n}", a.shape, mybir.dt.from_np(a.dtype), kind="ExternalInput").ap() for n, a in arrays.items()}
    d["out"] = nc.dram_tensor("out", (NB, L, D), F32, kind="ExternalOutput").ap()
    build(nc, d)
    r = run_bass_kernel_spmd(nc, [{f"in_{n}": a for n, a in arrays.items()}], core_ids=[0])
    return r.results[0]["out"]
```

```python
from contextlib import ExitStack

import numpy as np

import concourse.bass as bass
from concourse import mybir

P = 128
NB, L, D = 8, 256, 256
KT = D // P
TT = L // P
NT = NB * TT
HEADS, HD = 16, 16
PAIR = 2 * HD
GROUPS = P // PAIR
F_MLP = 1024
FT = F_MLP // P
R_MOD = 16
MOD_SCALE = 0.1
E_N, I_N, TOPK = 64, 176, 6
IH = I_N // 2
SH_I = 2 * I_N
SH_TILES = [(0, 128), (128, 128), (256, SH_I - 256)]
PAIRS = NB * L * TOPK
CHUNKS = E_N + (PAIRS - E_N) // P
CAP = P + NB * L
SPARE = CHUNKS - PAIRS // P
X_ROWS = E_N * CAP + (SPARE + 1) * P
XW = D + 8
Y_ROWS = PAIRS + (E_N + SPARE + 1) * P
NFFT = 2 * L
FREQ_TILES = L // P
RING = 6
YG = 4
HEAD = 9
LN_EPS, RMS_EPS = 1e-5, 1e-6
NEG = -1e38
RSQRT_MAGIC = 0x5F3759DF
ROUND = 8388608.0

F32, BF16 = mybir.dt.float32, mybir.dt.bfloat16
I32, U32 = mybir.dt.int32, mybir.dt.uint32
ALU = mybir.AluOpType
ACT = mybir.ActivationFunctionType
AX = mybir.AxisListType.X

VEC = {"bq": 0, "bk": 2, "bv": 4, "cqb": 6, "ckb": 8, "skip": 10, "ln1": 12, "ln2": 14, "cqw": 16, "ckw": 22}
VEC_N = 28
CST = {"ident": 0, "iota": 128, "region": 192, "even": 256, "odd": 257, "chunk": 258, "token": 260}
CST_N = 260 + TT
CSB = {"ident": 0, "ones": 128, "before": 256, "open": 384, "causal": 512}
CSB_N = 640


def constants():
    p = np.arange(P)
    c = np.zeros((P, CST_N), np.float32)
    c[:, 0:128] = np.eye(P)
    c[:, 128:192] = np.arange(E_N)
    c[:, 192:256] = np.arange(E_N) * CAP + P
    c[:, 256] = np.where(p % PAIR < HD, HD ** -0.5, 0)
    c[:, 257] = np.where(p % PAIR < HD, 0, HD ** -0.5)
    c[:, 258] = 2 * p
    c[:, 259] = 2 * p + 1
    c[:, 260:] = (np.arange(TT) * P + p[:, None]) * TOPK
    blank = np.full((E_N + SPARE + 1, P, XW - D), -1, np.float32)
    blank[:, :, 0] = PAIRS + np.arange((E_N + SPARE + 1) * P).reshape(-1, P)
    b = np.zeros((P, CSB_N), np.float32)
    b[:, 0:128] = np.eye(P)
    b[:, 128:256] = 1
    b[:, 256:384] = p[:, None] < p[None, :]
    tri = np.where(p[None, :] <= p[:, None], 0, NEG)
    b[:, 512:640] = tri
    t = np.arange(L)[:, None]
    f = np.arange(L)[None, :]
    w = 2 * np.pi * ((t * f) % NFFT) / NFFT
    re, im = np.cos(w), -np.sin(w)
    sign = 1.0 - 2.0 * (np.arange(L) % 2)
    im_packed = im.copy()
    im_packed[:, 0] = sign
    re_nyq = re[:, :P].copy()
    re_nyq[:, 0] = sign
    fwd = np.concatenate([re, im_packed, im[:, :P], re_nyq], 1)
    fwd = fwd.reshape(KT, P, 6 * P).transpose(1, 0, 2)
    weight = np.where(np.arange(L) == 0, 1.0, 2.0)[:, None] / NFFT
    ire = weight * re.T
    iim = weight * im.T
    iim[0] = sign / NFFT
    inv = np.concatenate([ire, iim], 0).reshape(2 * FREQ_TILES, P, L).transpose(1, 0, 2)
    return {
        "blank": blank, "cst": c, "csb": b.astype(mybir.dt.np(BF16)),
        "fwd": np.ascontiguousarray(fwd, np.float32), "inv": np.ascontiguousarray(inv, np.float32),
    }


def build(nc, d):
    x_rows = nc.dram_tensor("x_rows", (X_ROWS, XW), F32, kind="Internal").ap()
    q_parts = nc.dram_tensor("q_parts", (3, P, KT * L), BF16, kind="Internal").ap()
    k_parts = nc.dram_tensor("k_parts", (5, P, KT * L), BF16, kind="Internal").ap()
    y_rows = nc.dram_tensor("y_rows", (Y_ROWS, D), F32, kind="Internal").ap()

    with ExitStack() as ctx:
        def sb(name, shape, dt=F32):
            return ctx.enter_context(nc.sbuf_tensor(name, shape, dt))

        def sem(name):
            return ctx.enter_context(nc.semaphore(name))

        bank = ctx.enter_context(nc.psum_tensor("bank", [P, 8, 512], F32))

        cst, csb = sb("cst", [P, CST_N]), sb("csb", [P, CSB_N], BF16)
        ident, iota, region = cst[:, 0:128], cst[:, 128:192], cst[:, 192:256]
        even, odd, chunk_no, token_row = cst[:, 256:257], cst[:, 257:258], cst[:, 258:260], cst[:, 260:]
        identb, onesb, beforeb = csb[:, 0:128], csb[:, 128:256], csb[:, 256:384]
        masks = [csb[:, 640 - w:640].rearrange("p (o k) -> p o k", o=1).broadcast_to([P, 4 * P // w, w]) for w in (P, L)]
        vec = sb("vec", [P, VEC_N])
        fwd, inv = sb("fwd", [P, KT, 6 * P]), sb("inv", [P, 2 * FREQ_TILES, L])
        ssm = sb("ssm", [P, KT, D])
        a_w = {n: sb(f"a_w{n}", [P, KT, D]) for n in "qkvo"}
        bo = sb("bo", [P, D])
        b_w = {n: sb(f"b_w{n}", [P, KT, D]) for n in "qkv"}
        b_wo = sb("b_wo", [P, KT, D])
        b_a, b_b = sb("b_a", [P, KT, R_MOD]), sb("b_b", [R_MOD, F_MLP])
        w_in, w_up = sb("w_in", [P, KT, F_MLP]), sb("w_up", [P, KT, F_MLP])
        w_down = sb("w_down", [P, FT, D])
        d_w = {n: sb(f"d_w{n}", [P, KT, D]) for n in "qkvo"}
        gate_w = sb("gate_w", [P, KT, E_N])
        sh_gu = sb("sh_gu", [P, KT, 2 * SH_I])
        sh_dn = sb("sh_dn", [P, len(SH_TILES), D])

        X = sb("X", [P, NT, D])
        TOPW = sb("TOPW", [P, NT, TOPK])

        uT = sb("uT", [P, KT, L])
        q_sb, k_sb = sb("q_sb", [P, KT, L + 2]), sb("k_sb", [P, KT, L + 2])
        v_sb, qc, kc = sb("v_sb", [P, KT, L]), sb("qc", [P, KT, L]), sb("kc", [P, KT, L])
        kv, kvT = sb("kv", [P, KT, L]), sb("kvT", [P, TT, D])
        tabA, tabB, tabD = (sb(n, [P, FREQ_TILES, D]) for n in ("tabA", "tabB", "tabD"))
        products = sb("products", [P, 4, FREQ_TILES, D])
        pr = [products[:, n] for n in range(4)]
        Yre, Yim = pr[0], pr[2]
        z = sb("z", [P, KT, L])
        xn = sb("xn", [P, TT, D])
        d_kv = sb("d_kv", [P, KT, L])
        nrm = {}
        att = sb("att", [P, TT, D])
        for s, r in (("A", qc), ("B", att), ("D", d_kv), ("R", None), ("F", qc)):
            nrm[s] = dict(r=r, st=sb(f"st{s}", [P, TT, 6]), mv=sb(f"mv{s}", [P, TT, 2]), v=sb(f"v{s}", [P, TT]),
                          y=sb(f"y{s}", [P, TT]), var=f"n_var{s}", inv=f"n_inv{s}")
        minus_half = sb("minus_half", [P, TT])
        ms = sb("ms", [P, TT])
        h1T, h2T = sb("h1T", [P, KT, L]), sb("h2T", [P, KT, L])
        xnT = kc
        part = {n: products[:, 2 * i:2 * i + 2].rearrange("p n f d -> p (n f d)").bitcast(BF16)[:, 0:3 * KT * L]
                .rearrange("p (n k l) -> p n k l", n=3, k=KT) for i, n in enumerate("qk")}
        rest = {"q": z, "k": kvT}
        stack = {n: sb(f"stack_{n}", [P, HEADS // KT, KT, L], BF16) for n in "qk"}
        v1 = sb("v1", [P, TT, HEADS, HD + 1])
        UNITS = GROUPS + 2 * GROUPS
        nmx = sb("nmx", [P, UNITS, 4])
        prob, probT = sb("prob", [P, 2, 512]), sb("probT", [P, 2, 4, P])
        rec = sb("rec", [P, TT, HEADS])
        attT = sb("attT", [P, KT, L])
        woa = sb("woa", [P, KT, R_MOD])
        th, mh = sb("th", [R_MOD, L]), sb("mh", [R_MOD, L])
        gt, gs = sb("gt", [P, 2, L]), sb("gs", [P, 2, L])
        actT = sb("actT", [P, FT, L])
        x2, x2T = sb("x2", [P, TT, D]), sb("x2T", [P, KT, L])
        d_k, d_cs, vh = (sb(n, [P, KT, L]) for n in ("d_k", "d_cs", "vh"))
        ones_row = sb("ones_row", [P, L])
        x3_row, x3T = sb("x3_row", [P, TT, XW]), sb("x3T", [P, KT, L])
        x3, x3_meta = x3_row[:, :, 0:D], x3_row[:, :, D:XW]
        lg8, nlg = sb("lg8", [P, TT, 8]), sb("nlg", [P, TT])
        ex, top8, top8i = sb("ex", [P, TT, E_N]), sb("top8", [P, TT, 8]), sb("top8i", [P, TT, 8], U32)
        idxf, wsum, wrec = sb("idxf", [P, TT, 8]), sb("wsum", [P, TT]), sb("wrec", [P, TT])
        mk, mkb = sb("mk", [P, TT, E_N]), sb("mkb", [P, TT, E_N], BF16)
        seen = sb("seen", [P, E_N], BF16)
        pos, hit = sb("pos", [P, TT, E_N]), sb("hit", [P, TT, TOPK, E_N])
        destf, desti = sb("destf", [P, TT, TOPK]), sb("desti", [P, TT * TOPK], I32)
        sgt, sgs, sact = sb("sgt", [P, L]), sb("sgs", [P, L]), sb("sact", [P, len(SH_TILES), L])
        zeros = sb("zeros", [P, D])
        spare = sb("spare", [P, 2])
        cn, cum, pad_e = sb("cn", [P, E_N]), sb("cum", [P, E_N]), sb("pad_e", [P, E_N])
        ce, cb, co, crow = (sb(n, [P, 2]) for n in ("ce", "cb", "co", "crow"))
        ctab, table = sb("ctab", [P, 4]), gs[0:1].rearrange("p a b -> p (a b)").bitcast(I32)
        scr = h1T[:].rearrange("p a b -> p (a b)")[:, 0:3 * E_N].rearrange("p (n e) -> p n e", n=3)
        dead = [[t[:].rearrange("p a b -> p (a b)"), 0] for t in (w_in, w_up, w_down, fwd, inv, sh_gu, ssm, a_w["q"], a_w["k"], a_w["v"])]

        def again(rows, a, b):
            for t in dead:
                if t[1] + a * b <= t[0].shape[1]:
                    at, t[1] = t[1], t[1] + a * b
                    return t[0][0:rows, at:at + a * b].rearrange("p (a b) -> p a b", a=a)

        def ring(n, *shape):
            return [again(*shape) for _ in range(n)]

        w2, w1 = ring(RING, IH, 2, D), ring(RING, P, KT, I_N)
        xc_row = ring(RING, P, 1, XW)
        xc_row = [t[:, 0, :] for t in xc_row]
        xcT, hs = ring(3, P, KT, P), ring(3, IH, 2, P)
        yc, outb = ring(RING, P, 1, D), ring(YG, P, 1, D)
        yc, outb = [t[:, 0, :] for t in yc], [t[:, 0, :] for t in outb]

        yg = [t[:].rearrange("p a b -> p (a b)")[:, 0:TOPK * D].rearrange("p (k d) -> p k d", k=TOPK) for t in (w_in, w_up, actT)]
        yg.append(products[:].rearrange("p n f d -> p (n f) d")[:, 0:TOPK, :])
        diag = [t[:].rearrange("p a b -> p (a b)")[:, n * TOPK * P:(n + 1) * TOPK * P].rearrange("p (k c) -> p k c", k=TOPK)
                for t in (w_down, fwd) for n in range(2)]
        ids = [sb(f"ids{n}", [P, 1], I32) for n in range(RING)]
        choice = [sb(f"choice{n}", [P, 1]) for n in range(RING)]
        found = [sb(f"found{n}", [P, TOPK]) for n in range(RING)]
        spot = sb("spot", [P, TT, P], BF16)
        expert_of = gt[:, 0, :]

        S = {n: sem(n) for n in (
            "ld_vec ld_mlp p_spare n_varA n_varB n_varD n_varR n_invA n_invB n_invD n_invR ld_u ld_uT ld_cst ld_a ld_ssm ld_b ld_d set_pool set_dve set_pe set_woa ub "
            "a_q a_k a_v a_q_out a_k_out a_v_out a_qc a_kc a_kv a_kvT a_kvT_out a_X a_pr a_Y a_y a_z a_zq a_o a_r a_x1 "
            "b_xn b_hT b_h1 b_h2 b_xT b_q b_k b_v b_first b_rest b_second b_third st_qw st_kw st_q st_k b_v_out b_s b_max b_exp b_pT b_pT_out b_pv b_att "
            "b_attT b_attT_out b_mod b_tanh b_mh b_gu b_gt b_act b_dn b_r b_x2 "
            "d_xT d_xT_out d_q d_k_ps d_v d_k_out d_kv d_vh d_o d_r d_x3 d_x3T d_x3T_out d_lg d_max d_ex d_mask "
            "d_rank d_pos d_dest d_scat d_sg d_sgt d_sact d_sd d_base "
            "ch_a ch_b ch_d ch_r ch_f r_tot r_tab r_row r_table r_fill "
            "m_w0 m_x0 m_w1 m_x1 m_w2 m_x2 m_w3 m_x3 m_w4 m_x4 m_w5 m_x5 m_ids ch_m r_spot r_all m_xT m_xT_out m_h m_hs m_y m_y_out m_st0 m_st1 m_st2 m_st3 m_st4 m_st5 "
            "f_ld0 f_ld1 f_ld2 f_ld3 f_st0 f_st1   f_diag f_sum f_r f_out n_varF n_invF").split()}

        def need(eng, name, value):
            if isinstance(value, int) and value <= 0:
                return
            eng.wait_ge(S[name], value)

        def first(b):
            return isinstance(b, int) and b == 0

        def alone(eng):
            if eng.engine == nc.vector.engine:
                eng.memset(spare[:, 0:1], 0.0)
            else:
                eng.tensor_tensor(spare[:, 1:2], ones_row[:, 0:1], ones_row[:, 1:2], ALU.mult).then_inc(S["p_spare"], 1)

        class Chain:

            def __init__(self, eng, name, per):
                self.eng, self.name, self.per, self.k, self.b = eng, name, per, 0, 0

            def start(self, b):
                self.b, self.k = b, 0

            def step(self, ins):
                self.k += 1
                ins.then_inc(S[self.name], 1)

            def wait(self):
                self.eng.wait_ge(S[self.name], self.b * self.per + self.k)

            def link(self, ins):
                self.step(ins)
                self.wait()

        TURN = """A1 A1b D1 A1q u0 D2k A1k u1 D2x A2 u2 D2v A3a u3 A3b u4 A3p D2q D2w u5 t0 D3 u6 D3n A4a u7 D3o D4 A4b A4z
            u8 S0 u9 A5 u10 A5n D4l S1 u11 A5o D4m S2 A6n u12 SDa u13 t1 A6o D4t SDb SD B6a C1 B6c B6b f0 D4k f1 C2 f2 D5 f3 D5p C2v
            f4 D4w D5h f5 f6 f7 C2h B8 D6""".split()
        LAST = "D1 D2k D2x D2v D2q D2w D3 D3n D3o D4 D4l D4m D4t D4k D5 D5p D5h D6 S0 S1 S2 D4w SDa SDb SD".split()
        LAG = {"A": 0, "C": 0, "B": 1, "D": 2}
        STAGE = {"u": "B", "t": "B", "f": "B", "S": "D"}

        def turns(eng, parts):
            def turn(it, order=TURN):
                for name in order:
                    b = it - LAG[STAGE.get(name[0], name[0])]
                    if isinstance(b, int) and not 0 <= b < NB:
                        continue
                    if name in parts:
                        parts[name](b)
            for it in range(3):
                turn(it)
            with eng.Fori(3, NB) as it:
                turn(it)
            turn(NB)
            turn(NB + 1, LAST)

        class Chunk:

            def __init__(self, i, off):
                self.i, self.off, self.no = i, off, i * RING + off

            def slot(self, n):
                return self.off % n

            def before(self, n):
                return self.i * (RING // n) + self.off // n

        def chunk_values(eng, c):
            at = slice(2 * c.no, 2 * c.no + 2) if isinstance(c.no, int) else bass.ds(c.no * 2, 2)
            why = "the table was clamped where it was worked out"
            e, row = nc.values_load_multi_w_load_instructions(table[0:1, at], engines=(eng.engine,), min_val=0,
                                                              max_val=X_ROWS - P, skip_runtime_bounds_check_because=why)[1]
            return nc.s_assert_within(e, 0, E_N - 1, skip_runtime_bounds_check_because=why), row

        def chunk_loop(eng, skewed):
            def step(i, off):
                for lag, work in enumerate(skewed):
                    c = Chunk(i, off - lag)
                    if work and (not isinstance(c.no, int) or 0 <= c.no < CHUNKS):
                        work(c)

            def body(i):
                for off in range(HEAD, HEAD + RING):
                    step(i, off)

            turns_in_all = (CHUNKS - HEAD) // RING
            assert HEAD + turns_in_all * RING == CHUNKS
            for off in range(HEAD):
                step(0, off)
            with eng.Fori(0, turns_in_all) as i:
                body(i)
            for off in range(CHUNKS, CHUNKS + len(skewed) - 1):
                step(0, off)

        def pair_loop(eng, skewed):
            def step(i, off):
                for lag, work in enumerate(skewed):
                    pair = i * 2 + (off - lag)
                    if work and (not isinstance(pair, int) or 0 <= pair < NT // 2):
                        work(pair, (off - lag) % 2, i + (off - lag) // 2 + 1)
            for i in range(2):
                step(i, 0)
                step(i, 1)
            with eng.Fori(2, NT // 4) as i:
                step(i, 0)
                step(i, 1)
            for off in range(len(skewed) - 1):
                step(NT // 4, off)

        def unit_heads(u):
            if u < GROUPS:
                return [(u, eh, par) for eh in range(KT) for par in range(2)]
            return [((u - GROUPS) // KT, (u - GROUPS) % KT, par) for par in range(2)]

        block = ctx.enter_context(nc.Block())

        def psum(n, a=0, b=512):
            return bank[:, n, a:b]

        def psum3(n):
            return bank[:, n, :].rearrange("p (a b) -> p a b", a=2)

        @block.sync
        def _(sp):
            sp.dma_start(uT[:], d["uT"][0]).then_inc(S["ld_uT"], 16)
            for n in "qkv":
                sp.dma_start(a_w[n][:], d[f"a_w{n}"]).then_inc(S["ld_a"], 16)
            sp.dma_start(fwd[:], d["fwd"]).then_inc(S["ld_ssm"], 16)
            sp.dma_start(ssm[:], d["ssm"]).then_inc(S["ld_ssm"], 16)
            sp.dma_start(inv[:], d["inv"]).then_inc(S["ld_ssm"], 16)
            sp.dma_start(a_w["o"][:], d["a_wo"]).then_inc(S["ld_ssm"], 16)
            for t, n in ((b_wo, "b_wo"), (b_a, "b_a"), *((b_w[n], f"b_w{n}") for n in "qkv")):
                sp.dma_start(t[:], d[n]).then_inc(S["ld_b"], 16)
            for t, n in ((b_b, "b_b"), (w_in, "w_in"), (w_up, "w_up"), (w_down, "w_down")):
                sp.dma_start(t[:], d[n]).then_inc(S["ld_mlp"], 16)
            for n in "qkvo":
                sp.dma_start(d_w[n][:], d[f"d_w{n}"]).then_inc(S["ld_d"], 16)
            sp.dma_start(gate_w[:], d["gate_w"]).then_inc(S["ld_d"], 16)
            sp.dma_start(sh_gu[:], d["sh_gu"]).then_inc(S["ld_d"], 16)
            sp.dma_start(sh_dn[:, 0:2, :], d["sh_dn"][0:256].rearrange("(k p) n -> p k n", p=P)).then_inc(S["ld_d"], 16)
            sp.dma_start(sh_dn[0:SH_I - 256, 2, :], d["sh_dn"][256:SH_I]).then_inc(S["ld_d"], 16)

            def next_uT(b):
                sp.wait_ge(S["a_v"], b)
                n = slice(b, b + 1) if isinstance(b, int) else bass.ds(b, 1)
                sp.dma_start(uT[:], d["uT"][n].rearrange("o p k l -> p (o k) l")).then_inc(S["ld_uT"], 16)

            def stack_up(b):
                def rows(t, a, z):
                    return t[a:z].rearrange("n (e h) c -> (n e) (h c)", e=HD)

                def value(v):
                    return v if isinstance(v, int) else sp.snap(v)

                last = isinstance(b, int) and b == NB - 1
                following = None if last else value(b + 1)
                queries, keys = value(b * 2 + 1), value(b * 2 + 2)
                left = {"q": value(b * 16 + 16), "k": value(b * 32 + 32)}
                if not last:
                    next_uT(following)
                need(sp, "b_third", queries)
                sp.dma_start(q_parts.rearrange("n p c -> p n c"), part["q"].rearrange("p n k l -> p n (k l)")).then_inc(S["st_qw"], 16)
                need(sp, "b_third", keys)
                for a, n in ((0, 3), (3, 2)):
                    sp.dma_start(k_parts[a:a + n].rearrange("n p c -> p n c"), part["k"][:, 0:n].rearrange("p n k l -> p n (k l)")
                                 ).then_inc(S["st_kw"], 16)
                for n, t, first_parts in (("q", q_parts, (0, 0, 0)), ("k", k_parts, (1, 2, 0))):
                    need(sp, f"st_{n}w", left[n])
                    for j, a in enumerate(first_parts):
                        parts = 3 if j < 2 else 2
                        sp.dma_start(stack[n][j * 3 * HD:(j * 3 + parts) * HD].rearrange("p h k l -> p (h k l)"),
                                     rows(t, a, a + parts)).then_inc(S[f"st_{n}"], 16)

            stack_up(0)
            sp.wait_ge(S["set_pool"], 1)
            def blank(rows, at, n):
                sp.dma_start(rows[:, :, 0:D], zeros[:].rearrange("p (o d) -> p o d", o=1).broadcast_to([P, n, D])
                             ).then_inc(S["r_fill"], 16)
                sp.dma_start(rows[:, :, D:XW], d["blank"][at:at + n].rearrange("n p w -> p n w")).then_inc(S["r_fill"], 16)

            blank(x_rows[0:E_N * CAP].rearrange("(e c) d -> c e d", c=CAP)[0:P], 0, E_N)
            blank(x_rows[E_N * CAP:].rearrange("(n p) d -> p n d", p=P), E_N, SPARE + 1)
            with sp.Fori(1, NB - 1) as b:
                stack_up(b)
            stack_up(NB - 1)
            sp.wait_ge(S["r_table"], 1)

            def load(c):
                s = c.slot(RING)
                e, row = chunk_values(sp, c)
                if first(c.no):
                    sp.wait_ge(S["d_scat"], 16 * TT * TOPK * NB)
                need(sp, "m_xT", c.no - (RING - 1))
                need(sp, "m_ids", c.no - (RING - 1))
                sp.dma_start(xc_row[s], x_rows[bass.ds(row, P), :]).then_inc(S[f"m_x{s}"], 16)
                need(sp, "m_h", c.no - (RING - 1))
                sp.dma_start(w1[s], d["e_w1"][bass.ds(e, 1)].rearrange("o p k i -> p (o k) i")).then_inc(S[f"m_w{s}"], 16)

            chunk_loop(sp, [load])

        @block.gpsimd
        def _(pool):
            for t in (q_sb, k_sb):
                pool.memset(t[:, :, 0:2], 0.0)
            pool.memset(v1[:, :, :, HD:HD + 1], 1.0)
            pool.memset(ones_row[:], 1.0)
            pool.memset(minus_half[:], -0.5)
            pool.memset(seen[:], 0.0)
            pool.memset(zeros[:], 0.0).then_inc(S["set_pool"], 1)
            pool.wait_ge(S["ld_vec"], 16)
            pool.wait_ge(S["ld_u"], 32)
            pool.tensor_tensor(X[:], X[:], bo[:].rearrange("p (o n) -> p o n", o=1).broadcast_to([P, NT, D]),
                               ALU.add).then_inc(S["ub"], 1)

            def A3(b):
                need(pool, "a_pr", b + 1)
                pool.tensor_tensor(Yre, pr[0], pr[1], ALU.subtract)
                pool.tensor_tensor(Yim, pr[2], pr[3], ALU.add).then_inc(S["a_Y"], 1)

            def inverse_root(which):
                m = nrm[which]
                def part(b):
                    need(pool, m["var"], b + 1)
                    pool.tensor_tensor(m["y"][:], m["v"][:], minus_half[:], ALU.pow).then_inc(S[m["inv"]], 1)
                return part

            def C2v(b):
                for i, n in enumerate("qk"):
                    need(pool, "b_second", b * 2 + i + 1)
                    pool.tensor_tensor(part[n][:, 2], rest[n][:], part[n][:, 1], ALU.subtract).then_inc(S["b_third"], 1)

            def C2h(b):
                need(pool, "b_xT", b + 1)
                need(pool, "b_gu", b * FT)
                at = VEC["ln2"]
                pool.tensor_tensor(h2T[:], xnT[:], vec[:, at:at + KT].rearrange("p (k o) -> p k o", o=1).broadcast_to([P, KT, L]),
                                   ALU.mult).then_inc(S["b_h2"], 1)

            def D6(b):
                need(pool, "p_spare", b)
                if first(b):
                    pool.wait_ge(S["r_fill"], 64)
                need(pool, "d_dest", b + 1)
                alone(pool)
                for tt in range(TT):
                    for k in range(TOPK):
                        n = tt * TOPK + k
                        pool.indirect_dma_start(x_rows, bass.IndirectOffsetOnAxis(ap=desti[:, n:n + 1].bitcast(U32), axis=0),
                                                x3_row[:, tt, :], None).then_inc(S["d_scat"], 16)

            turns(pool, {"A3p": A3, "C2v": C2v, "C2h": C2h, "D6": D6, "D3n": inverse_root("D"), "A5n": inverse_root("A"), "A6n": inverse_root("R"),
                         "B8": inverse_root("B")})

            def spread(c):
                s = c.slot(RING)
                need(pool, "p_spare", c.no + NB)
                need(pool, "m_ids", c.no + 1)
                need(pool, "m_y_out", c.no + 1)
                alone(pool)
                pool.indirect_dma_start(y_rows, bass.IndirectOffsetOnAxis(ap=ids[s][:].bitcast(U32), axis=0), yc[s], None
                                        ).then_inc(S[f"m_st{s}"], 16)

            chunk_loop(pool, [None, None, None, spread])

            def root(pair, h, nth):
                need(pool, "n_varF", pair + 1)
                pool.tensor_tensor(nrm["F"]["y"][:], nrm["F"]["v"][:], minus_half[:], ALU.pow).then_inc(S["n_invF"], 1)

            pair_loop(pool, [root])

        @block.tensor
        def _(pe):
            def project(out, w, x):
                for eh in range(KT):
                    for kt in range(KT):
                        mm = pe.matmul(out[:, eh * L:(eh + 1) * L], w[:, kt, eh * P:(eh + 1) * P], x[:, kt, :],
                                       start=(kt == 0), stop=(kt == KT - 1))
                return mm

            def by_token(out, x, w):
                for tt in range(TT):
                    for kt in range(KT):
                        mm = pe.matmul(out[:, tt * D:(tt + 1) * D], x[:, kt, tt * P:(tt + 1) * P], w[:, kt, :],
                                       start=(kt == 0), stop=(kt == KT - 1))
                return mm

            def turn(out, x):
                return pe.transpose(out, x, ident)

            def turn_tiles(out, x):
                for a in range(2):
                    for b in range(2):
                        t = turn(out[:, b * 256 + a * P:b * 256 + (a + 1) * P], x[:, a, b * P:(b + 1) * P])
                return t

            def A1(b):
                need(pe, "ld_uT", b * 16 + 16)
                if first(b):
                    pe.wait_ge(S["ld_a"], 48)
                need(pe, "b_v_out", b)
                project(psum(4), a_w["q"], uT).then_inc(S["a_q"], 1)

            def A1b(b):
                need(pe, "b_rest", b * 2)
                project(psum(5), a_w["k"], uT).then_inc(S["a_k"], 1)
                need(pe, "a_q_out", b + 1)
                project(psum(4), a_w["v"], uT).then_inc(S["a_v"], 1)

            def A2(b):
                if first(b):
                    pe.wait_ge(S["ld_cst"], 32)
                    pe.wait_ge(S["ld_ssm"], 64)
                    for n, tile0, tile1 in ((0, 0, 1), (1, 4, 3), (2, 5, 1)):
                        for ft, m in enumerate((tile0, tile1)):
                            for kt in range(KT):
                                mm = pe.matmul(psum(n, ft * D, (ft + 1) * D), fwd[:, kt, m * P:(m + 1) * P], ssm[:, kt, :],
                                               start=(kt == 0), stop=(kt == KT - 1))
                        mm.then_inc(S["set_pe"], 1)
                need(pe, "a_kv", b + 1)
                need(pe, "a_k_out", b + 1)
                turn_tiles(psum(5), kv).then_inc(S["a_kvT"], 1)

            def forward(part):
                def A3(b):
                    if part == 0:
                        need(pe, "a_kvT_out", b + 1)
                        need(pe, "a_v_out", b + 1)
                    for n in range(part * FREQ_TILES, (part + 1) * FREQ_TILES):
                        for kt in range(KT):
                            mm = pe.matmul(psum(4 + part, (n % 2) * D, (n % 2 + 1) * D), fwd[:, kt, n * P:(n + 1) * P],
                                           kvT[:, kt, :], start=(kt == 0), stop=(kt == KT - 1))
                    mm.then_inc(S["a_X"], 1)
                return A3

            def inverse(dh):
                def A4(b):
                    if dh == 0:
                        need(pe, "a_Y", b + 1)
                    for n in range(2 * FREQ_TILES):
                        y = Yre if n < FREQ_TILES else Yim
                        mm = pe.matmul(psum(4, dh * L, (dh + 1) * L), y[:, n % FREQ_TILES, dh * P:(dh + 1) * P],
                                       inv[:, n, :], start=(n == 0), stop=(n == 2 * FREQ_TILES - 1))
                    mm.then_inc(S["a_y"], 1)
                return A4

            def A5(b):
                need(pe, "a_zq", b + 1)
                by_token(psum(5), z, a_w["o"]).then_inc(S["a_o"], 1)

            def C1(b):
                if first(b):
                    pe.wait_ge(S["ld_b"], 80)
                    for eh in range(KT):
                        for kt in range(KT):
                            mm = pe.matmul(psum(1, eh * R_MOD, (eh + 1) * R_MOD), b_wo[:, kt, eh * P:(eh + 1) * P],
                                           b_a[:, kt, :], start=(kt == 0), stop=(kt == KT - 1))
                    mm.then_inc(S["set_woa"], 1)
                    pe.wait_ge(S["set_dve"], 2)
                need(pe, "b_xn", b + 1)
                need(pe, "a_r", b + 1)
                turn_tiles(psum(5), xn).then_inc(S["b_hT"], 1)

            def C2(b):
                need(pe, "b_h1", b + 1)
                need(pe, "a_z", b + 1)
                project(psum(4), b_w["q"], h1T).then_inc(S["b_q"], 1)
                need(pe, "b_xT", b + 1)
                project(psum(5), b_w["k"], h1T).then_inc(S["b_k"], 1)

            def C2v(b):
                need(pe, "b_rest", b * 2 + 1)
                by_token(psum(4), h1T, b_w["v"]).then_inc(S["b_v"], 1)

            def scores(b, u):
                if u == 0:
                    need(pe, "b_act", b * FT)
                    need(pe, "st_q", (b + 1) * 48)
                    need(pe, "st_k", (b + 1) * 48)
                if u == 1:
                    need(pe, "b_r", b)
                if u >= 2:
                    need(pe, "b_exp", b * UNITS + u - 1)
                n = u % 2
                w = P if u < GROUPS else L
                pe.matmul(bank[:, n, :].rearrange("p (h k) -> p h k", k=w), identb, masks[u >= GROUPS], start=True, stop=False,
                          skip_group_check=True)
                for h, (g, eh, par) in enumerate(unit_heads(u)):
                    mm = pe.matmul(psum(n, h * w, (h + 1) * w), stack["q"][:, 2 * g + par, eh, w - P:w],
                                   stack["k"][:, 2 * g + par, eh, 0:w], start=False, stop=True, skip_group_check=True)
                mm.then_inc(S["b_s"], 1)

            def turn_probs(b, u):
                need(pe, "b_exp", b * UNITS + u + 1)
                if u:
                    need(pe, "b_pT_out", b * UNITS + u)
                for j in range(4):
                    t = turn(psum(2, j * P, (j + 1) * P), prob[:, u % 2, j * P:(j + 1) * P])
                t.then_inc(S["b_pT"], 1)

            def values(b, u):
                need(pe, "b_pT_out", b * UNITS + u + 1)
                if u == 0:
                    need(pe, "b_v_out", b + 1)
                if u == GROUPS:
                    need(pe, "b_att", b * 2 + 1)
                for h, (g, eh, par) in enumerate(unit_heads(u)):
                    head = eh * 8 + 2 * g + par
                    out = psum(3, head * (HD + 1), (head + 1) * (HD + 1))
                    if u < GROUPS:
                        mm = pe.matmul(out, probT[:, u % 2, h, :], v1[:, 0, head, :], start=True, stop=True)
                    else:
                        for kt in range(TT):
                            mm = pe.matmul(out, probT[:, u % 2, 2 * h + kt, :], v1[:, kt, head, :],
                                           start=(kt == 0), stop=(kt == TT - 1))
                mm.then_inc(S["b_pv"], 1)

            def unit(u):
                def part(b):
                    if u < UNITS:
                        scores(b, u)
                    if 1 <= u <= UNITS:
                        turn_probs(b, u - 1)
                    if 2 <= u:
                        values(b, u - 2)
                return part

            def B6a(b):
                need(pe, "b_att", b * 2 + 2)
                turn_tiles(psum(0), att).then_inc(S["b_attT"], 1)

            def B6c(b):
                need(pe, "b_exp", (b + 1) * UNITS)
                need(pe, "b_h2", b + 1)
                for kt in range(KT):
                    pe.matmul(bank[0:R_MOD, 1, L:2 * L], b_a[:, kt, :], h2T[:, kt, :], start=(kt == 0), stop=(kt == KT - 1))

            def B6b(b):
                need(pe, "b_attT_out", b + 1)
                for kt in range(KT):
                    mm = pe.matmul(bank[0:R_MOD, 1, 0:L], woa[:, kt, :], attT[:, kt, :], start=(kt == 0), stop=(kt == KT - 1))
                mm.then_inc(S["b_mod"], 1)

            def mlp(f):
                def part(b):
                    if f == 0 and first(b):
                        pe.wait_ge(S["ld_mlp"], 64)
                    n = (0, 2, 3)[f % 3]
                    cols = slice(f * P, (f + 1) * P)
                    if f >= 3:
                        need(pe, "b_act", b * FT + f - 2)
                    for kt in range(KT):
                        pe.matmul(psum(n, L, 2 * L), w_up[:, kt, cols], h2T[:, kt, :], start=(kt == 0), stop=(kt == KT - 1))
                    for kt in range(KT):
                        pe.matmul(psum(n, 0, L), w_in[:, kt, cols], h2T[:, kt, :], start=(kt == 0), stop=False)
                    if f == 0:
                        need(pe, "b_mh", b + 1)
                    pe.matmul(psum(n, 0, L), b_b[:, cols], mh[:], start=False, stop=True).then_inc(S["b_gu"], 1)
                return part

            def B8(b):
                for tt in range(TT):
                    for f in range(FT):
                        if tt == 0:
                            need(pe, "b_act", b * FT + f + 1)
                        mm = pe.matmul(psum(1, tt * D, (tt + 1) * D), actT[:, f, tt * P:(tt + 1) * P], w_down[:, f, :],
                                       start=(f == 0), stop=(f == FT - 1))
                mm.then_inc(S["b_dn"], 1)

            def D1(b):
                need(pe, "b_x2", b + 1)
                need(pe, "d_pos", b)
                turn_tiles(psum(6), x2).then_inc(S["d_xT"], 1)

            def D2(b):
                if first(b):
                    pe.wait_ge(S["ld_d"], 128)
                need(pe, "d_xT_out", b + 1)
                need(pe, "d_base", b)
                project(psum(7), d_w["k"], x2T).then_inc(S["d_k_ps"], 1)

            def D2x(b):
                project(psum(6), d_w["v"], x2T).then_inc(S["d_v"], 1)

            def D2q(b):
                need(pe, "d_k_out", b + 1)
                project(psum(7), d_w["q"], x2T).then_inc(S["d_q"], 1)

            def D3(b):
                need(pe, "d_vh", b + 1)
                by_token(psum(6), vh, d_w["o"]).then_inc(S["d_o"], 1)

            def D4(b):
                need(pe, "d_x3", b + 1)
                turn_tiles(psum(7), x3).then_inc(S["d_x3T"], 1)

            def D4l(b):
                need(pe, "d_x3T_out", b + 1)
                need(pe, "d_r", b + 1)
                for tt in range(TT):
                    for kt in range(KT):
                        mm = pe.matmul(psum(6, tt * E_N, (tt + 1) * E_N), x3T[:, kt, tt * P:(tt + 1) * P], gate_w[:, kt, :],
                                       start=(kt == 0), stop=(kt == KT - 1))
                mm.then_inc(S["d_lg"], 1)

            def shared(n):
                at, w = SH_TILES[n]
                def part(b):
                    if n:
                        need(pe, "d_sact", b * 3 + n)
                    else:
                        need(pe, "d_x3T_out", b + 1)
                    for g in range(2):
                        for kt in range(KT):
                            mm = pe.matmul(bank[0:w, 7, g * L:(g + 1) * L], sh_gu[:, kt, g * SH_I + at:g * SH_I + at + w],
                                           x3T[:, kt, :], start=(kt == 0), stop=(kt == KT - 1))
                    mm.then_inc(S["d_sg"], 1)
                return part

            def D5(b):
                need(pe, "d_mask", b + 1)
                pe.matmul(psum(6, 128, 192), beforeb, mkb[:, 0, :], start=True, stop=False)
                pe.matmul(psum(6, 128, 192), onesb, seen[:], start=False, stop=True)
                pe.matmul(psum(6, 192, 256), beforeb, mkb[:, 1, :], start=True, stop=False)
                pe.matmul(psum(6, 192, 256), onesb, mkb[:, 0, :], start=False, stop=False)
                pe.matmul(psum(6, 192, 256), onesb, seen[:], start=False, stop=True).then_inc(S["d_rank"], 1)

            def shared_out(tt):
                def part(b):
                    if tt == 0:
                        need(pe, "d_sact", b * 3 + 3)
                    for n, (_, w) in enumerate(SH_TILES):
                        mm = pe.matmul(psum(7, tt * D, (tt + 1) * D), sact[0:w, n, tt * P:(tt + 1) * P], sh_dn[0:w, n, :],
                                       start=(n == 0), stop=(n == len(SH_TILES) - 1))
                    if tt == TT - 1:
                        mm.then_inc(S["d_sd"], 1)
                return part

            turns(pe, {"A1": A1, "A1b": A1b, "C1": C1, "C2": C2, "C2v": C2v, "A2": A2, "A3a": forward(0), "A3b": forward(1), "A4a": inverse(0), "A4b": inverse(1),
                       "A5": A5, "B6a": B6a, "B6b": B6b, "B6c": B6c, "B8": B8,
                       "D1": D1, "D2k": D2, "D2x": D2x, "D2q": D2q, "D3": D3, "D4": D4, "D4l": D4l, "D5": D5, "SDa": shared_out(0), "SDb": shared_out(1),
                       **{f"u{u}": unit(u) for u in range(UNITS + 2)}, **{f"f{f}": mlp(f) for f in range(FT)},
                       **{f"S{n}": shared(n) for n in range(3)}})

            pe.wait_ge(S["d_pos"], NB)
            pe.wait_ge(S["d_base"], NB)
            pe.wait_ge(S["d_dest"], NB)
            pe.matmul(psum(6, 0, E_N), onesb, seen[:], start=True, stop=True).then_inc(S["r_tot"], 1)
            pe.wait_ge(S["r_tab"], 1)
            for j in range(4):
                mm = pe.matmul(bank[0:1, 7, :].rearrange("o (c j) -> o c j", j=4)[:, :, j], ctab[:, j:j + 1], ident,
                               start=True, stop=True)
            mm.then_inc(S["r_row"], 1)
            pe.wait_ge(S["r_spot"], 1)
            for k in range(2):
                mm = pe.matmul(psum(6, k * 2 * P, k * 2 * P + P), onesb, spot[:, k, :], start=True, stop=True)
            mm.then_inc(S["r_all"], 1)

            def turn_rows(c):
                s, out = c.slot(RING), psum(c.slot(3))
                need(pe, f"m_x{s}", c.before(RING) * 16 + 16)
                need(pe, "m_xT_out", c.no - 2)
                for kt in range(KT):
                    t = turn(out[:, kt * P:(kt + 1) * P], xc_row[s][:, kt * P:(kt + 1) * P])
                t.then_inc(S["m_xT"], 1)

            def inner(c):
                s, n = c.slot(RING), c.slot(3)
                need(pe, f"m_w{s}", c.before(RING) * 32 + 32)
                need(pe, "m_xT_out", c.no + 1)
                need(pe, "m_hs", c.no - 2)
                for m in range(2):
                    for kt in range(KT):
                        mm = pe.matmul(bank[0:IH, 3 + n, m * P:(m + 1) * P], w1[s][:, kt, m * IH:(m + 1) * IH], xcT[n][:, kt, :],
                                       start=(kt == 0), stop=(kt == KT - 1))
                mm.then_inc(S["m_h"], 1)

            def outer(c):
                s, n = c.slot(RING), c.slot(3)
                need(pe, "m_hs", c.no + 1)
                need(pe, "m_y_out", c.no - 1)
                for m in range(2):
                    mm = pe.matmul(psum(6 + c.slot(2), 0, D), hs[n][:, m, :], w2[s][:, m, :], start=(m == 0), stop=(m == 1))
                mm.then_inc(S["m_y"], 1)

            chunk_loop(pe, [turn_rows, inner, None, outer])

            def add_up(pair, h, nth):
                for t in range(2):
                    need(pe, f"f_ld{2 * h + t}", nth * 16)
                need(pe, "f_diag", pair + 1)
                need(pe, "f_r", pair - 1)
                for t in range(2):
                    for k in range(TOPK):
                        mm = pe.matmul(psum(h, t * D, (t + 1) * D), diag[2 * h + t][:, k, :], yg[2 * h + t][:, k, :],
                                       start=(k == 0), stop=(k == TOPK - 1))
                mm.then_inc(S["f_sum"], 1)

            pair_loop(pe, [add_up])

        @block.scalar
        def _(act):
            act.dma_start(vec[:], d["vec"]).then_inc(S["ld_vec"], 16)
            act.dma_start(cst[:], d["cst"]).then_inc(S["ld_cst"], 16)
            act.dma_start(csb[:], d["csb"]).then_inc(S["ld_cst"], 16)
            act.wait_ge(S["ld_a"], 48)
            act.dma_start(X[:], d["u"].rearrange("b (t p) d -> p (b t) d", p=P)).then_inc(S["ld_u"], 16)
            act.dma_start(bo[:], d["bo"]).then_inc(S["ld_u"], 16)

            def column(name, kt):
                return vec[:, VEC[name] + kt:VEC[name] + kt + 1]

            act.wait_ge(S["ld_vec"], 16)
            act.wait_ge(S["set_pool"], 1)

            def biased(*names):
                def part(b):
                    for n, dst, at, bk, used in names:
                        need(act, f"a_{n}", b + 1)
                        need(act, used, b)
                        for eh in range(KT):
                            i = act.activation(dst[:, eh, at:at + L], psum(bk, eh * L, (eh + 1) * L), ACT.Identity,
                                               bias=column("b" + n, eh))
                        i.then_inc(S[f"a_{n}_out"], 1)
                return part

            def A2(b):
                need(act, "a_kvT", b + 1)
                need(act, "b_third", b * 2)
                need(act, "a_X", b * 2)
                act.activation(kvT[:], psum3(5), ACT.Copy).then_inc(S["a_kvT_out"], 1)

            def C1(b):
                need(act, "b_hT", b + 1)
                need(act, "b_v", b)
                for kt in range(KT):
                    i = act.activation(h1T[:, kt, :], psum(5, kt * L, (kt + 1) * L), ACT.Identity, scale=column("ln1", kt))
                i.then_inc(S["b_h1"], 1)
                need(act, "b_h2", b)
                act.activation(xnT[:], psum3(5), ACT.Copy).then_inc(S["b_xT"], 1)

            def C2(b):
                for n, bk, scale, left in (("q", 4, HD ** -0.5, 16), ("k", 5, 1.0, 32)):
                    need(act, f"b_{n}", b + 1)
                    need(act, f"st_{n}w", b * left)
                    act.activation(part[n][:, 0], psum3(bk), ACT.Copy, scale=scale).then_inc(S["b_first"], 1)

            def C2v(b):
                for i, n in enumerate("qk"):
                    need(act, "b_rest", b * 2 + i + 1)
                    act.activation(part[n][:, 1], rest[n][:], ACT.Copy).then_inc(S["b_second"], 1)
                need(act, "b_v", b + 1)
                need(act, "b_pv", b * UNITS)
                act.activation(v1[:, :, :, 0:HD], bank[:, 4, :].rearrange("p (t h e) -> p t h e", t=TT, h=HEADS),
                               ACT.Copy).then_inc(S["b_v_out"], 1)

            def unit(u):
                def part(b):
                    if u < UNITS:
                        need(act, "b_max", b * UNITS + u + 1)
                        need(act, "b_pT", b * UNITS + u - 1)
                        w = P if u < GROUPS else L
                        for h in range(512 // w):
                            i = act.activation(prob[:, u % 2, h * w:(h + 1) * w], psum(u % 2, h * w, (h + 1) * w), ACT.Exp,
                                               bias=nmx[:, u, h:h + 1])
                        i.then_inc(S["b_exp"], 1)
                    if 1 <= u <= UNITS:
                        need(act, "b_pT", b * UNITS + u)
                        need(act, "b_pv", b * UNITS + u - 2)
                        act.activation(probT[:, (u - 1) % 2, :, :], bank[:, 2, :].rearrange("p (j q) -> p j q", j=4), ACT.Copy
                                       ).then_inc(S["b_pT_out"], 1)
                return part

            def B6a(b):
                need(act, "b_attT", b + 1)
                need(act, "b_mod", b)
                act.activation(attT[:], psum3(0), ACT.Copy).then_inc(S["b_attT_out"], 1)

            def B6b(b):
                need(act, "b_mod", b + 1)
                need(act, "b_mh", b)
                act.activation(th[:], bank[0:R_MOD, 1, 0:L], ACT.Tanh).then_inc(S["b_tanh"], 1)

            def mlp(f):
                def part(b):
                    need(act, "b_gu", b * FT + f + 1)
                    need(act, "b_act", b * FT + f - 1)
                    act.activation(gt[:, f % 2, :], psum((0, 2, 3)[f % 3], 0, L), ACT.Tanh, scale=0.5).then_inc(S["b_gt"], 1)
                return part

            def D1(b):
                need(act, "d_xT", b + 1)
                need(act, "d_q", b)
                act.activation(x2T[:], psum3(6), ACT.Copy).then_inc(S["d_xT_out"], 1)

            def D2(b):
                need(act, "d_k_ps", b + 1)
                need(act, "d_kv", b)
                act.activation(d_k[:], psum3(7), ACT.Copy, scale=float(D) ** 0.5 / L).then_inc(S["d_k_out"], 1)

            def D4(b):
                need(act, "d_x3T", b + 1)
                need(act, "d_sg", b * 3)
                act.activation(x3T[:], psum3(7), ACT.Copy).then_inc(S["d_x3T_out"], 1)

            def D4m(b):
                need(act, "d_max", b + 1)
                for tt in range(TT):
                    i = act.activation(ex[:, tt, :], psum(6, tt * E_N, (tt + 1) * E_N), ACT.Exp, bias=nlg[:, tt:tt + 1])
                i.then_inc(S["d_ex"], 1)

            def shared(n):
                w = SH_TILES[n][1]
                def part(b):
                    need(act, "d_sg", b * 3 + n + 1)
                    need(act, "d_sact", b * 3 + n)
                    act.activation(sgt[0:w, :], bank[0:w, 7, 0:L], ACT.Tanh, scale=0.5).then_inc(S["d_sgt"], 1)
                return part

            turns(act, {"A1": biased(("q", q_sb, 2, 4, "a_qc")), "A1b": biased(("k", k_sb, 2, 5, "a_kc"), ("v", v_sb, 0, 4, "a_kv")),
                        "A2": A2, "C1": C1, "C2": C2, "C2v": C2v, "B6a": B6a, "B6b": B6b, "D1": D1, "D2k": D2, "D4": D4, "D4m": D4m,
                        **{f"u{u}": unit(u) for u in range(UNITS + 2)}, **{f"f{f}": mlp(f) for f in range(FT)},
                        **{f"S{n}": shared(n) for n in range(3)}})

            def silu(c):
                n = c.slot(3)
                need(act, "m_h", c.no + 1)
                need(act, "m_y", c.no - 2)
                act.activation(hs[n], bank[0:IH, 3 + n, 0:2 * P].rearrange("p (a b) -> p a b", a=2), ACT.Silu
                               ).then_inc(S["m_hs"], 1)

            def load(c):
                s = c.slot(RING)
                e, _ = chunk_values(act, c)
                need(act, "m_y", c.no - (RING - 1))
                act.dma_start(w2[s], d["e_w2"][bass.ds(e, 1)].rearrange("o p k h -> p (o k) h")).then_inc(S[f"m_w{s}"], 16)

            act.wait_ge(S["r_table"], 1)
            chunk_loop(act, [load, None, None, silu])

            for s in range(RING):
                act.wait_ge(S[f"m_st{s}"], 16 * ((CHUNKS - s + RING - 1) // RING))

            def collect(pair, h, nth):
                if first(pair):
                    act.wait_ge(S["m_y"], CHUNKS)
                need(act, "f_sum", pair - 1)
                for t in range(2):
                    n = pair * 2 + t
                    rows = slice(n * P * TOPK, (n + 1) * P * TOPK) if isinstance(n, int) else bass.ds(n * P * TOPK, P * TOPK)
                    act.dma_start(yg[2 * h + t], y_rows[rows, :].rearrange("(p k) d -> p k d", k=TOPK)
                                  ).then_inc(S[f"f_ld{2 * h + t}"], 16)
                weigh(pair, h)


            def weigh(pair, h):
                for t in range(2):
                    n = pair * 2 + t
                    w = TOPW[:, slice(n, n + 1) if isinstance(n, int) else bass.ds(n, 1), :].rearrange("p o k -> p (o k)")
                    for k in range(TOPK):
                        i = act.activation(diag[2 * h + t][:, k, :], ident, ACT.Identity, scale=w[:, k:k + 1])
                i.then_inc(S["f_diag"], 1)

            out = d["out"].rearrange("b (t p) d -> (b t) p d", p=P)

            def put(pair, h, nth):
                need(act, "f_out", pair + 1)
                for t in range(2):
                    n = pair * 2 + t
                    n = slice(n, n + 1) if isinstance(n, int) else bass.ds(n, 1)
                    act.dma_start(out[n].rearrange("o p d -> p (o d)"), outb[2 * h + t]).then_inc(S[f"f_st{h}"], 16)

            pair_loop(act, [collect, None, put])
            for h in range(2):
                act.wait_ge(S[f"f_st{h}"], 16 * (NT // 2))

        @block.vector
        def _(dve):
            ca, cbn, cd = Chain(dve, "ch_a", 7), Chain(dve, "ch_b", 12), Chain(dve, "ch_d", 25)

            def col(name, kt, n=1, j=0):
                at = VEC[name] + kt * n + j
                return vec[:, at:at + 1]

            def moments(ch, m, n=TT):
                for t in range(n):
                    i = dve.bn_stats(m["st"][:, t, :], m["r"][:, t, :])
                ch.link(i)
                alone(dve)
                for t in range(n):
                    i = dve.bn_aggr(m["mv"][:, t, :], m["st"][:, t, :])
                ch.link(i)
                return dve.tensor_scalar(m["v"][:, 0:n], m["mv"][:, 0:n, 1], LN_EPS, None, ALU.add)

            def scaled(m, outs):
                for t, out in enumerate(outs):
                    i = dve.tensor_scalar(out, m["r"][:, t, :], m["mv"][:, t, 0:1], m["y"][:, t:t + 1], ALU.subtract, ALU.mult)
                return i

            def slot(b, tt):
                n = b * TT + tt
                return X[:, n, :] if isinstance(n, int) else X[:, bass.ds(n, 1), :].rearrange("p o d -> p (o d)")

            def slots(t, b):
                return t[:, b * TT:(b + 1) * TT] if isinstance(b, int) else t[:, bass.ds(b * TT, TT)]

            dve.memset(x3_meta[:, :, 1 + TOPK:], 0.0)
            dve.wait_ge(S["ld_vec"], 16)
            dve.wait_ge(S["ld_cst"], 32)
            dve.wait_ge(S["set_pool"], 1)

            def conv(n, src, dst):
                def part(b):
                    if n == "q":
                        ca.start(b)
                        need(dve, "a_x1", b)
                    if n == "k":
                        need(dve, "b_h2", b)
                    need(dve, f"a_{n}_out", b + 1)
                    for eh in range(KT):
                        i = dve.tensor_scalar(dst[:, eh, :], src[:, eh, 2:2 + L], col(f"c{n}w", eh, 3, 2), col(f"c{n}b", eh),
                                              ALU.mult, ALU.add)
                    ca.link(i)
                    for j in (1, 0):
                        for eh in range(KT):
                            i = dve.scalar_tensor_tensor(dst[:, eh, :], src[:, eh, j:j + L], col(f"c{n}w", eh, 3, j),
                                                         dst[:, eh, :], ALU.mult, ALU.add)
                        if j == 1:
                            ca.link(i)
                    i.then_inc(S[f"a_{n}c"], 1)
                    if n == "k":
                        need(dve, "a_kc", b + 1)
                        need(dve, "a_v_out", b + 1)
                        need(dve, "a_kvT", b)
                        dve.tensor_tensor(kv[:], kc[:], v_sb[:], ALU.mult).then_inc(S["a_kv"], 1)
                return part

            def A3(b):
                if first(b):
                    dve.wait_ge(S["set_pe"], 3)
                    for n, t in enumerate((tabA, tabB, tabD)):
                        i = dve.tensor_copy(t[:], psum3(n))
                    i.then_inc(S["set_dve"], 1)
                    dve.wait_ge(S["set_dve"], 1)
                need(dve, "a_X", b * 2 + 2)
                for n, left in (("q", 16), ("k", 32)):
                    need(dve, f"st_{n}w", b * left)
                need(dve, "a_y", b * 2)
                for n, (bk, tab) in enumerate(((4, tabA), (5, tabB), (4, tabB), (5, tabD))):
                    i = dve.tensor_tensor(pr[n], psum3(bk), tab[:], ALU.mult)
                i.then_inc(S["a_pr"], 1)

            def A4(b):
                need(dve, "a_y", b * 2 + 2)
                need(dve, "a_kv", b + 1)
                for eh in range(KT):
                    i = dve.scalar_tensor_tensor(kv[:, eh, :], kv[:, eh, :], col("skip", eh), psum(4, eh * L, (eh + 1) * L),
                                                 ALU.mult, ALU.add)
                i.then_inc(S["a_z"], 1)
                need(dve, "a_z", b + 1)
                need(dve, "a_qc", b + 1)
                need(dve, "b_third", b * 2 - 1)
                need(dve, "a_o", b)
                dve.tensor_tensor(z[:], kv[:], qc[:], ALU.mult).then_inc(S["a_zq"], 1)

            def A5(b):
                need(dve, "a_o", b + 1)
                if first(b):
                    dve.wait_ge(S["ub"], 1)
                m = nrm["A"]
                dve.tensor_tensor(m["r"][:], psum3(5), slots(X, b), ALU.add).then_inc(S["a_r"], 1)
                need(dve, "a_r", b + 1)
                moments(ca, m).then_inc(S["n_varA"], 1)

            def A5o(b):
                need(dve, "n_invA", b + 1)
                scaled(nrm["A"], [slot(b, tt) for tt in range(TT)]).then_inc(S["a_x1"], 1)

            def A6(b):
                need(dve, "a_x1", b + 1)
                need(dve, "b_hT", b)
                need(dve, "b_xn", b)
                for tt in range(TT):
                    i = dve.scalar_tensor_tensor(xn[:, tt, :], slot(b, tt), 1.0 / D, slot(b, tt), ALU.mult, ALU.mult,
                                                 accum_out=ms[:, tt:tt + 1])
                ca.link(i)
                dve.tensor_scalar(nrm["R"]["v"][:], ms[:], RMS_EPS, None, ALU.add).then_inc(S["n_varR"], 1)

            def A6o(b):
                need(dve, "n_invR", b + 1)
                for tt in range(TT):
                    i = dve.tensor_scalar(xn[:, tt, :], slot(b, tt), nrm["R"]["y"][:, tt:tt + 1], None, ALU.mult)
                i.then_inc(S["b_xn"], 1)

            def C1(b):
                if first(b):
                    dve.wait_ge(S["set_woa"], 1)
                    dve.tensor_copy(woa[:], psum(1, 0, KT * R_MOD).rearrange("p (k r) -> p k r", k=KT)).then_inc(S["set_dve"], 1)

            def C2(b):
                for i, (n, bk, scale) in enumerate((("q", 4, HD ** -0.5), ("k", 5, 1.0))):
                    need(dve, "b_first", b * 2 + i + 1)
                    need(dve, "b_third", b * 2 + i - 1)
                    dve.scalar_tensor_tensor(rest[n][:], psum3(bk), scale, part[n][:, 0], ALU.mult, ALU.subtract
                                             ).then_inc(S["b_rest"], 1)

            def unit(u):
                w = P if u < GROUPS else L
                def part(b):
                    if u == 0:
                        cbn.start(b)
                    need(dve, "b_s", b * UNITS + u + 1)
                    need(dve, "b_exp", (b - 1) * UNITS + u + 1)
                    dve.tensor_reduce(nmx[:, u, 0:512 // w], bank[:, u % 2, :].rearrange("p (h k) -> p h k", k=w), AX, ALU.max,
                                      negate=True).then_inc(S["b_max"], 1)
                return part

            def divide(tt):
                def part(b):
                    need(dve, "b_pv", b * UNITS + (GROUPS, UNITS)[tt])
                    o = psum(3, 0, HEADS * (HD + 1)).rearrange("p (h e) -> p h e", h=HEADS)
                    cbn.link(dve.reciprocal(rec[:, tt, :], o[:, :, HD]))
                    need(dve, "b_x2", b)
                    dve.tensor_tensor(att[:, tt, :].rearrange("p (h e) -> p h e", h=HEADS), o[:, :, 0:HD],
                                      rec[:, tt, :].rearrange("p (h o) -> p h o", o=1).broadcast_to([P, HEADS, HD]),
                                      ALU.mult).then_inc(S["b_att"], 1)
                return part

            def B6(b):
                need(dve, "b_tanh", b + 1)
                need(dve, "b_gu", b * FT)
                dve.scalar_tensor_tensor(mh[:], th[:], MOD_SCALE, bank[0:R_MOD, 1, L:2 * L], ALU.mult, ALU.mult
                                         ).then_inc(S["b_mh"], 1)

            def mlp(f):
                def part(b):
                    n = (0, 2, 3)[f % 3]
                    if f == 0:
                        need(dve, "b_dn", b)
                    need(dve, "b_gt", b * FT + f + 1)
                    cbn.link(dve.scalar_tensor_tensor(gs[:, f % 2, :], gt[:, f % 2, :], 1.0, psum(n, 0, L), ALU.add, ALU.mult))
                    dve.scalar_tensor_tensor(actT[:, f, :], gs[:, f % 2, :], 0.5, psum(n, L, 2 * L), ALU.mult, ALU.mult
                                             ).then_inc(S["b_act"], 1)
                return part

            def B8(b):
                need(dve, "b_dn", b + 1)
                m = nrm["B"]
                for tt in range(TT):
                    i = dve.scalar_tensor_tensor(m["r"][:, tt, :], slot(b, tt), 2.0, psum(1, tt * D, (tt + 1) * D), ALU.mult, ALU.add)
                i.then_inc(S["b_r"], 1)
                need(dve, "b_r", b + 1)
                moments(cbn, m).then_inc(S["n_varB"], 1)
                need(dve, "n_invB", b + 1)
                need(dve, "d_r", b)
                need(dve, "d_xT", b)
                scaled(m, [x2[:, tt, :] for tt in range(TT)]).then_inc(S["b_x2"], 1)

            def D2(b):
                cd.start(b)
                need(dve, "d_x3", b)
                need(dve, "d_k_out", b + 1)
                need(dve, "d_v", b + 1)
                dve.tensor_tensor(d_kv[:], d_k[:], psum3(6), ALU.mult).then_inc(S["d_kv"], 1)
                need(dve, "d_kv", b + 1)
                for eh in range(KT):
                    i = dve.tensor_tensor_scan(d_cs[:, eh, :], ones_row[:], d_kv[:, eh, :], 0.0, ALU.mult, ALU.add)
                cd.link(i)

            def D2w(b):
                need(dve, "d_q", b + 1)
                need(dve, "d_o", b)
                dve.tensor_tensor(vh[:], psum3(7), d_cs[:], ALU.mult).then_inc(S["d_vh"], 1)

            def D3(b):
                need(dve, "d_o", b + 1)
                need(dve, "b_x2", b + 1)
                m = nrm["D"]
                dve.tensor_tensor(m["r"][:], psum3(6), x2[:], ALU.add).then_inc(S["d_r"], 1)
                need(dve, "d_r", b + 1)
                moments(cd, m).then_inc(S["n_varD"], 1)

            def D3o(b):
                need(dve, "n_invD", b + 1)
                need(dve, "d_scat", b * 16 * TT * TOPK)
                need(dve, "d_base", b)
                scaled(nrm["D"], [x3[:, tt, :] for tt in range(TT)]).then_inc(S["d_x3"], 1)

            def D4m(b):
                need(dve, "d_lg", b + 1)
                alone(dve)
                for tt in range(TT):
                    i = dve.max(lg8[:, tt, :], psum(6, tt * E_N, (tt + 1) * E_N))
                cd.link(i)
                dve.tensor_scalar(nlg[:], lg8[:, :, 0], -1.0, None, ALU.mult).then_inc(S["d_max"], 1)

            def D4t(b):
                need(dve, "d_ex", b + 1)
                alone(dve)
                for tt in range(TT):
                    i = dve.max(top8[:, tt, :], ex[:, tt, :])
                cd.link(i)
                alone(dve)
                for tt in range(TT):
                    i = dve.max_index(top8i[:, tt, :], top8[:, tt, :], ex[:, tt, :])
                cd.link(i)
                cd.link(dve.tensor_copy(idxf[:], top8i[:]))

            def D4k(b):
                for k in range(TOPK):
                    for tt in range(TT):
                        if k == 0:
                            i = dve.tensor_scalar(mk[:, tt, :], iota, idxf[:, tt, 0:1], None, ALU.is_equal)
                        else:
                            dst = mkb if k == TOPK - 1 else mk
                            i = dve.scalar_tensor_tensor(dst[:, tt, :], iota, idxf[:, tt, k:k + 1], mk[:, tt, :], ALU.is_equal, ALU.add)
                    if k < TOPK - 1:
                        cd.link(i)
                i.then_inc(S["d_mask"], 1)

            def D4w(b):
                cd.link(dve.tensor_reduce(wsum[:], top8[:, :, 0:TOPK], AX, ALU.add))
                cd.link(dve.reciprocal(wrec[:], wsum[:]))
                cd.step(dve.tensor_tensor(slots(TOPW, b), top8[:, :, 0:TOPK],
                                          wrec[:].rearrange("p (t o) -> p t o", o=1).broadcast_to([P, TT, TOPK]), ALU.mult))

            def shared(n):
                w = SH_TILES[n][1]
                def part(b):
                    need(dve, "d_sgt", b * 3 + n + 1)
                    cd.link(dve.scalar_tensor_tensor(sgs[0:w, :], sgt[0:w, :], 1.0, bank[0:w, 7, 0:L], ALU.add, ALU.mult))
                    if n == 0:
                        need(dve, "d_sd", b)
                    dve.scalar_tensor_tensor(sact[0:w, n, :], sgs[0:w, :], 0.5, bank[0:w, 7, L:2 * L], ALU.mult, ALU.mult
                                             ).then_inc(S["d_sact"], 1)
                return part

            def D5p(b):
                need(dve, "d_rank", b + 1)
                for tt in range(TT):
                    i = dve.tensor_tensor(pos[:, tt, :], psum(6, 128 + tt * E_N, 192 + tt * E_N), region, ALU.add)
                i.then_inc(S["d_pos"], 1)
                for tt in range(TT):
                    cd.link(dve.tensor_tensor(seen[:], seen[:], mkb[:, tt, :], ALU.add))

            def D5h(b):
                need(dve, "d_pos", b + 1)
                for tt in range(TT):
                    for k in range(TOPK):
                        i = dve.scalar_tensor_tensor(hit[:, tt, k, :], iota, idxf[:, tt, k:k + 1], pos[:, tt, :], ALU.is_equal, ALU.mult)
                cd.link(i)
                cd.link(dve.tensor_reduce(destf[:], hit[:], AX, ALU.add))
                need(dve, "d_scat", b * 16 * TT * TOPK)
                cd.step(dve.tensor_copy(x3_meta[:, :, 1:1 + TOPK], idxf[:, :, 0:TOPK]))
                cd.link(dve.tensor_copy(x3_meta[:, :, 0], token_row))
                cd.step(dve.tensor_scalar(token_row, token_row, float(L * TOPK), None, ALU.add))
                dve.tensor_copy(desti[:].rearrange("p (t k) -> p t k", t=TT), destf[:]).then_inc(S["d_dest"], 1)

            def SD(b):
                need(dve, "d_sd", b + 1)
                for tt in range(TT):
                    i = dve.tensor_tensor(slot(b, tt), psum(7, tt * D, (tt + 1) * D), x3[:, tt, :], ALU.add)
                i.then_inc(S["d_base"], 1)

            turns(dve, {"A1q": conv("q", q_sb, qc), "A1k": conv("k", k_sb, kc), "A3p": A3, "A4z": A4, "A5n": A5, "A5o": A5o,
                        "A6n": A6, "A6o": A6o, "C1": C1, "C2": C2, **{f"u{u}": unit(u) for u in range(UNITS)},
                        "t0": divide(0), "t1": divide(1), "B6b": B6, **{f"f{f}": mlp(f) for f in range(FT)}, "B8": B8,
                        "D2v": D2, "D2w": D2w, "D3n": D3, "D3o": D3o, "D4m": D4m, "D4t": D4t, "D4k": D4k, "D4w": D4w, "D5p": D5p, "D5h": D5h,
                        **{f"S{n}": shared(n) for n in range(3)}, "SD": SD})
            for ch in (ca, cbn, cd):
                assert ch.k == ch.per, (ch.name, ch.k, ch.per)

            cr = Chain(dve, "ch_r", 0)
            dve.wait_ge(S["r_tot"], 1)
            tot = psum(6, 0, E_N)
            cr.link(dve.tensor_scalar(cn[:], tot, 1.0 / P, (P - 1.0) / P - 0.5 + 0.5 / P / 2, ALU.mult, ALU.add))
            cr.link(dve.tensor_scalar(cn[:], cn[:], ROUND, None, ALU.add))
            cr.link(dve.tensor_scalar(cn[:], cn[:], -ROUND, None, ALU.add))
            cr.step(dve.scalar_tensor_tensor(pad_e[:], cn[:], -float(P), tot, ALU.mult, ALU.add))
            cr.link(dve.tensor_tensor_scan(cum[:], ones_row[:, 0:E_N], cn[:], 0.0, ALU.mult, ALU.add))
            for k in range(2):
                cr.step(dve.scalar_tensor_tensor(scr[:, 0, :], cum[:], chunk_no[:, k:k + 1], ones_row[:, 0:E_N], ALU.is_le, ALU.mult,
                                                 accum_out=ce[:, k:k + 1]))
                cr.link(dve.scalar_tensor_tensor(scr[:, 1, :], cum[:], chunk_no[:, k:k + 1], cn[:], ALU.is_le, ALU.mult,
                                                 accum_out=cb[:, k:k + 1]))
                cr.link(dve.scalar_tensor_tensor(scr[:, 2, :], iota, ce[:, k:k + 1], pad_e[:], ALU.is_equal, ALU.mult,
                                                 accum_out=co[:, k:k + 1]))
            cr.link(dve.tensor_tensor(cb[:], chunk_no, cb[:], ALU.subtract))
            cr.link(dve.scalar_tensor_tensor(co[:], cb[:], float(P), co[:], ALU.mult, ALU.add))
            cr.link(dve.scalar_tensor_tensor(crow[:], ce[:], float(CAP), co[:], ALU.mult, ALU.add))
            dve.tensor_scalar(ctab[:, 1::2], crow[:], float(P), None, ALU.add)
            dve.tensor_scalar(ctab[:, 0::2], ce[:], float(E_N - 1), None, ALU.min).then_inc(S["r_tab"], 1)
            dve.wait_ge(S["r_row"], 1)
            dve.tensor_copy(table, bank[0:1, 7, :]).then_inc(S["r_table"], 1)
            for k in range(2):
                i = dve.tensor_scalar(spot[:, k, :], ident, ctab[:, 2 * k:2 * k + 1], None, ALU.mult)
            i.then_inc(S["r_spot"], 1)
            dve.wait_ge(S["r_all"], 1)
            cr.link(dve.tensor_copy(expert_of.rearrange("p (c k) -> p k c", k=2), psum3(6)[:, :, 0:P]))
            cm = Chain(dve, "ch_m", 1)

            def turned(c):
                n = c.slot(3)
                need(dve, "m_xT", c.no + 1)
                need(dve, "m_h", c.no - 2)
                dve.tensor_copy(xcT[n], bank[:, n, 0:2 * P].rearrange("p (a b) -> p a b", a=2)).then_inc(S["m_xT_out"], 1)

            def places(c):
                s = c.slot(RING)
                meta = xc_row[s][:, D:XW]
                cm.start(c.no)
                need(dve, f"m_x{s}", c.before(RING) * 16 + 16)
                need(dve, f"m_st{s}", c.before(RING) * 16)
                e = expert_of[:, c.no:c.no + 1] if isinstance(c.no, int) else expert_of[:, bass.ds(c.no, 1)]
                cm.link(dve.scalar_tensor_tensor(found[s][:], meta[:, 1:1 + TOPK], e, iota[:, 0:TOPK], ALU.is_equal, ALU.mult,
                                                 accum_out=choice[s][:]))
                dve.tensor_tensor(ids[s][:], meta[:, 0:1], choice[s][:], ALU.add).then_inc(S["m_ids"], 1)

            def result(c):
                s = c.slot(RING)
                need(dve, "m_y", c.no + 1)
                need(dve, f"m_st{s}", c.before(RING) * 16)
                dve.tensor_copy(yc[s], psum(6 + c.slot(2), 0, D)).then_inc(S["m_y_out"], 1)

            chunk_loop(dve, [turned, places, None, result])

            cf = Chain(dve, "ch_f", 2)
            m = nrm["F"]

            def finish(pair, h, nth):
                cf.start(pair)
                need(dve, "f_sum", pair + 1)
                need(dve, "f_out", pair)
                dve.tensor_tensor(m["r"][:], psum3(h), slots(X, pair), ALU.add).then_inc(S["f_r"], 1)
                need(dve, "f_r", pair + 1)
                moments(cf, m).then_inc(S["n_varF"], 1)
                need(dve, "n_invF", pair + 1)
                need(dve, f"f_st{h}", (nth - 1) * 32)
                scaled(m, outb[2 * h:2 * h + 2]).then_inc(S["f_out"], 1)

            pair_loop(dve, [finish])


def layouts(x):
    def tiles(a, p=P):
        return np.ascontiguousarray(a.reshape(-1, p, a.shape[-1]).swapaxes(0, 1))

    def transposed(name):
        return tiles(x[name].T)

    def channel(name):
        return x[name].reshape(KT, P, -1).swapaxes(0, 1).reshape(P, -1)

    u = x["L0_attn_u"]
    a = {"u": u, "uT": np.ascontiguousarray(u.swapaxes(1, 2).reshape(NB, KT, P, L).swapaxes(1, 2))}
    a["vec"] = np.concatenate([channel(n) for n in (
        "L0_attn_bq", "L0_attn_bk", "L0_attn_bv", "L0_attn_convq_b", "L0_attn_convk_b", "L0_attn_D_skip", "L0_ffn_ln1_w",
        "L0_ffn_ln2_w", "L0_attn_convq_w", "L0_attn_convk_w")], 1)
    a["bo"] = np.ascontiguousarray(np.broadcast_to(x["L0_attn_bo"], (P, D)))
    a["ssm"] = transposed("L0_attn_ssm_kernel")
    for n in "qkvo":
        a[f"a_w{n}"] = transposed(f"L0_attn_W{n}")
        a[f"d_w{n}"] = transposed(f"L1_attn_W{n}")
    for n in "qkv":
        a[f"b_w{n}"] = transposed(f"L0_ffn_W{n}")
    for n in "qk":
        a[f"b_w{n}"] = np.ascontiguousarray(a[f"b_w{n}"].reshape(P, KT, KT, HEADS // KT, HD).swapaxes(3, 4).reshape(P, KT, D))
    a["b_wo"], a["b_a"], a["b_b"] = tiles(x["L0_ffn_Wo"]), tiles(x["L0_ffn_A"]), x["L0_ffn_B"]
    a["w_in"], a["w_up"], a["w_down"] = (transposed(f"L0_ffn_W_{n}") for n in ("in_base", "up_base", "down"))
    a["gate_w"] = transposed("L1_ffn_gate_w")
    a["sh_gu"] = transposed("L1_ffn_shared_gate_up")
    a["sh_dn"] = np.ascontiguousarray(x["L1_ffn_shared_down"].T)
    a["e_w1"] = np.ascontiguousarray(x["L1_ffn_experts_w1"].swapaxes(1, 2).reshape(E_N, KT, P, I_N).swapaxes(1, 2))
    a["e_w2"] = np.ascontiguousarray(x["L1_ffn_experts_w2"].swapaxes(1, 2).reshape(E_N, 2, IH, D).swapaxes(1, 2))
    return a


def kernel(**inputs):
    import concourse.bacc as bacc
    from concourse.bass_utils import run_bass_kernel_spmd

    arrays = {n: np.ascontiguousarray(a) for n, a in layouts({n: np.asarray(v) for n, v in inputs.items()}).items()}
    arrays.update(constants())
    nc = bacc.Bacc("TRN2", target_bir_lowering=False, num_devices=1)
    d = {n: nc.dram_tensor(f"in_{n}", a.shape, mybir.dt.from_np(a.dtype), kind="ExternalInput").ap() for n, a in arrays.items()}
    d["out"] = nc.dram_tensor("out", (NB, L, D), F32, kind="ExternalOutput").ap()
    build(nc, d)
    r = run_bass_kernel_spmd(nc, [{f"in_{n}": a for n, a in arrays.items()}], core_ids=[0])
    return r.results[0]["out"]
```

```python
from contextlib import ExitStack

import numpy as np

import concourse.bass as bass
from concourse import mybir

P = 128
NB, L, D = 8, 256, 256
KT = D // P
TT = L // P
NT = NB * TT
HEADS, HD = 16, 16
PAIR = 2 * HD
GROUPS = P // PAIR
F_MLP = 1024
FT = F_MLP // P
R_MOD = 16
MOD_SCALE = 0.1
E_N, I_N, TOPK = 64, 176, 6
IH = I_N // 2
SH_I = 2 * I_N
SH_TILES = [(0, 128), (128, 128), (256, SH_I - 256)]
PAIRS = NB * L * TOPK
CHUNKS = E_N + (PAIRS - E_N) // P
CAP = P + NB * L
SPARE = CHUNKS - PAIRS // P
X_ROWS = E_N * CAP + (SPARE + 1) * P
XW = D + 8
Y_ROWS = PAIRS + (E_N + SPARE + 1) * P
NFFT = 2 * L
FREQ_TILES = L // P
RING = 6
YG = 4
HEAD = 9
LN_EPS, RMS_EPS = 1e-5, 1e-6
NEG = -1e38
ROUND = 8388608.0

F32, BF16 = mybir.dt.float32, mybir.dt.bfloat16
I32, U32 = mybir.dt.int32, mybir.dt.uint32
ALU = mybir.AluOpType
ACT = mybir.ActivationFunctionType
AX = mybir.AxisListType.X

VEC = {"bq": 0, "bk": 2, "bv": 4, "cqb": 6, "ckb": 8, "skip": 10, "ln1": 12, "ln2": 14, "cqw": 16, "ckw": 22}
VEC_N = 28
CST = {"ident": 0, "iota": 128, "region": 192, "parts": 256, "chunk": 259, "token": 261}
CST_N = 261 + TT
CSB = {"ident": 0, "ones": 128, "before": 256, "open": 384, "causal": 512}
CSB_N = 640


def constants():
    p = np.arange(P)
    c = np.zeros((P, CST_N), np.float32)
    c[:, 0:128] = np.eye(P)
    c[:, 128:192] = np.arange(E_N)
    c[:, 192:256] = np.arange(E_N) * CAP + P
    for n, groups in enumerate(((0, 4, 6), (1, 5, 7), (2,))):
        c[:, 256 + n] = np.isin(p // R_MOD, groups)
    c[:, 259] = 2 * p
    c[:, 260] = 2 * p + 1
    c[:, 261:] = (np.arange(TT) * P + p[:, None]) * TOPK
    blank = np.full((E_N + SPARE + 1, P, XW - D), -1, np.float32)
    blank[:, :, 0] = PAIRS + np.arange((E_N + SPARE + 1) * P).reshape(-1, P)
    b = np.zeros((P, CSB_N), np.float32)
    b[:, 0:128] = np.eye(P)
    b[:, 128:256] = 1
    b[:, 256:384] = p[:, None] < p[None, :]
    tri = np.where(p[None, :] <= p[:, None], 0, NEG)
    b[:, 512:640] = tri
    t = np.arange(L)[:, None]
    f = np.arange(L)[None, :]
    w = 2 * np.pi * ((t * f) % NFFT) / NFFT
    re, im = np.cos(w), -np.sin(w)
    sign = 1.0 - 2.0 * (np.arange(L) % 2)
    im_packed = im.copy()
    im_packed[:, 0] = sign
    re_nyq = re[:, :P].copy()
    re_nyq[:, 0] = sign
    fwd = np.concatenate([re, im_packed, im[:, :P], re_nyq], 1)
    fwd = fwd.reshape(KT, P, 6 * P).transpose(1, 0, 2)
    weight = np.where(np.arange(L) == 0, 1.0, 2.0)[:, None] / NFFT
    ire = weight * re.T
    iim = weight * im.T
    iim[0] = sign / NFFT
    inv = np.concatenate([ire, iim], 0).reshape(2 * FREQ_TILES, P, L).transpose(1, 0, 2)
    return {
        "blank": blank, "cst": c, "csb": b.astype(mybir.dt.np(BF16)),
        "fwd": np.ascontiguousarray(fwd, np.float32), "inv": np.ascontiguousarray(inv, np.float32),
    }


def build(nc, d):
    x_rows = nc.dram_tensor("x_rows", (X_ROWS, XW), F32, kind="Internal").ap()
    q_parts = nc.dram_tensor("q_parts", (3, P, KT * L), BF16, kind="Internal").ap()
    k_parts = nc.dram_tensor("k_parts", (5, P, KT * L), BF16, kind="Internal").ap()
    y_rows = nc.dram_tensor("y_rows", (Y_ROWS, D), F32, kind="Internal").ap()

    with ExitStack() as ctx:
        def sb(name, shape, dt=F32):
            return ctx.enter_context(nc.sbuf_tensor(name, shape, dt))

        def sem(name):
            return ctx.enter_context(nc.semaphore(name))

        bank = ctx.enter_context(nc.psum_tensor("bank", [P, 8, 512], F32))

        cst, csb = sb("cst", [P, CST_N]), sb("csb", [P, CSB_N], BF16)
        ident, iota, region = cst[:, 0:128], cst[:, 128:192], cst[:, 192:256]
        part_of, chunk_no, token_row = cst[:, 256:259], cst[:, 259:261], cst[:, 261:]
        identb, onesb, beforeb = csb[:, 0:128], csb[:, 128:256], csb[:, 256:384]
        masks = [csb[:, 640 - w:640].rearrange("p (o k) -> p o k", o=1).broadcast_to([P, 4 * P // w, w]) for w in (P, L)]
        vec = sb("vec", [P, VEC_N])
        fwd, inv = sb("fwd", [P, KT, 6 * P]), sb("inv", [P, 2 * FREQ_TILES, L])
        ssm = sb("ssm", [P, KT, D])
        a_w = {n: sb(f"a_w{n}", [P, KT, D]) for n in "qkvo"}
        bo = sb("bo", [P, D])
        b_w = {n: sb(f"b_w{n}", [P, KT, D]) for n in "qkv"}
        b_wo = sb("b_wo", [P, KT, D])
        b_a = sb("b_a", [P, KT, P])
        w_in, w_up = sb("w_in", [P, KT, F_MLP]), sb("w_up", [P, KT, F_MLP])
        w_down = sb("w_down", [P, FT, D])
        d_w = {n: sb(f"d_w{n}", [P, KT, D]) for n in "qkvo"}
        gate_w = sb("gate_w", [P, KT, E_N])
        sh_gu = sb("sh_gu", [P, KT, 2 * SH_I])
        sh_dn = sb("sh_dn", [P, len(SH_TILES), D])

        X = sb("X", [P, NT, D])
        TOPW = sb("TOPW", [P, NT, TOPK])

        uT = sb("uT", [P, KT, L])
        q_sb, k_sb = sb("q_sb", [P, KT, L + 2]), sb("k_sb", [P, KT, L + 2])
        v_sb, qc, kc = sb("v_sb", [P, KT, L]), sb("qc", [P, KT, L]), sb("kc", [P, KT, L])
        kv, kvT = sb("kv", [P, KT, L]), sb("kvT", [P, TT, D])
        tabA, tabB, tabD = (sb(n, [P, FREQ_TILES, D]) for n in ("tabA", "tabB", "tabD"))
        products = sb("products", [P, 4, FREQ_TILES, D])
        pr = [products[:, n] for n in range(4)]
        Yre, Yim = pr[0], pr[2]
        z = sb("z", [P, KT, L])
        xn = sb("xn", [P, TT, D])
        d_kv = sb("d_kv", [P, KT, L])
        nrm = {}
        att = sb("att", [P, TT, D])
        for s, r in (("A", qc), ("B", att), ("D", d_kv), ("R", None), ("F", qc)):
            nrm[s] = dict(r=r, st=sb(f"st{s}", [P, TT, 6]), mv=sb(f"mv{s}", [P, TT, 2]), v=sb(f"v{s}", [P, TT]),
                          y=sb(f"y{s}", [P, TT]), var=f"n_var{s}", inv=f"n_inv{s}")
        minus_half = sb("minus_half", [P, TT])
        ms = sb("ms", [P, TT])
        h1T, h2T = sb("h1T", [P, KT, L]), sb("h2T", [P, KT, L])
        xnT = kc
        part = {n: products[:, 2 * i:2 * i + 2].rearrange("p n f d -> p (n f d)").bitcast(BF16)[:, 0:3 * KT * L]
                .rearrange("p (n k l) -> p n k l", n=3, k=KT) for i, n in enumerate("qk")}
        rest = {"q": z, "k": kvT}
        stack = {n: sb(f"stack_{n}", [P, HEADS // KT, KT, L], BF16) for n in "qk"}
        v1 = sb("v1", [P, TT, HEADS, HD + 1])
        UNITS = GROUPS + 2 * GROUPS
        nmx = sb("nmx", [P, UNITS, 4])
        prob, probT = sb("prob", [P, 2, 512]), sb("probT", [P, 2, 4, P])
        rec = sb("rec", [P, TT, HEADS])
        attT = sb("attT", [P, KT, L])
        woa = sb("woa", [P, KT, P])
        th, mh = sb("th", [P, L]), sb("mh", [P, L])
        b_stack, m_stack = sb("b_stack", [P, F_MLP], BF16), sb("m_stack", [P, L], BF16)
        gt, gs = sb("gt", [P, 2, L]), sb("gs", [P, 2, L])
        actT = sb("actT", [P, FT, L])
        b_b, b_rest = (actT[:, n * FT // 2:(n + 1) * FT // 2, :].rearrange("p a b -> p (a b)") for n in range(2))
        b_part = [t[:].rearrange("p a b -> p (a b)").bitcast(BF16)[:, 0:F_MLP] for t in (gt, gs, prob)]
        x2, x2T = sb("x2", [P, TT, D]), sb("x2T", [P, KT, L])
        d_k, d_cs, vh = (sb(n, [P, KT, L]) for n in ("d_k", "d_cs", "vh"))
        ones_row = sb("ones_row", [P, L])
        x3_row, x3T = sb("x3_row", [P, TT, XW]), sb("x3T", [P, KT, L])
        x3, x3_meta = x3_row[:, :, 0:D], x3_row[:, :, D:XW]
        lg8, nlg = sb("lg8", [P, TT, 8]), sb("nlg", [P, TT])
        ex, top8, top8i = sb("ex", [P, TT, E_N]), sb("top8", [P, TT, 8]), sb("top8i", [P, TT, 8], U32)
        idxf, wsum, wrec = sb("idxf", [P, TT, 8]), sb("wsum", [P, TT]), sb("wrec", [P, TT])
        mk, mkb = sb("mk", [P, TT, E_N]), sb("mkb", [P, TT, E_N], BF16)
        seen = sb("seen", [P, E_N], BF16)
        pos, hit = sb("pos", [P, TT, E_N]), sb("hit", [P, TT, TOPK, E_N])
        destf, desti = sb("destf", [P, TT, TOPK]), sb("desti", [P, TT * TOPK], I32)
        sgt, sgs, sact = sb("sgt", [P, L]), sb("sgs", [P, L]), sb("sact", [P, len(SH_TILES), L])
        zeros = sb("zeros", [P, D])
        spare = sb("spare", [P, 2])
        cn, cum, pad_e = sb("cn", [P, E_N]), sb("cum", [P, E_N]), sb("pad_e", [P, E_N])
        ce, cb, co, crow = (sb(n, [P, 2]) for n in ("ce", "cb", "co", "crow"))
        ctab, table = sb("ctab", [P, 4]), gs[0:1].rearrange("p a b -> p (a b)").bitcast(I32)
        scr = h1T[:].rearrange("p a b -> p (a b)")[:, 0:3 * E_N].rearrange("p (n e) -> p n e", n=3)
        dead = [[t[:].rearrange("p a b -> p (a b)"), 0] for t in (w_in, w_up, w_down, fwd, inv, sh_gu, ssm, a_w["q"], a_w["k"], a_w["v"])]

        def again(rows, a, b):
            for t in dead:
                if t[1] + a * b <= t[0].shape[1]:
                    at, t[1] = t[1], t[1] + a * b
                    return t[0][0:rows, at:at + a * b].rearrange("p (a b) -> p a b", a=a)

        def ring(n, *shape):
            return [again(*shape) for _ in range(n)]

        w2, w1 = ring(RING, IH, 2, D), ring(RING, P, KT, I_N)
        xc_row = ring(RING, P, 1, XW)
        xc_row = [t[:, 0, :] for t in xc_row]
        xcT, hs = ring(3, P, KT, P), ring(3, IH, 2, P)
        yc, outb = ring(RING, P, 1, D), ring(YG, P, 1, D)
        yc, outb = [t[:, 0, :] for t in yc], [t[:, 0, :] for t in outb]

        yg = [t[:].rearrange("p a b -> p (a b)")[:, 0:TOPK * D].rearrange("p (k d) -> p k d", k=TOPK) for t in (w_in, w_up, actT)]
        yg.append(products[:].rearrange("p n f d -> p (n f) d")[:, 0:TOPK, :])
        ON_PE = TOPK - 1
        diag = [stack[n][:].rearrange("p h k l -> p (h k l)").bitcast(F32)[:, t * ON_PE * P:(t + 1) * ON_PE * P]
                .rearrange("p (k c) -> p k c", k=ON_PE) for n in "qk" for t in range(2)]
        ids = [sb(f"ids{n}", [P, 1], I32) for n in range(RING)]
        choice = [sb(f"choice{n}", [P, 1]) for n in range(RING)]
        found = [sb(f"found{n}", [P, TOPK]) for n in range(RING)]
        spot = sb("spot", [P, TT, P], BF16)
        expert_of = gt[:, 0, :]

        S = {n: sem(n) for n in (
            "ld_vec ld_mlp p_spare n_varA n_varB n_varD n_varR n_invA n_invB n_invD n_invR ld_u ld_uT ld_cst ld_a ld_ssm ld_b ld_d set_pool set_dve set_pe set_woa ub "
            "a_q a_k a_v a_q_out a_k_out a_v_out a_qc a_kc a_kv a_kvT a_kvT_out a_X a_pr a_Y a_y a_z a_zq a_o a_r a_x1 "
            "b_xn b_hT b_h1 b_h2 b_xT b_q b_k b_v b_first b_rest b_second b_third st_qw st_kw st_q st_k b_v_out b_s b_max b_exp b_pT b_pT_out b_pv b_att "
            "b_attT b_attT_out b_mod b_tanh b_mh b_gu b_gt b_act b_dn b_r b_x2 "
            "d_xT d_xT_out d_q d_k_ps d_v d_k_out d_kv d_vh d_o d_r d_x3 d_x3T d_x3T_out d_lg d_max d_ex d_mask "
            "d_rank d_pos d_dest d_scat d_sg d_sgt d_sact d_sd d_base "
            "ch_a ch_b ch_d ch_r ch_f r_tot r_tab r_row r_table r_fill "
            "m_w0 m_x0 m_w1 m_x1 m_w2 m_x2 m_w3 m_x3 m_w4 m_x4 m_w5 m_x5 m_ids ch_m r_spot r_all m_xT m_xT_out m_h m_hs m_y m_y_out m_st0 m_st1 m_st2 m_st3 m_st4 m_st5 "
            "f_ld0 f_ld1 f_ld2 f_ld3 f_st0 f_st1   f_diag f_sum f_r f_out n_varF n_invF").split()}

        def need(eng, name, value):
            if isinstance(value, int) and value <= 0:
                return
            eng.wait_ge(S[name], value)

        def first(b):
            return isinstance(b, int) and b == 0

        def alone(eng):
            if eng.engine == nc.vector.engine:
                eng.memset(spare[:, 0:1], 0.0)
            else:
                eng.tensor_tensor(spare[:, 1:2], ones_row[:, 0:1], ones_row[:, 1:2], ALU.mult).then_inc(S["p_spare"], 1)

        class Chain:

            def __init__(self, eng, name, per):
                self.eng, self.name, self.per, self.k, self.b = eng, name, per, 0, 0

            def start(self, b):
                self.b, self.k = b, 0

            def step(self, ins):
                self.k += 1
                ins.then_inc(S[self.name], 1)

            def wait(self):
                self.eng.wait_ge(S[self.name], self.b * self.per + self.k)

            def link(self, ins):
                self.step(ins)
                self.wait()

        TURN = """A1 A1b D1 A1q u0 D2k A1k u1 D2x A2 u2 D2v A3a u3 A3b u4 A3p D2q D2w u5 t0 D3 u6 D3n A4a u7 D3o D4 A4b A4z
            u8 S0 u9 A5 u10 A5n D4l S1 u11 A5o D4m S2 A6n u12 SDa u13 t1 A6o D4t SDb SD B6a B6c B6b C1 f0 D4k f1 C2 f2 D5 f3 D5p C2v
            f4 D4w D5h f5 f6 f7 C2h B8 D6""".split()
        SECOND = """A1 A1b A1q A1k A2 A3a u0 A3b u1 A3p u2 u3 A4a u4 A4b A4z u5 t0 u6 A5 u7 A5n u8 A5o u9 A6n u10 A6o u11 u12 u13 t1
            B6a B6c B6b C1 f0 f1 C2 f2 f3 C2v f4 f5 f6 f7 C2h B8""".split()
        LAST_BUT_ONE = """u0 D1 u1 D2k u2 D2x u3 D2v D2q u4 D2w u5 t0 D3 u6 D3n u7 D3o D4 u8 S0 u9 D4l S1 u10 D4m S2 u11 SDa u12 D4t
            u13 t1 SDb SD B6a B6c B6b f0 D4k f1 f2 D5 f3 D5p f4 D4w D5h f5 f6 f7 B8 D6""".split()
        LAST = "D1 D2k D2x D2v D2q D2w D3 D3n D3o D4 D4l D4m D4t D4k D5 D5p D5h D6 DTa S0 DTb S1 S2 D4w SDa SDb SD".split()
        LAG = {"A": 0, "C": 0, "B": 1, "D": 2}
        STAGE = {"u": "B", "t": "B", "f": "B", "S": "D"}

        def turns(eng, parts):
            def turn(it, order=TURN):
                for name in order:
                    b = it - LAG[STAGE.get(name[0], name[0])]
                    if isinstance(b, int) and not 0 <= b < NB:
                        continue
                    if name in parts:
                        parts[name](b)
            turn(0)
            turn(1, SECOND)
            turn(2)
            with eng.Fori(3, NB) as it:
                turn(it)
            turn(NB, LAST_BUT_ONE)
            turn(NB + 1, LAST)

        class Chunk:
            turn = RING

            def __init__(self, i, off):
                self.i, self.off, self.no = i, off, i * self.turn + off

            def slot(self, n):
                return self.off % n

            def before(self, n):
                return self.i * (self.turn // n) + self.off // n

        class Tile(Chunk):
            turn = YG

        def chunk_values(eng, c):
            at = slice(2 * c.no, 2 * c.no + 2) if isinstance(c.no, int) else bass.ds(c.no * 2, 2)
            why = "the table was clamped where it was worked out"
            e, row = nc.values_load_multi_w_load_instructions(table[0:1, at], engines=(eng.engine,), min_val=0,
                                                              max_val=X_ROWS - P, skip_runtime_bounds_check_because=why)[1]
            return nc.s_assert_within(e, 0, E_N - 1, skip_runtime_bounds_check_because=why), row

        def chunk_loop(eng, skewed):
            def step(i, off):
                for lag, work in enumerate(skewed):
                    c = Chunk(i, off - lag)
                    if work and (not isinstance(c.no, int) or 0 <= c.no < CHUNKS):
                        work(c)

            def body(i):
                for off in range(HEAD, HEAD + RING):
                    step(i, off)

            turns_in_all = (CHUNKS - HEAD) // RING
            assert HEAD + turns_in_all * RING == CHUNKS
            for off in range(HEAD):
                step(0, off)
            with eng.Fori(0, turns_in_all) as i:
                body(i)
            for off in range(CHUNKS, CHUNKS + len(skewed) - 1):
                step(0, off)

        def tile_loop(eng, skewed):
            def step(i, off):
                for lag, work in enumerate(skewed):
                    c = Tile(i, off - lag)
                    if work and (not isinstance(c.no, int) or 0 <= c.no < NT):
                        work(c)
            for off in range(YG):
                step(0, off)
            with eng.Fori(0, NT // YG - 1) as i:
                for off in range(YG, 2 * YG):
                    step(i, off)
            for off in range(NT, NT + len(skewed) - 1):
                step(0, off)

        def tile_of(t, n):
            return t[:, n, :] if isinstance(n, int) else t[:, bass.ds(n, 1), :].rearrange("p o d -> p (o d)")

        def unit_heads(u):
            if u < GROUPS:
                return [(u, eh, par) for eh in range(KT) for par in range(2)]
            return [((u - GROUPS) // KT, (u - GROUPS) % KT, par) for par in range(2)]

        block = ctx.enter_context(nc.Block())

        def psum(n, a=0, b=512):
            return bank[:, n, a:b]

        def psum3(n):
            return bank[:, n, :].rearrange("p (a b) -> p a b", a=2)

        @block.sync
        def _(sp):
            sp.dma_start(uT[:], d["uT"][0]).then_inc(S["ld_uT"], 16)
            for n in "qkv":
                sp.dma_start(a_w[n][:], d[f"a_w{n}"]).then_inc(S["ld_a"], 16)
            sp.dma_start(fwd[:], d["fwd"]).then_inc(S["ld_ssm"], 16)
            sp.dma_start(ssm[:], d["ssm"]).then_inc(S["ld_ssm"], 16)
            sp.dma_start(inv[:], d["inv"]).then_inc(S["ld_ssm"], 16)
            sp.dma_start(a_w["o"][:], d["a_wo"]).then_inc(S["ld_ssm"], 16)
            for t, n in ((b_wo, "b_wo"), (b_a, "b_a"), (b_b, "b_b"), *((b_w[n], f"b_w{n}") for n in "qkv")):
                sp.dma_start(t if n == "b_b" else t[:], d[n]).then_inc(S["ld_b"], 16)
            for t, n in ((w_in, "w_in"), (w_up, "w_up"), (w_down, "w_down")):
                sp.dma_start(t[:], d[n]).then_inc(S["ld_mlp"], 16)
            for n in "qkvo":
                sp.dma_start(d_w[n][:], d[f"d_w{n}"]).then_inc(S["ld_d"], 16)
            sp.dma_start(gate_w[:], d["gate_w"]).then_inc(S["ld_d"], 16)
            sp.dma_start(sh_gu[:], d["sh_gu"]).then_inc(S["ld_d"], 16)
            sp.dma_start(sh_dn[:, 0:2, :], d["sh_dn"][0:256].rearrange("(k p) n -> p k n", p=P)).then_inc(S["ld_d"], 16)
            sp.dma_start(sh_dn[0:SH_I - 256, 2, :], d["sh_dn"][256:SH_I]).then_inc(S["ld_d"], 16)

            def next_uT(b):
                sp.wait_ge(S["a_v"], b)
                n = slice(b, b + 1) if isinstance(b, int) else bass.ds(b, 1)
                sp.dma_start(uT[:], d["uT"][n].rearrange("o p k l -> p (o k) l")).then_inc(S["ld_uT"], 16)

            def stack_up(b):
                def rows(t, a, z):
                    return t[a:z].rearrange("n (e h) c -> (n e) (h c)", e=HD)

                def value(v):
                    return v if isinstance(v, int) else sp.snap(v)

                last = isinstance(b, int) and b == NB - 1
                following = None if last else value(b + 1)
                queries, keys = value(b * 2 + 1), value(b * 2 + 2)
                left = {"q": value(b * 16 + 16), "k": value(b * 32 + 32)}
                if not last:
                    next_uT(following)
                need(sp, "b_third", queries)
                sp.dma_start(q_parts.rearrange("n p c -> p n c"), part["q"].rearrange("p n k l -> p n (k l)")).then_inc(S["st_qw"], 16)
                need(sp, "b_third", keys)
                for a, n in ((0, 3), (3, 2)):
                    sp.dma_start(k_parts[a:a + n].rearrange("n p c -> p n c"), part["k"][:, 0:n].rearrange("p n k l -> p n (k l)")
                                 ).then_inc(S["st_kw"], 16)
                for n, t, first_parts in (("q", q_parts, (0, 0, 0)), ("k", k_parts, (1, 2, 0))):
                    need(sp, f"st_{n}w", left[n])
                    for j, a in enumerate(first_parts):
                        parts = 3 if j < 2 else 2
                        sp.dma_start(stack[n][j * 3 * HD:(j * 3 + parts) * HD].rearrange("p h k l -> p (h k l)"),
                                     rows(t, a, a + parts)).then_inc(S[f"st_{n}"], 16)

            stack_up(0)
            sp.wait_ge(S["set_pool"], 1)
            def blank(rows, at, n):
                sp.dma_start(rows[:, :, 0:D], zeros[:].rearrange("p (o d) -> p o d", o=1).broadcast_to([P, n, D])
                             ).then_inc(S["r_fill"], 16)
                sp.dma_start(rows[:, :, D:XW], d["blank"][at:at + n].rearrange("n p w -> p n w")).then_inc(S["r_fill"], 16)

            blank(x_rows[0:E_N * CAP].rearrange("(e c) d -> c e d", c=CAP)[0:P], 0, E_N)
            blank(x_rows[E_N * CAP:].rearrange("(n p) d -> p n d", p=P), E_N, SPARE + 1)
            with sp.Fori(1, NB - 1) as b:
                stack_up(b)
            stack_up(NB - 1)
            sp.wait_ge(S["r_table"], 1)

            def load(c):
                s = c.slot(RING)
                e, row = chunk_values(sp, c)
                if first(c.no):
                    sp.wait_ge(S["d_scat"], 16 * TT * TOPK * NB)
                need(sp, "m_xT", c.no - (RING - 1))
                need(sp, "m_ids", c.no - (RING - 1))
                sp.dma_start(xc_row[s], x_rows[bass.ds(row, P), :]).then_inc(S[f"m_x{s}"], 16)
                need(sp, "m_h", c.no - (RING - 1))
                sp.dma_start(w1[s], d["e_w1"][bass.ds(e, 1)].rearrange("o p k i -> p (o k) i")).then_inc(S[f"m_w{s}"], 16)

            chunk_loop(sp, [load])

        @block.gpsimd
        def _(pool):
            for t in (q_sb, k_sb):
                pool.memset(t[:, :, 0:2], 0.0)
            pool.memset(v1[:, :, :, HD:HD + 1], 1.0)
            pool.memset(ones_row[:], 1.0)
            pool.memset(minus_half[:], -0.5)
            pool.memset(seen[:], 0.0)
            pool.memset(zeros[:], 0.0).then_inc(S["set_pool"], 1)
            pool.wait_ge(S["ld_vec"], 16)

            def A3(b):
                pool.wait_ge(S["a_pr"], b + 1)
                pool.tensor_tensor(Yre, pr[0], pr[1], ALU.subtract)
                pool.tensor_tensor(Yim, pr[2], pr[3], ALU.add).then_inc(S["a_Y"], 1)
                if first(b):
                    pool.wait_ge(S["ld_u"], 32)
                    pool.tensor_tensor(X[:], X[:], bo[:].rearrange("p (o n) -> p o n", o=1).broadcast_to([P, NT, D]),
                                       ALU.add).then_inc(S["ub"], 1)

            def inverse_root(which):
                m = nrm[which]
                def part(b):
                    pool.wait_ge(S[m["var"]], b + 1)
                    pool.tensor_tensor(m["y"][:], m["v"][:], minus_half[:], ALU.pow).then_inc(S[m["inv"]], 1)
                return part

            def C2v(b):
                for i, n in enumerate("qk"):
                    pool.wait_ge(S["b_second"], b * 2 + i + 1)
                    pool.tensor_tensor(part[n][:, 2], rest[n][:], part[n][:, 1], ALU.subtract).then_inc(S["b_third"], 1)

            def C2h(b):
                pool.wait_ge(S["b_xT"], b + 1)
                need(pool, "b_gu", b * FT)
                at = VEC["ln2"]
                pool.tensor_tensor(h2T[:], xnT[:], vec[:, at:at + KT].rearrange("p (k o) -> p k o", o=1).broadcast_to([P, KT, L]),
                                   ALU.mult).then_inc(S["b_h2"], 1)

            def D6(b):
                need(pool, "p_spare", b)
                if first(b):
                    pool.wait_ge(S["r_fill"], 64)
                pool.wait_ge(S["d_dest"], b + 1)
                alone(pool)
                for tt in range(TT):
                    for k in range(TOPK):
                        n = tt * TOPK + k
                        pool.indirect_dma_start(x_rows, bass.IndirectOffsetOnAxis(ap=desti[:, n:n + 1].bitcast(U32), axis=0),
                                                x3_row[:, tt, :], None).then_inc(S["d_scat"], 16)

            turns(pool, {"A3p": A3, "C2v": C2v, "C2h": C2h, "D6": D6, "D3n": inverse_root("D"), "A5n": inverse_root("A"), "A6n": inverse_root("R"),
                         "B8": inverse_root("B")})

            def spread(c):
                s = c.slot(RING)
                need(pool, "p_spare", c.no + NB)
                pool.wait_ge(S["m_ids"], c.no + 1)
                pool.wait_ge(S["m_y_out"], c.no + 1)
                alone(pool)
                pool.indirect_dma_start(y_rows, bass.IndirectOffsetOnAxis(ap=ids[s][:].bitcast(U32), axis=0), yc[s], None
                                        ).then_inc(S[f"m_st{s}"], 16)

            chunk_loop(pool, [None, None, None, spread])

            def root(c):
                h = c.slot(2)
                pool.wait_ge(S["n_varF"], c.no + 1)
                pool.tensor_tensor(nrm["F"]["y"][:, h:h + 1], nrm["F"]["v"][:, h:h + 1], minus_half[:, 0:1], ALU.pow
                                   ).then_inc(S["n_invF"], 1)

            tile_loop(pool, [root])

        @block.tensor
        def _(pe):
            def project(out, w, x):
                for eh in range(KT):
                    for kt in range(KT):
                        mm = pe.matmul(out[:, eh * L:(eh + 1) * L], w[:, kt, eh * P:(eh + 1) * P], x[:, kt, :],
                                       start=(kt == 0), stop=(kt == KT - 1))
                return mm

            def by_token(out, x, w):
                for tt in range(TT):
                    for kt in range(KT):
                        mm = pe.matmul(out[:, tt * D:(tt + 1) * D], x[:, kt, tt * P:(tt + 1) * P], w[:, kt, :],
                                       start=(kt == 0), stop=(kt == KT - 1))
                return mm

            def turn(out, x):
                return pe.transpose(out, x, ident)

            def turn_tiles(out, x):
                for a in range(2):
                    for b in range(2):
                        t = turn(out[:, b * 256 + a * P:b * 256 + (a + 1) * P], x[:, a, b * P:(b + 1) * P])
                return t

            def A1(b):
                pe.wait_ge(S["ld_uT"], b * 16 + 16)
                if first(b):
                    pe.wait_ge(S["ld_a"], 48)
                need(pe, "b_v_out", b)
                project(psum(4), a_w["q"], uT).then_inc(S["a_q"], 1)

            def A1b(b):
                need(pe, "b_rest", b * 2)
                project(psum(5), a_w["k"], uT).then_inc(S["a_k"], 1)
                pe.wait_ge(S["a_q_out"], b + 1)
                project(psum(4), a_w["v"], uT).then_inc(S["a_v"], 1)

            def A2(b):
                if first(b):
                    pe.wait_ge(S["ld_cst"], 32)
                    pe.wait_ge(S["ld_ssm"], 64)
                    for n, tile0, tile1 in ((0, 0, 1), (1, 4, 3), (2, 5, 1)):
                        for ft, m in enumerate((tile0, tile1)):
                            for kt in range(KT):
                                mm = pe.matmul(psum(n, ft * D, (ft + 1) * D), fwd[:, kt, m * P:(m + 1) * P], ssm[:, kt, :],
                                               start=(kt == 0), stop=(kt == KT - 1))
                        mm.then_inc(S["set_pe"], 1)
                pe.wait_ge(S["a_kv"], b + 1)
                pe.wait_ge(S["a_k_out"], b + 1)
                turn_tiles(psum(5), kv).then_inc(S["a_kvT"], 1)

            def forward(part):
                def A3(b):
                    if part == 0:
                        pe.wait_ge(S["a_kvT_out"], b + 1)
                        pe.wait_ge(S["a_v_out"], b + 1)
                    for n in range(part * FREQ_TILES, (part + 1) * FREQ_TILES):
                        for kt in range(KT):
                            mm = pe.matmul(psum(4 + part, (n % 2) * D, (n % 2 + 1) * D), fwd[:, kt, n * P:(n + 1) * P],
                                           kvT[:, kt, :], start=(kt == 0), stop=(kt == KT - 1))
                    mm.then_inc(S["a_X"], 1)
                return A3

            def inverse(dh):
                def A4(b):
                    if dh == 0:
                        pe.wait_ge(S["a_Y"], b + 1)
                    for n in range(2 * FREQ_TILES):
                        y = Yre if n < FREQ_TILES else Yim
                        mm = pe.matmul(psum(4, dh * L, (dh + 1) * L), y[:, n % FREQ_TILES, dh * P:(dh + 1) * P],
                                       inv[:, n, :], start=(n == 0), stop=(n == 2 * FREQ_TILES - 1))
                    mm.then_inc(S["a_y"], 1)
                return A4

            def A5(b):
                pe.wait_ge(S["a_zq"], b + 1)
                by_token(psum(5), z, a_w["o"]).then_inc(S["a_o"], 1)

            def C1(b):
                if first(b):
                    pe.wait_ge(S["ld_b"], 96)
                    for eh in range(KT):
                        for kt in range(KT):
                            mm = pe.matmul(psum(1, eh * P, (eh + 1) * P), b_wo[:, kt, eh * P:(eh + 1) * P],
                                           b_a[:, kt, :], start=(kt == 0), stop=(kt == KT - 1))
                    mm.then_inc(S["set_woa"], 1)
                    pe.wait_ge(S["set_dve"], 9)
                pe.wait_ge(S["b_xn"], b + 1)
                pe.wait_ge(S["a_r"], b + 1)
                turn_tiles(psum(5), xn).then_inc(S["b_hT"], 1)

            def C2(b):
                pe.wait_ge(S["b_h1"], b + 1)
                pe.wait_ge(S["a_z"], b + 1)
                project(psum(4), b_w["q"], h1T).then_inc(S["b_q"], 1)
                pe.wait_ge(S["b_xT"], b + 1)
                project(psum(5), b_w["k"], h1T).then_inc(S["b_k"], 1)

            def C2v(b):
                pe.wait_ge(S["b_rest"], b * 2 + 1)
                by_token(psum(4), h1T, b_w["v"]).then_inc(S["b_v"], 1)

            def scores(b, u):
                if u == 0:
                    need(pe, "b_act", b * FT)
                    pe.wait_ge(S["st_q"], (b + 1) * 48)
                    pe.wait_ge(S["st_k"], (b + 1) * 48)
                if u == 1:
                    need(pe, "b_r", b)
                if u >= 2:
                    need(pe, "b_exp", b * UNITS + u - 1)
                n = u % 2
                w = P if u < GROUPS else L
                pe.matmul(bank[:, n, :].rearrange("p (h k) -> p h k", k=w), identb, masks[u >= GROUPS], start=True, stop=False,
                          skip_group_check=True)
                for h, (g, eh, par) in enumerate(unit_heads(u)):
                    mm = pe.matmul(psum(n, h * w, (h + 1) * w), stack["q"][:, 2 * g + par, eh, w - P:w],
                                   stack["k"][:, 2 * g + par, eh, 0:w], start=False, stop=True, skip_group_check=True)
                mm.then_inc(S["b_s"], 1)

            def turn_probs(b, u):
                pe.wait_ge(S["b_exp"], b * UNITS + u + 1)
                if u:
                    need(pe, "b_pT_out", b * UNITS + u)
                for j in range(4):
                    t = turn(psum(2, j * P, (j + 1) * P), prob[:, u % 2, j * P:(j + 1) * P])
                t.then_inc(S["b_pT"], 1)

            def values(b, u):
                pe.wait_ge(S["b_pT_out"], b * UNITS + u + 1)
                if u == 0:
                    pe.wait_ge(S["b_v_out"], b + 1)
                if u == GROUPS:
                    pe.wait_ge(S["b_att"], b * 2 + 1)
                for h, (g, eh, par) in enumerate(unit_heads(u)):
                    head = eh * 8 + 2 * g + par
                    out = psum(3, head * (HD + 1), (head + 1) * (HD + 1))
                    if u < GROUPS:
                        mm = pe.matmul(out, probT[:, u % 2, h, :], v1[:, 0, head, :], start=True, stop=True)
                    else:
                        for kt in range(TT):
                            mm = pe.matmul(out, probT[:, u % 2, 2 * h + kt, :], v1[:, kt, head, :],
                                           start=(kt == 0), stop=(kt == TT - 1))
                mm.then_inc(S["b_pv"], 1)

            def unit(u):
                def part(b):
                    if u < UNITS:
                        scores(b, u)
                    if 1 <= u <= UNITS:
                        turn_probs(b, u - 1)
                    if 2 <= u:
                        values(b, u - 2)
                return part

            def B6a(b):
                pe.wait_ge(S["b_att"], b * 2 + 2)
                turn_tiles(psum(0), att).then_inc(S["b_attT"], 1)

            def B6c(b):
                pe.wait_ge(S["b_exp"], (b + 1) * UNITS)
                pe.wait_ge(S["b_h2"], b + 1)
                for kt in range(KT):
                    pe.matmul(psum(1, L, 2 * L), b_a[:, kt, :], h2T[:, kt, :], start=(kt == 0), stop=(kt == KT - 1))

            def B6b(b):
                pe.wait_ge(S["b_attT_out"], b + 1)
                for kt in range(KT):
                    mm = pe.matmul(psum(1, 0, L), woa[:, kt, :], attT[:, kt, :], start=(kt == 0), stop=(kt == KT - 1))
                mm.then_inc(S["b_mod"], 1)

            def mlp(f):
                def part(b):
                    if f == 0 and first(b):
                        pe.wait_ge(S["ld_mlp"], 48)
                    n = (0, 2, 3)[f % 3]
                    cols = slice(f * P, (f + 1) * P)
                    if f >= 3:
                        need(pe, "b_act", b * FT + f - 2)
                    for kt in range(KT):
                        pe.matmul(psum(n, L, 2 * L), w_up[:, kt, cols], h2T[:, kt, :], start=(kt == 0), stop=(kt == KT - 1))
                    for kt in range(KT):
                        pe.matmul(psum(n, 0, L), w_in[:, kt, cols], h2T[:, kt, :], start=(kt == 0), stop=False)
                    if f == 0:
                        pe.wait_ge(S["b_mh"], b + 1)
                    pe.matmul(psum(n, 0, L), b_stack[:, cols], m_stack[:], start=False, stop=True).then_inc(S["b_gu"], 1)
                return part

            def B8(b):
                for tt in range(TT):
                    for f in range(FT):
                        if tt == 0:
                            pe.wait_ge(S["b_act"], b * FT + f + 1)
                        mm = pe.matmul(psum(1, tt * D, (tt + 1) * D), actT[:, f, tt * P:(tt + 1) * P], w_down[:, f, :],
                                       start=(f == 0), stop=(f == FT - 1))
                mm.then_inc(S["b_dn"], 1)

            def D1(b):
                pe.wait_ge(S["b_x2"], b + 1)
                need(pe, "d_pos", b)
                turn_tiles(psum(6), x2).then_inc(S["d_xT"], 1)

            def D2(b):
                if first(b):
                    pe.wait_ge(S["ld_d"], 128)
                pe.wait_ge(S["d_xT_out"], b + 1)
                need(pe, "d_base", b)
                project(psum(7), d_w["k"], x2T).then_inc(S["d_k_ps"], 1)

            def D2x(b):
                project(psum(6), d_w["v"], x2T).then_inc(S["d_v"], 1)

            def D2q(b):
                pe.wait_ge(S["d_k_out"], b + 1)
                project(psum(7), d_w["q"], x2T).then_inc(S["d_q"], 1)

            def D3(b):
                pe.wait_ge(S["d_vh"], b + 1)
                by_token(psum(6), vh, d_w["o"]).then_inc(S["d_o"], 1)

            def D4(b):
                pe.wait_ge(S["d_x3"], b + 1)
                turn_tiles(psum(7), x3).then_inc(S["d_x3T"], 1)

            def D4l(b):
                pe.wait_ge(S["d_x3T_out"], b + 1)
                pe.wait_ge(S["d_r"], b + 1)
                for tt in range(TT):
                    for kt in range(KT):
                        mm = pe.matmul(psum(6, tt * E_N, (tt + 1) * E_N), x3T[:, kt, tt * P:(tt + 1) * P], gate_w[:, kt, :],
                                       start=(kt == 0), stop=(kt == KT - 1))
                mm.then_inc(S["d_lg"], 1)

            def shared(n):
                at, w = SH_TILES[n]
                def part(b):
                    if n:
                        need(pe, "d_sact", b * 3 + n)
                    else:
                        pe.wait_ge(S["d_x3T_out"], b + 1)
                    for g in range(2):
                        for kt in range(KT):
                            mm = pe.matmul(bank[0:w, 7, g * L:(g + 1) * L], sh_gu[:, kt, g * SH_I + at:g * SH_I + at + w],
                                           x3T[:, kt, :], start=(kt == 0), stop=(kt == KT - 1))
                    mm.then_inc(S["d_sg"], 1)
                return part

            def D5(b):
                pe.wait_ge(S["d_mask"], b + 1)
                pe.matmul(psum(6, 128, 192), beforeb, mkb[:, 0, :], start=True, stop=False)
                pe.matmul(psum(6, 128, 192), onesb, seen[:], start=False, stop=True)
                pe.matmul(psum(6, 192, 256), beforeb, mkb[:, 1, :], start=True, stop=False)
                pe.matmul(psum(6, 192, 256), onesb, mkb[:, 0, :], start=False, stop=False)
                pe.matmul(psum(6, 192, 256), onesb, seen[:], start=False, stop=True).then_inc(S["d_rank"], 1)

            def shared_out(tt):
                def part(b):
                    if tt == 0:
                        pe.wait_ge(S["d_sact"], b * 3 + 3)
                    for n, (_, w) in enumerate(SH_TILES):
                        mm = pe.matmul(psum(7, tt * D, (tt + 1) * D), sact[0:w, n, tt * P:(tt + 1) * P], sh_dn[0:w, n, :],
                                       start=(n == 0), stop=(n == len(SH_TILES) - 1))
                    if tt == TT - 1:
                        mm.then_inc(S["d_sd"], 1)
                return part

            def DTa(b):
                pe.wait_ge(S["d_pos"], b + 1)
                pe.wait_ge(S["d_dest"], b + 1)
                pe.matmul(psum(6, 0, E_N), onesb, seen[:], start=True, stop=True).then_inc(S["r_tot"], 1)

            def DTb(b):
                pe.wait_ge(S["r_tab"], 1)
                for j in range(4):
                    mm = pe.matmul(bank[0:1, 0, :].rearrange("o (c j) -> o c j", j=4)[:, :, j], ctab[:, j:j + 1], ident,
                                   start=True, stop=True)
                mm.then_inc(S["r_row"], 1)
                pe.wait_ge(S["r_spot"], 1)
                for k in range(2):
                    mm = pe.matmul(psum(6, k * 2 * P, k * 2 * P + P), onesb, spot[:, k, :], start=True, stop=True)
                mm.then_inc(S["r_all"], 1)

            turns(pe, {"DTa": DTa, "DTb": DTb, "A1": A1, "A1b": A1b, "C1": C1, "C2": C2, "C2v": C2v, "A2": A2, "A3a": forward(0), "A3b": forward(1), "A4a": inverse(0), "A4b": inverse(1),
                       "A5": A5, "B6a": B6a, "B6b": B6b, "B6c": B6c, "B8": B8,
                       "D1": D1, "D2k": D2, "D2x": D2x, "D2q": D2q, "D3": D3, "D4": D4, "D4l": D4l, "D5": D5, "SDa": shared_out(0), "SDb": shared_out(1),
                       **{f"u{u}": unit(u) for u in range(UNITS + 2)}, **{f"f{f}": mlp(f) for f in range(FT)},
                       **{f"S{n}": shared(n) for n in range(3)}})

            def turn_rows(c):
                s, out = c.slot(RING), psum(c.slot(3))
                pe.wait_ge(S[f"m_x{s}"], c.before(RING) * 16 + 16)
                need(pe, "m_xT_out", c.no - 2)
                for kt in range(KT):
                    t = turn(out[:, kt * P:(kt + 1) * P], xc_row[s][:, kt * P:(kt + 1) * P])
                t.then_inc(S["m_xT"], 1)

            def inner(c):
                s, n = c.slot(RING), c.slot(3)
                pe.wait_ge(S[f"m_w{s}"], c.before(RING) * 32 + 32)
                pe.wait_ge(S["m_xT_out"], c.no + 1)
                need(pe, "m_hs", c.no - 2)
                for m in range(2):
                    for kt in range(KT):
                        mm = pe.matmul(bank[0:IH, 3 + n, m * P:(m + 1) * P], w1[s][:, kt, m * IH:(m + 1) * IH], xcT[n][:, kt, :],
                                       start=(kt == 0), stop=(kt == KT - 1))
                mm.then_inc(S["m_h"], 1)

            def outer(c):
                s, n = c.slot(RING), c.slot(3)
                pe.wait_ge(S["m_hs"], c.no + 1)
                need(pe, "m_y_out", c.no - 1)
                for m in range(2):
                    mm = pe.matmul(psum(6 + c.slot(2), 0, D), hs[n][:, m, :], w2[s][:, m, :], start=(m == 0), stop=(m == 1))
                mm.then_inc(S["m_y"], 1)

            chunk_loop(pe, [turn_rows, inner, None, outer])

            def add_up(c):
                s = c.slot(YG)
                pe.wait_ge(S[f"f_ld{s}"], c.before(YG) * 16 + 16)
                pe.wait_ge(S["f_diag"], c.no + 1)
                need(pe, "f_r", c.no - (YG - 1))
                for k in range(ON_PE):
                    mm = pe.matmul(psum(s, 0, D), diag[s][:, k, :], yg[s][:, k, :], start=(k == 0), stop=(k == ON_PE - 1))
                mm.then_inc(S["f_sum"], 1)

            tile_loop(pe, [add_up])

        @block.scalar
        def _(act):
            act.dma_start(vec[:], d["vec"]).then_inc(S["ld_vec"], 16)
            act.dma_start(cst[:], d["cst"]).then_inc(S["ld_cst"], 16)
            act.dma_start(csb[:], d["csb"]).then_inc(S["ld_cst"], 16)
            act.wait_ge(S["ld_a"], 48)
            act.dma_start(X[:], d["u"].rearrange("b (t p) d -> p (b t) d", p=P)).then_inc(S["ld_u"], 16)
            act.dma_start(bo[:], d["bo"]).then_inc(S["ld_u"], 16)

            def column(name, kt):
                return vec[:, VEC[name] + kt:VEC[name] + kt + 1]

            act.wait_ge(S["ld_vec"], 16)
            act.wait_ge(S["set_pool"], 1)

            def biased(*names):
                def part(b):
                    for n, dst, at, bk, used in names:
                        act.wait_ge(S[f"a_{n}"], b + 1)
                        need(act, used, b)
                        for eh in range(KT):
                            i = act.activation(dst[:, eh, at:at + L], psum(bk, eh * L, (eh + 1) * L), ACT.Identity,
                                               bias=column("b" + n, eh))
                        i.then_inc(S[f"a_{n}_out"], 1)
                return part

            def A2(b):
                act.wait_ge(S["a_kvT"], b + 1)
                need(act, "b_third", b * 2)
                need(act, "a_X", b * 2)
                act.activation(kvT[:], psum3(5), ACT.Copy).then_inc(S["a_kvT_out"], 1)

            def C1(b):
                act.wait_ge(S["b_hT"], b + 1)
                need(act, "b_v", b)
                for kt in range(KT):
                    i = act.activation(h1T[:, kt, :], psum(5, kt * L, (kt + 1) * L), ACT.Identity, scale=column("ln1", kt))
                i.then_inc(S["b_h1"], 1)
                need(act, "b_h2", b)
                act.activation(xnT[:], psum3(5), ACT.Copy).then_inc(S["b_xT"], 1)

            def C2(b):
                for n, bk, scale, left in (("q", 4, HD ** -0.5, 16), ("k", 5, 1.0, 32)):
                    act.wait_ge(S[f"b_{n}"], b + 1)
                    need(act, f"st_{n}w", b * left)
                    act.activation(part[n][:, 0], psum3(bk), ACT.Copy, scale=scale).then_inc(S["b_first"], 1)

            def C2v(b):
                for i, n in enumerate("qk"):
                    act.wait_ge(S["b_rest"], b * 2 + i + 1)
                    act.activation(part[n][:, 1], rest[n][:], ACT.Copy).then_inc(S["b_second"], 1)
                act.wait_ge(S["b_v"], b + 1)
                need(act, "b_pv", b * UNITS)
                act.activation(v1[:, :, :, 0:HD], bank[:, 4, :].rearrange("p (t h e) -> p t h e", t=TT, h=HEADS),
                               ACT.Copy).then_inc(S["b_v_out"], 1)

            def unit(u):
                def part(b):
                    if u < UNITS:
                        act.wait_ge(S["b_max"], b * UNITS + u + 1)
                        need(act, "b_pT", b * UNITS + u - 1)
                        w = P if u < GROUPS else L
                        for h in range(512 // w):
                            i = act.activation(prob[:, u % 2, h * w:(h + 1) * w], psum(u % 2, h * w, (h + 1) * w), ACT.Exp,
                                               bias=nmx[:, u, h:h + 1])
                        i.then_inc(S["b_exp"], 1)
                    if 1 <= u <= UNITS:
                        need(act, "b_pT", b * UNITS + u)
                        need(act, "b_pv", b * UNITS + u - 2)
                        act.activation(probT[:, (u - 1) % 2, :, :], bank[:, 2, :].rearrange("p (j q) -> p j q", j=4), ACT.Copy
                                       ).then_inc(S["b_pT_out"], 1)
                return part

            def B6a(b):
                act.wait_ge(S["b_attT"], b + 1)
                need(act, "b_mod", b)
                act.activation(attT[:], psum3(0), ACT.Copy).then_inc(S["b_attT_out"], 1)

            def B6b(b):
                act.wait_ge(S["b_mod"], b + 1)
                need(act, "b_mh", b)
                act.activation(th[:], psum(1, 0, L), ACT.Tanh).then_inc(S["b_tanh"], 1)

            def mlp(f):
                def part(b):
                    act.wait_ge(S["b_gu"], b * FT + f + 1)
                    need(act, "b_act", b * FT + f - 1)
                    act.activation(gt[:, f % 2, :], psum((0, 2, 3)[f % 3], 0, L), ACT.Tanh, scale=0.5).then_inc(S["b_gt"], 1)
                return part

            def D1(b):
                act.wait_ge(S["d_xT"], b + 1)
                need(act, "d_q", b)
                act.activation(x2T[:], psum3(6), ACT.Copy).then_inc(S["d_xT_out"], 1)

            def D2(b):
                act.wait_ge(S["d_k_ps"], b + 1)
                need(act, "d_kv", b)
                act.activation(d_k[:], psum3(7), ACT.Copy, scale=float(D) ** 0.5 / L).then_inc(S["d_k_out"], 1)

            def D4(b):
                act.wait_ge(S["d_x3T"], b + 1)
                need(act, "d_sg", b * 3)
                act.activation(x3T[:], psum3(7), ACT.Copy).then_inc(S["d_x3T_out"], 1)

            def D4m(b):
                act.wait_ge(S["d_max"], b + 1)
                for tt in range(TT):
                    i = act.activation(ex[:, tt, :], psum(6, tt * E_N, (tt + 1) * E_N), ACT.Exp, bias=nlg[:, tt:tt + 1])
                i.then_inc(S["d_ex"], 1)

            def shared(n):
                w = SH_TILES[n][1]
                def part(b):
                    act.wait_ge(S["d_sg"], b * 3 + n + 1)
                    need(act, "d_sact", b * 3 + n)
                    act.activation(sgt[0:w, :], bank[0:w, 7, 0:L], ACT.Tanh, scale=0.5).then_inc(S["d_sgt"], 1)
                return part

            turns(act, {"A1": biased(("q", q_sb, 2, 4, "a_qc")), "A1b": biased(("k", k_sb, 2, 5, "a_kc"), ("v", v_sb, 0, 4, "a_kv")),
                        "A2": A2, "C1": C1, "C2": C2, "C2v": C2v, "B6a": B6a, "B6b": B6b, "D1": D1, "D2k": D2, "D4": D4, "D4m": D4m,
                        **{f"u{u}": unit(u) for u in range(UNITS + 2)}, **{f"f{f}": mlp(f) for f in range(FT)},
                        **{f"S{n}": shared(n) for n in range(3)}})

            def silu(c):
                n = c.slot(3)
                act.wait_ge(S["m_h"], c.no + 1)
                need(act, "m_y", c.no - 2)
                act.activation(hs[n], bank[0:IH, 3 + n, 0:2 * P].rearrange("p (a b) -> p a b", a=2), ACT.Silu
                               ).then_inc(S["m_hs"], 1)

            def load(c):
                s = c.slot(RING)
                e, _ = chunk_values(act, c)
                need(act, "m_y", c.no - (RING - 1))
                act.dma_start(w2[s], d["e_w2"][bass.ds(e, 1)].rearrange("o p k h -> p (o k) h")).then_inc(S[f"m_w{s}"], 16)

            act.wait_ge(S["r_table"], 1)
            chunk_loop(act, [load, None, None, silu])

            def collect(c):
                s = c.slot(YG)
                if first(c.no):
                    act.wait_ge(S["m_y"], CHUNKS)
                need(act, "f_r", c.no - (YG - 1))
                rows = (slice(c.no * P * TOPK, (c.no + 1) * P * TOPK) if isinstance(c.no, int)
                        else bass.ds(c.no * P * TOPK, P * TOPK))
                act.dma_start(yg[s], y_rows[rows, :].rearrange("(p k) d -> p k d", k=TOPK)).then_inc(S[f"f_ld{s}"], 16)
                if not isinstance(c.no, int):
                    weigh(c)

            def weigh(c):
                w = tile_of(TOPW, c.no)
                for k in range(ON_PE):
                    i = act.activation(diag[c.slot(YG)][:, k, :], ident, ACT.Identity, scale=w[:, k:k + 1])
                i.then_inc(S["f_diag"], 1)

            out = d["out"].rearrange("b (t p) d -> (b t) p d", p=P)

            def put(c):
                h = c.slot(2)
                act.wait_ge(S["f_out"], c.no + 1)
                n = slice(c.no, c.no + 1) if isinstance(c.no, int) else bass.ds(c.no, 1)
                act.dma_start(out[n].rearrange("o p d -> p (o d)"), outb[h]).then_inc(S[f"f_st{h}"], 16)

            act.wait_ge(S["d_dest"], NB)
            for n in range(YG):
                weigh(Tile(0, n))
            for s in range(RING):
                act.wait_ge(S[f"m_st{s}"], 16 * ((CHUNKS - s + RING - 1) // RING))
            tile_loop(act, [collect, None, None, None, put])
            for h in range(2):
                act.wait_ge(S[f"f_st{h}"], 16 * (NT // 2))

        @block.vector
        def _(dve):
            ca, cbn, cd = Chain(dve, "ch_a", 7), Chain(dve, "ch_b", 16), Chain(dve, "ch_d", 25)

            def col(name, kt, n=1, j=0):
                at = VEC[name] + kt * n + j
                return vec[:, at:at + 1]

            def moments(ch, m, tiles=range(TT)):
                for t in tiles:
                    i = dve.bn_stats(m["st"][:, t, :], m["r"][:, t, :])
                ch.link(i)
                alone(dve)
                for t in tiles:
                    i = dve.bn_aggr(m["mv"][:, t, :], m["st"][:, t, :])
                ch.link(i)
                a, z = tiles[0], tiles[-1] + 1
                return dve.tensor_scalar(m["v"][:, a:z], m["mv"][:, a:z, 1], LN_EPS, None, ALU.add)

            def scaled(m, outs):
                for t, out in outs.items():
                    i = dve.tensor_scalar(out, m["r"][:, t, :], m["mv"][:, t, 0:1], m["y"][:, t:t + 1], ALU.subtract, ALU.mult)
                return i

            def slot(b, tt):
                n = b * TT + tt
                return X[:, n, :] if isinstance(n, int) else X[:, bass.ds(n, 1), :].rearrange("p o d -> p (o d)")

            def slots(t, b):
                return t[:, b * TT:(b + 1) * TT] if isinstance(b, int) else t[:, bass.ds(b * TT, TT)]

            dve.memset(x3_meta[:, :, 1 + TOPK:], 0.0)
            dve.wait_ge(S["ld_vec"], 16)
            dve.wait_ge(S["ld_cst"], 32)
            dve.wait_ge(S["set_pool"], 1)

            def conv(n, src, dst):
                def part(b):
                    if n == "q":
                        ca.start(b)
                        need(dve, "a_x1", b)
                    if n == "k":
                        need(dve, "b_h2", b)
                    dve.wait_ge(S[f"a_{n}_out"], b + 1)
                    for eh in range(KT):
                        i = dve.tensor_scalar(dst[:, eh, :], src[:, eh, 2:2 + L], col(f"c{n}w", eh, 3, 2), col(f"c{n}b", eh),
                                              ALU.mult, ALU.add)
                    ca.link(i)
                    for j in (1, 0):
                        for eh in range(KT):
                            i = dve.scalar_tensor_tensor(dst[:, eh, :], src[:, eh, j:j + L], col(f"c{n}w", eh, 3, j),
                                                         dst[:, eh, :], ALU.mult, ALU.add)
                        if j == 1:
                            ca.link(i)
                    i.then_inc(S[f"a_{n}c"], 1)
                    if n == "k":
                        dve.wait_ge(S["a_kc"], b + 1)
                        dve.wait_ge(S["a_v_out"], b + 1)
                        need(dve, "a_kvT", b)
                        dve.tensor_tensor(kv[:], kc[:], v_sb[:], ALU.mult).then_inc(S["a_kv"], 1)
                return part

            def A3(b):
                if first(b):
                    dve.wait_ge(S["set_pe"], 3)
                    for n, t in enumerate((tabA, tabB, tabD)):
                        i = dve.tensor_copy(t[:], psum3(n))
                    i.then_inc(S["set_dve"], 1)
                    dve.wait_ge(S["set_dve"], 1)
                dve.wait_ge(S["a_X"], b * 2 + 2)
                for n, left in (("q", 16), ("k", 32)):
                    need(dve, f"st_{n}w", b * left)
                need(dve, "a_y", b * 2)
                for n, (bk, tab) in enumerate(((4, tabA), (5, tabB), (4, tabB), (5, tabD))):
                    i = dve.tensor_tensor(pr[n], psum3(bk), tab[:], ALU.mult)
                i.then_inc(S["a_pr"], 1)
                if first(b):
                    dve.wait_ge(S["ld_b"], 96)
                    cs = Chain(dve, "set_dve", 0)
                    cs.k = 1
                    cs.link(dve.tensor_copy(b_part[0], b_b))
                    cs.link(dve.tensor_tensor(b_rest, b_b, b_part[0], ALU.subtract))
                    cs.link(dve.tensor_copy(b_part[1], b_rest))
                    cs.link(dve.tensor_tensor(b_part[2], b_rest, b_part[1], ALU.subtract))
                    cs.link(dve.tensor_scalar(b_stack[:], b_part[0], part_of[:, 0:1], None, ALU.mult))
                    for n in (1, 2):
                        cs.link(dve.scalar_tensor_tensor(b_stack[:], b_part[n], part_of[:, n:n + 1], b_stack[:], ALU.mult, ALU.add))

            def A4(b):
                dve.wait_ge(S["a_y"], b * 2 + 2)
                dve.wait_ge(S["a_kv"], b + 1)
                for eh in range(KT):
                    i = dve.scalar_tensor_tensor(kv[:, eh, :], kv[:, eh, :], col("skip", eh), psum(4, eh * L, (eh + 1) * L),
                                                 ALU.mult, ALU.add)
                i.then_inc(S["a_z"], 1)
                dve.wait_ge(S["a_z"], b + 1)
                dve.wait_ge(S["a_qc"], b + 1)
                need(dve, "b_third", b * 2 - 1)
                need(dve, "a_o", b)
                dve.tensor_tensor(z[:], kv[:], qc[:], ALU.mult).then_inc(S["a_zq"], 1)

            def A5(b):
                dve.wait_ge(S["a_o"], b + 1)
                if first(b):
                    dve.wait_ge(S["ub"], 1)
                m = nrm["A"]
                dve.tensor_tensor(m["r"][:], psum3(5), slots(X, b), ALU.add).then_inc(S["a_r"], 1)
                dve.wait_ge(S["a_r"], b + 1)
                moments(ca, m).then_inc(S["n_varA"], 1)

            def A5o(b):
                dve.wait_ge(S["n_invA"], b + 1)
                scaled(nrm["A"], {tt: slot(b, tt) for tt in range(TT)}).then_inc(S["a_x1"], 1)

            def A6(b):
                dve.wait_ge(S["a_x1"], b + 1)
                need(dve, "b_hT", b)
                need(dve, "b_xn", b)
                for tt in range(TT):
                    i = dve.scalar_tensor_tensor(xn[:, tt, :], slot(b, tt), 1.0 / D, slot(b, tt), ALU.mult, ALU.mult,
                                                 accum_out=ms[:, tt:tt + 1])
                ca.link(i)
                dve.tensor_scalar(nrm["R"]["v"][:], ms[:], RMS_EPS, None, ALU.add).then_inc(S["n_varR"], 1)

            def A6o(b):
                dve.wait_ge(S["n_invR"], b + 1)
                for tt in range(TT):
                    i = dve.tensor_scalar(xn[:, tt, :], slot(b, tt), nrm["R"]["y"][:, tt:tt + 1], None, ALU.mult)
                i.then_inc(S["b_xn"], 1)

            def C1(b):
                if first(b):
                    dve.wait_ge(S["set_woa"], 1)
                    dve.tensor_copy(woa[:], psum(1, 0, KT * P).rearrange("p (k r) -> p k r", k=KT)).then_inc(S["set_dve"], 1)

            def C2(b):
                for i, (n, bk, scale) in enumerate((("q", 4, HD ** -0.5), ("k", 5, 1.0))):
                    dve.wait_ge(S["b_first"], b * 2 + i + 1)
                    need(dve, "b_third", b * 2 + i - 1)
                    dve.scalar_tensor_tensor(rest[n][:], psum3(bk), scale, part[n][:, 0], ALU.mult, ALU.subtract
                                             ).then_inc(S["b_rest"], 1)

            def unit(u):
                w = P if u < GROUPS else L
                def part(b):
                    if u == 0:
                        cbn.start(b)
                    dve.wait_ge(S["b_s"], b * UNITS + u + 1)
                    need(dve, "b_exp", (b - 1) * UNITS + u + 1)
                    dve.tensor_reduce(nmx[:, u, 0:512 // w], bank[:, u % 2, :].rearrange("p (h k) -> p h k", k=w), AX, ALU.max,
                                      negate=True).then_inc(S["b_max"], 1)
                return part

            def divide(tt):
                def part(b):
                    need(dve, "b_pv", b * UNITS + (GROUPS, UNITS)[tt])
                    o = psum(3, 0, HEADS * (HD + 1)).rearrange("p (h e) -> p h e", h=HEADS)
                    cbn.link(dve.reciprocal(rec[:, tt, :], o[:, :, HD]))
                    need(dve, "b_x2", b)
                    dve.tensor_tensor(att[:, tt, :].rearrange("p (h e) -> p h e", h=HEADS), o[:, :, 0:HD],
                                      rec[:, tt, :].rearrange("p (h o) -> p h o", o=1).broadcast_to([P, HEADS, HD]),
                                      ALU.mult).then_inc(S["b_att"], 1)
                return part

            def B6(b):
                dve.wait_ge(S["b_tanh"], b + 1)
                need(dve, "b_gu", b * FT)
                lower, last = slice(P // 2, P), slice(3 * P // 4, P)
                cbn.step(dve.scalar_tensor_tensor(m_stack[:], th[:], MOD_SCALE, psum(1, L, 2 * L), ALU.mult, ALU.mult))
                cbn.link(dve.scalar_tensor_tensor(mh[lower], th[lower], MOD_SCALE, bank[lower, 1, L:2 * L], ALU.mult, ALU.mult))
                cbn.link(dve.tensor_tensor(mh[lower], mh[lower], m_stack[lower], ALU.subtract))
                cbn.link(dve.tensor_copy(m_stack[lower], mh[lower]))
                dve.tensor_tensor(m_stack[last], mh[last], m_stack[last], ALU.subtract).then_inc(S["b_mh"], 1)

            def mlp(f):
                def part(b):
                    n = (0, 2, 3)[f % 3]
                    if f == 0:
                        need(dve, "b_dn", b)
                    dve.wait_ge(S["b_gt"], b * FT + f + 1)
                    cbn.link(dve.scalar_tensor_tensor(gs[:, f % 2, :], gt[:, f % 2, :], 1.0, psum(n, 0, L), ALU.add, ALU.mult))
                    dve.scalar_tensor_tensor(actT[:, f, :], gs[:, f % 2, :], 0.5, psum(n, L, 2 * L), ALU.mult, ALU.mult
                                             ).then_inc(S["b_act"], 1)
                return part

            def B8(b):
                dve.wait_ge(S["b_dn"], b + 1)
                m = nrm["B"]
                for tt in range(TT):
                    i = dve.scalar_tensor_tensor(m["r"][:, tt, :], slot(b, tt), 2.0, psum(1, tt * D, (tt + 1) * D), ALU.mult, ALU.add)
                i.then_inc(S["b_r"], 1)
                dve.wait_ge(S["b_r"], b + 1)
                moments(cbn, m).then_inc(S["n_varB"], 1)
                dve.wait_ge(S["n_invB"], b + 1)
                need(dve, "d_r", b)
                need(dve, "d_xT", b)
                scaled(m, {tt: x2[:, tt, :] for tt in range(TT)}).then_inc(S["b_x2"], 1)

            def D2(b):
                cd.start(b)
                need(dve, "d_x3", b)
                dve.wait_ge(S["d_k_out"], b + 1)
                dve.wait_ge(S["d_v"], b + 1)
                dve.tensor_tensor(d_kv[:], d_k[:], psum3(6), ALU.mult).then_inc(S["d_kv"], 1)
                dve.wait_ge(S["d_kv"], b + 1)
                for eh in range(KT):
                    i = dve.tensor_tensor_scan(d_cs[:, eh, :], ones_row[:], d_kv[:, eh, :], 0.0, ALU.mult, ALU.add)
                cd.link(i)

            def D2w(b):
                dve.wait_ge(S["d_q"], b + 1)
                need(dve, "d_o", b)
                dve.tensor_tensor(vh[:], psum3(7), d_cs[:], ALU.mult).then_inc(S["d_vh"], 1)

            def D3(b):
                dve.wait_ge(S["d_o"], b + 1)
                dve.wait_ge(S["b_x2"], b + 1)
                m = nrm["D"]
                dve.tensor_tensor(m["r"][:], psum3(6), x2[:], ALU.add).then_inc(S["d_r"], 1)
                dve.wait_ge(S["d_r"], b + 1)
                moments(cd, m).then_inc(S["n_varD"], 1)

            def D3o(b):
                dve.wait_ge(S["n_invD"], b + 1)
                need(dve, "d_scat", b * 16 * TT * TOPK)
                need(dve, "d_base", b)
                scaled(nrm["D"], {tt: x3[:, tt, :] for tt in range(TT)}).then_inc(S["d_x3"], 1)

            def D4m(b):
                dve.wait_ge(S["d_lg"], b + 1)
                alone(dve)
                for tt in range(TT):
                    i = dve.max(lg8[:, tt, :], psum(6, tt * E_N, (tt + 1) * E_N))
                cd.link(i)
                dve.tensor_scalar(nlg[:], lg8[:, :, 0], -1.0, None, ALU.mult).then_inc(S["d_max"], 1)

            def D4t(b):
                dve.wait_ge(S["d_ex"], b + 1)
                alone(dve)
                for tt in range(TT):
                    i = dve.max(top8[:, tt, :], ex[:, tt, :])
                cd.link(i)
                alone(dve)
                for tt in range(TT):
                    i = dve.max_index(top8i[:, tt, :], top8[:, tt, :], ex[:, tt, :])
                cd.link(i)
                cd.link(dve.tensor_copy(idxf[:], top8i[:]))

            def D4k(b):
                for k in range(TOPK):
                    for tt in range(TT):
                        if k == 0:
                            i = dve.tensor_scalar(mk[:, tt, :], iota, idxf[:, tt, 0:1], None, ALU.is_equal)
                        else:
                            dst = mkb if k == TOPK - 1 else mk
                            i = dve.scalar_tensor_tensor(dst[:, tt, :], iota, idxf[:, tt, k:k + 1], mk[:, tt, :], ALU.is_equal, ALU.add)
                    if k < TOPK - 1:
                        cd.link(i)
                i.then_inc(S["d_mask"], 1)

            def D4w(b):
                cd.link(dve.tensor_reduce(wsum[:], top8[:, :, 0:TOPK], AX, ALU.add))
                cd.link(dve.reciprocal(wrec[:], wsum[:]))
                cd.step(dve.tensor_tensor(slots(TOPW, b), top8[:, :, 0:TOPK],
                                          wrec[:].rearrange("p (t o) -> p t o", o=1).broadcast_to([P, TT, TOPK]), ALU.mult))

            def shared(n):
                w = SH_TILES[n][1]
                def part(b):
                    dve.wait_ge(S["d_sgt"], b * 3 + n + 1)
                    cd.link(dve.scalar_tensor_tensor(sgs[0:w, :], sgt[0:w, :], 1.0, bank[0:w, 7, 0:L], ALU.add, ALU.mult))
                    if n == 0:
                        need(dve, "d_sd", b)
                    dve.scalar_tensor_tensor(sact[0:w, n, :], sgs[0:w, :], 0.5, bank[0:w, 7, L:2 * L], ALU.mult, ALU.mult
                                             ).then_inc(S["d_sact"], 1)
                return part

            def D5p(b):
                dve.wait_ge(S["d_rank"], b + 1)
                for tt in range(TT):
                    i = dve.tensor_tensor(pos[:, tt, :], psum(6, 128 + tt * E_N, 192 + tt * E_N), region, ALU.add)
                i.then_inc(S["d_pos"], 1)
                for tt in range(TT):
                    cd.link(dve.tensor_tensor(seen[:], seen[:], mkb[:, tt, :], ALU.add))

            def D5h(b):
                dve.wait_ge(S["d_pos"], b + 1)
                for tt in range(TT):
                    for k in range(TOPK):
                        i = dve.scalar_tensor_tensor(hit[:, tt, k, :], iota, idxf[:, tt, k:k + 1], pos[:, tt, :], ALU.is_equal, ALU.mult)
                cd.link(i)
                cd.link(dve.tensor_reduce(destf[:], hit[:], AX, ALU.add))
                need(dve, "d_scat", b * 16 * TT * TOPK)
                cd.step(dve.tensor_copy(x3_meta[:, :, 1:1 + TOPK], idxf[:, :, 0:TOPK]))
                cd.link(dve.tensor_copy(x3_meta[:, :, 0], token_row))
                cd.step(dve.tensor_scalar(token_row, token_row, float(L * TOPK), None, ALU.add))
                dve.tensor_copy(desti[:].rearrange("p (t k) -> p t k", t=TT), destf[:]).then_inc(S["d_dest"], 1)

            def SD(b):
                dve.wait_ge(S["d_sd"], b + 1)
                for tt in range(TT):
                    i = dve.tensor_tensor(slot(b, tt), psum(7, tt * D, (tt + 1) * D), x3[:, tt, :], ALU.add)
                i.then_inc(S["d_base"], 1)

            cr = Chain(dve, "ch_r", 0)

            def DTa(b):
                dve.wait_ge(S["r_tot"], 1)
                tot = psum(6, 0, E_N)
                cr.link(dve.tensor_scalar(cn[:], tot, 1.0 / P, (P - 1.0) / P - 0.5 + 0.5 / P / 2, ALU.mult, ALU.add))
                cr.link(dve.tensor_scalar(cn[:], cn[:], ROUND, None, ALU.add))
                cr.link(dve.tensor_scalar(cn[:], cn[:], -ROUND, None, ALU.add))
                cr.step(dve.scalar_tensor_tensor(pad_e[:], cn[:], -float(P), tot, ALU.mult, ALU.add))
                cr.link(dve.tensor_tensor_scan(cum[:], ones_row[:, 0:E_N], cn[:], 0.0, ALU.mult, ALU.add))
                for k in range(2):
                    cr.step(dve.scalar_tensor_tensor(scr[:, 0, :], cum[:], chunk_no[:, k:k + 1], ones_row[:, 0:E_N], ALU.is_le, ALU.mult,
                                                     accum_out=ce[:, k:k + 1]))
                    cr.link(dve.scalar_tensor_tensor(scr[:, 1, :], cum[:], chunk_no[:, k:k + 1], cn[:], ALU.is_le, ALU.mult,
                                                     accum_out=cb[:, k:k + 1]))
                    cr.link(dve.scalar_tensor_tensor(scr[:, 2, :], iota, ce[:, k:k + 1], pad_e[:], ALU.is_equal, ALU.mult,
                                                     accum_out=co[:, k:k + 1]))
                cr.link(dve.tensor_tensor(cb[:], chunk_no, cb[:], ALU.subtract))
                cr.link(dve.scalar_tensor_tensor(co[:], cb[:], float(P), co[:], ALU.mult, ALU.add))
                cr.link(dve.scalar_tensor_tensor(crow[:], ce[:], float(CAP), co[:], ALU.mult, ALU.add))
                dve.tensor_scalar(ctab[:, 1::2], crow[:], float(P), None, ALU.add)
                dve.tensor_scalar(ctab[:, 0::2], ce[:], float(E_N - 1), None, ALU.min).then_inc(S["r_tab"], 1)
                dve.wait_ge(S["r_tab"], 1)
                for k in range(2):
                    i = dve.tensor_scalar(spot[:, k, :], ident, ctab[:, 2 * k:2 * k + 1], None, ALU.mult)
                i.then_inc(S["r_spot"], 1)

            def DTb(b):
                dve.wait_ge(S["r_row"], 1)
                dve.tensor_copy(table, bank[0:1, 0, :]).then_inc(S["r_table"], 1)
                dve.wait_ge(S["r_all"], 1)
                cr.link(dve.tensor_copy(expert_of.rearrange("p (c k) -> p k c", k=2), psum3(6)[:, :, 0:P]))

            turns(dve, {"DTa": DTa, "DTb": DTb, "A1q": conv("q", q_sb, qc), "A1k": conv("k", k_sb, kc), "A3p": A3, "A4z": A4, "A5n": A5, "A5o": A5o,
                        "A6n": A6, "A6o": A6o, "C1": C1, "C2": C2, **{f"u{u}": unit(u) for u in range(UNITS)},
                        "t0": divide(0), "t1": divide(1), "B6b": B6, **{f"f{f}": mlp(f) for f in range(FT)}, "B8": B8,
                        "D2v": D2, "D2w": D2w, "D3n": D3, "D3o": D3o, "D4m": D4m, "D4t": D4t, "D4k": D4k, "D4w": D4w, "D5p": D5p, "D5h": D5h,
                        **{f"S{n}": shared(n) for n in range(3)}, "SD": SD})
            for ch in (ca, cbn, cd):
                assert ch.k == ch.per, (ch.name, ch.k, ch.per)

            cm = Chain(dve, "ch_m", 1)

            def turned(c):
                n = c.slot(3)
                dve.wait_ge(S["m_xT"], c.no + 1)
                need(dve, "m_h", c.no - 2)
                dve.tensor_copy(xcT[n], bank[:, n, 0:2 * P].rearrange("p (a b) -> p a b", a=2)).then_inc(S["m_xT_out"], 1)

            def places(c):
                s = c.slot(RING)
                meta = xc_row[s][:, D:XW]
                cm.start(c.no)
                dve.wait_ge(S[f"m_x{s}"], c.before(RING) * 16 + 16)
                need(dve, f"m_st{s}", c.before(RING) * 16)
                e = expert_of[:, c.no:c.no + 1] if isinstance(c.no, int) else expert_of[:, bass.ds(c.no, 1)]
                cm.link(dve.scalar_tensor_tensor(found[s][:], meta[:, 1:1 + TOPK], e, iota[:, 0:TOPK], ALU.is_equal, ALU.mult,
                                                 accum_out=choice[s][:]))
                dve.tensor_tensor(ids[s][:], meta[:, 0:1], choice[s][:], ALU.add).then_inc(S["m_ids"], 1)

            def result(c):
                s = c.slot(RING)
                dve.wait_ge(S["m_y"], c.no + 1)
                need(dve, f"m_st{s}", c.before(RING) * 16)
                dve.tensor_copy(yc[s], psum(6 + c.slot(2), 0, D)).then_inc(S["m_y_out"], 1)

            chunk_loop(dve, [turned, places, None, result])

            cf = Chain(dve, "ch_f", 3)
            m = nrm["F"]

            def add_last(c):
                h, s = c.slot(2), c.slot(YG)
                cf.start(c.no)
                need(dve, "f_out", c.no - 1)
                dve.wait_ge(S[f"f_ld{s}"], c.before(YG) * 16 + 16)
                cf.link(dve.scalar_tensor_tensor(m["r"][:, h, :], yg[s][:, ON_PE, :], tile_of(TOPW, c.no)[:, ON_PE:TOPK],
                                                 tile_of(X, c.no), ALU.mult, ALU.add))
                dve.wait_ge(S["f_sum"], c.no + 1)
                dve.tensor_tensor(m["r"][:, h, :], m["r"][:, h, :], psum(s, 0, D), ALU.add).then_inc(S["f_r"], 1)
                dve.wait_ge(S["f_r"], c.no + 1)
                moments(cf, m, [h]).then_inc(S["n_varF"], 1)

            def finish(c):
                h = c.slot(2)
                dve.wait_ge(S["n_invF"], c.no + 1)
                need(dve, f"f_st{h}", c.before(2) * 16)
                scaled(m, {h: outb[h]}).then_inc(S["f_out"], 1)

            tile_loop(dve, [add_last, finish])


def layouts(x):
    def tiles(a, p=P):
        return np.ascontiguousarray(a.reshape(-1, p, a.shape[-1]).swapaxes(0, 1))

    def transposed(name):
        return tiles(x[name].T)

    def channel(name):
        return x[name].reshape(KT, P, -1).swapaxes(0, 1).reshape(P, -1)

    u = x["L0_attn_u"]
    a = {"u": u, "uT": np.ascontiguousarray(u.swapaxes(1, 2).reshape(NB, KT, P, L).swapaxes(1, 2))}
    a["vec"] = np.concatenate([channel(n) for n in (
        "L0_attn_bq", "L0_attn_bk", "L0_attn_bv", "L0_attn_convq_b", "L0_attn_convk_b", "L0_attn_D_skip", "L0_ffn_ln1_w",
        "L0_ffn_ln2_w", "L0_attn_convq_w", "L0_attn_convk_w")], 1)
    a["bo"] = np.ascontiguousarray(np.broadcast_to(x["L0_attn_bo"], (P, D)))
    a["ssm"] = transposed("L0_attn_ssm_kernel")
    for n in "qkvo":
        a[f"a_w{n}"] = transposed(f"L0_attn_W{n}")
        a[f"d_w{n}"] = transposed(f"L1_attn_W{n}")
    for n in "qkv":
        a[f"b_w{n}"] = transposed(f"L0_ffn_W{n}")
    for n in "qk":
        a[f"b_w{n}"] = np.ascontiguousarray(a[f"b_w{n}"].reshape(P, KT, KT, HEADS // KT, HD).swapaxes(3, 4).reshape(P, KT, D))
    a["b_wo"], a["b_a"], a["b_b"] = tiles(x["L0_ffn_Wo"]), tiles(np.tile(x["L0_ffn_A"], (1, P // R_MOD))), np.tile(x["L0_ffn_B"], (P // R_MOD, 1))
    a["w_in"], a["w_up"], a["w_down"] = (transposed(f"L0_ffn_W_{n}") for n in ("in_base", "up_base", "down"))
    a["gate_w"] = transposed("L1_ffn_gate_w")
    a["sh_gu"] = transposed("L1_ffn_shared_gate_up")
    a["sh_dn"] = np.ascontiguousarray(x["L1_ffn_shared_down"].T)
    a["e_w1"] = np.ascontiguousarray(x["L1_ffn_experts_w1"].swapaxes(1, 2).reshape(E_N, KT, P, I_N).swapaxes(1, 2))
    a["e_w2"] = np.ascontiguousarray(x["L1_ffn_experts_w2"].swapaxes(1, 2).reshape(E_N, 2, IH, D).swapaxes(1, 2))
    return a


def kernel(**inputs):
    import concourse.bacc as bacc
    from concourse.bass_utils import run_bass_kernel_spmd

    arrays = {n: np.ascontiguousarray(a) for n, a in layouts({n: np.asarray(v) for n, v in inputs.items()}).items()}
    arrays.update(constants())
    nc = bacc.Bacc("TRN2", target_bir_lowering=False, num_devices=1)
    d = {n: nc.dram_tensor(f"in_{n}", a.shape, mybir.dt.from_np(a.dtype), kind="ExternalInput").ap() for n, a in arrays.items()}
    d["out"] = nc.dram_tensor("out", (NB, L, D), F32, kind="ExternalOutput").ap()
    build(nc, d)
    r = run_bass_kernel_spmd(nc, [{f"in_{n}": a for n, a in arrays.items()}], core_ids=[0])
    return r.results[0]["out"]
```
